# Optimizing a Trainium2 kernel written in Bass

```python
import numpy as np
import jax
import jax.numpy as jnp

def _softmax(x, axis=-1):
    return jax.nn.softmax(x, axis=axis)

def _gelu(x):
    return jax.nn.gelu(x, approximate=True)

def _silu(x):
    return jax.nn.silu(x)

def _sigmoid(x):
    return jax.nn.sigmoid(x)

def _layernorm(x, axis=-1, eps=1e-05):
    m = jnp.mean(x, axis=axis, keepdims=True)
    v = jnp.var(x, axis=axis, keepdims=True)
    return (x - m) / jnp.sqrt(v + eps)

def _scatter_add(tgt, idx, src, axis=0):
    return tgt.at[idx].add(src)

def _segment_sum(src, seg, n):
    return jax.ops.segment_sum(src, seg, n)
kernel_name = 'mk_decoder_postln_d2_seqx_r8_b54261'

def setup_inputs(seed: int=0):
    np.random.seed(seed)
    _w = jnp.asarray

    def _rec_inputs():
        import jax
        import jax.numpy as jnp
        _rk = jax.random.key(seed)
        x = -0.0002928 + 1 * jax.random.normal(jax.random.fold_in(_rk, 1), (4, 512, 128), jnp.float32)
        _lenS = 512 - jax.random.randint(jax.random.fold_in(_rk, 7), (4,), 0, max(1, 512 // 4) + 1, jnp.int32)
        _lenS2 = 77 - jax.random.randint(jax.random.fold_in(_rk, 8), (4,), 0, max(1, 77 // 4) + 1, jnp.int32)
        _ctx_1024P = jax.random.normal(jax.random.fold_in(_rk, 11), (4, 16, 128), jnp.float32)
        _ctx_1024c = jax.random.dirichlet(jax.random.fold_in(_rk, 511), 0.3 * jnp.ones((16,), jnp.float32), (4, 77))
        _ctx_1024t = jnp.einsum('bsk,bkd->bsd', _ctx_1024c, _ctx_1024P)
        _ctx_1024t = _ctx_1024t * jax.lax.rsqrt(jnp.mean(jnp.square(_ctx_1024t)) + 1e-12) * 0.953939
        ctx_1024 = -1.39393e-06 + 0.999914 * (_ctx_1024t + 0.3 * jax.random.normal(jax.random.fold_in(_rk, 611), (4, 77, 128), jnp.float32))
        return (x, ctx_1024)
    x, ctx_1024 = _rec_inputs()

    def _L0_attn_setup():
        import jax, jax.numpy as jnp
        import numpy as np
        EPS = 1e-08
        key = jax.random.key(seed)
        x = jax.random.normal(key, (32, 200, 128), dtype=jnp.float32)
        return {'x': x}
    _L0_attn_all = _L0_attn_setup()
    _L0_attn_in = {k: v for k, v in _L0_attn_all.items() if k in ()}
    del _L0_attn_all

    def _L0_xattn_setup():
        import jax, jax.numpy as jnp
        import numpy as np
        D_MODEL = 128
        NUM_HEADS = 16
        HEAD_DIM = D_MODEL // NUM_HEADS
        B, S = (2, 256)

        def _split_heads(x):
            b, s, _ = x.shape
            return x.reshape(b, s, NUM_HEADS, HEAD_DIM).transpose(0, 2, 1, 3)
        key = jax.random.key(seed)
        ks = jax.random.split(key, 11)
        s = 1.0 / np.sqrt(D_MODEL)
        return {'query': jax.random.normal(ks[0], (B, S, D_MODEL), jnp.float32), 'key_': jax.random.normal(ks[1], (B, S, D_MODEL), jnp.float32), 'value': jax.random.normal(ks[2], (B, S, D_MODEL), jnp.float32), 'Wq': jax.random.normal(ks[3], (D_MODEL, D_MODEL), jnp.float32) * s, 'bq': jnp.zeros((D_MODEL,), jnp.float32), 'Wk': jax.random.normal(ks[4], (D_MODEL, D_MODEL), jnp.float32) * s, 'bk': jnp.zeros((D_MODEL,), jnp.float32), 'Wv': jax.random.normal(ks[5], (D_MODEL, D_MODEL), jnp.float32) * s, 'bv': jnp.zeros((D_MODEL,), jnp.float32), 'Wo': jax.random.normal(ks[6], (D_MODEL, D_MODEL), jnp.float32) * s, 'bo': jnp.zeros((D_MODEL,), jnp.float32)}
    _L0_xattn_all = _L0_xattn_setup()
    _L0_xattn_in = {k: v for k, v in _L0_xattn_all.items() if k in ('Wq', 'bq', 'Wk', 'bk', 'Wv', 'bv', 'Wo', 'bo')}
    del _L0_xattn_all

    def _L0_ffn_setup():
        import jax, jax.numpy as jnp
        import numpy as np
        B, S, D, H, E, K = (2, 256, 128, 256, 8, 2)
        key = jax.random.key(seed)
        ks = jax.random.split(key, 9)
        sc_d = 1.0 / np.sqrt(D)
        sc_h = 1.0 / np.sqrt(H)
        return {'x': jax.random.normal(ks[0], (B, S, D), dtype=jnp.float32), 'w_router': jax.random.normal(ks[1], (E, D), dtype=jnp.float32) * sc_d, 'Wg': jax.random.normal(ks[2], (E, H, D), dtype=jnp.float32) * sc_d, 'Wu': jax.random.normal(ks[3], (E, H, D), dtype=jnp.float32) * sc_d, 'Wd': jax.random.normal(ks[4], (E, D, H), dtype=jnp.float32) * sc_h, 'sg': jax.random.normal(ks[5], (H, D), dtype=jnp.float32) * sc_d, 'su': jax.random.normal(ks[6], (H, D), dtype=jnp.float32) * sc_d, 'sd': jax.random.normal(ks[7], (D, H), dtype=jnp.float32) * sc_h}
    _L0_ffn_all = _L0_ffn_setup()
    _L0_ffn_in = {k: v for k, v in _L0_ffn_all.items() if k in ('w_router', 'Wg', 'Wu', 'Wd', 'sg', 'su', 'sd')}
    del _L0_ffn_all

    def _L1_attn_setup():
        import jax, jax.numpy as jnp
        import numpy as np
        NUM_HEADS = 16
        EPS = 1e-06
        L2_EPS = 1e-12

        def _l2_normalize(x):
            n = jnp.linalg.norm(x, axis=-1, keepdims=True)
            return x / jnp.maximum(n, L2_EPS)
        key = jax.random.key(seed)
        k1, k2 = jax.random.split(key)
        x = jax.random.normal(k1, (2, 1024, 128), dtype=jnp.float32)
        W_qkv = jax.random.normal(k2, (384, 128), dtype=jnp.float32) * 0.02
        return {'x': x, 'W_qkv': W_qkv}
    _L1_attn_all = _L1_attn_setup()
    _L1_attn_in = {k: v for k, v in _L1_attn_all.items() if k in ('W_qkv',)}
    del _L1_attn_all

    def _L1_xattn_setup():
        import jax, jax.numpy as jnp
        import numpy as np
        DIM = 128
        HEADS = 16
        DIM_HEAD = 64
        INNER = HEADS * DIM_HEAD

        def _layernorm(x, w, b, eps=1e-05):
            mu = jnp.mean(x, axis=-1, keepdims=True)
            var = jnp.var(x, axis=-1, keepdims=True)
            return (x - mu) * jax.lax.rsqrt(var + eps) * w + b
        key = jax.random.key(seed)
        ks = jax.random.split(key, 12)
        b, n, m = (8, 512, 64)
        s = lambda fan_in: 1.0 / np.sqrt(fan_in)
        return {'x': jax.random.normal(ks[0], (b, n, DIM), jnp.float32), 'latents': jax.random.normal(ks[1], (b, m, DIM), jnp.float32), 'ln_media_w': jnp.ones((DIM,), jnp.float32), 'ln_media_b': jnp.zeros((DIM,), jnp.float32), 'ln_lat_w': jnp.ones((DIM,), jnp.float32), 'ln_lat_b': jnp.zeros((DIM,), jnp.float32), 'Wq': jax.random.normal(ks[2], (DIM, INNER), jnp.float32) * s(DIM), 'bq': jnp.zeros((INNER,), jnp.float32), 'Wkv': jax.random.normal(ks[3], (DIM, 2 * INNER), jnp.float32) * s(DIM), 'bkv': jnp.zeros((2 * INNER,), jnp.float32), 'Wout': jax.random.normal(ks[4], (INNER, DIM), jnp.float32) * s(INNER), 'bout': jnp.zeros((DIM,), jnp.float32)}
    _L1_xattn_all = _L1_xattn_setup()
    _L1_xattn_in = {k: v for k, v in _L1_xattn_all.items() if k in ('ln_media_w', 'ln_media_b', 'ln_lat_w', 'ln_lat_b', 'Wq', 'bq', 'Wkv', 'bkv', 'Wout', 'bout')}
    del _L1_xattn_all

    def _L1_ffn_setup():
        import jax, jax.numpy as jnp
        import numpy as np
        B, S, DIM = (4, 512, 128)
        BASE_COUPLING = 0.1
        NUM_CYCLES = 3

        def _gelu(x):
            return jax.nn.gelu(x, approximate=False)

        def _coupling_net(h, w1, b1, w2, b2, w3, b3, w4, b4):
            h = _gelu(h @ w1 + b1)
            h = _gelu(h @ w2 + b2)
            h = _gelu(h @ w3 + b3)
            return jax.nn.sigmoid(h @ w4 + b4)

        def _global_net(h, w1, b1, w2, b2, w3, b3):
            h = _gelu(h @ w1 + b1)
            h = _gelu(h @ w2 + b2)
            return jax.nn.sigmoid(h @ w3 + b3)

        def _twist(x):
            o_r, o_i, p_r, p_i = jnp.split(x, 4, axis=-1)
            return jnp.concatenate([p_r, -p_i, -o_r, o_i], axis=-1)
        key = jax.random.key(seed)
        ks = jax.random.split(key, 9)
        d = DIM

        def w(k, fan_in, fan_out):
            return jax.random.normal(k, (fan_in, fan_out), dtype=jnp.float32) / np.sqrt(fan_in).astype(np.float32)
        inp = {'x': jax.random.normal(ks[0], (B, S, d), dtype=jnp.float32)}
        cn_dims = [(d, d), (d, d // 2), (d // 2, d // 4), (d // 4, 1)]
        for i, (a, b) in enumerate(cn_dims):
            inp[f'cn_w{i + 1}'] = w(ks[1 + i], a, b)
            inp[f'cn_b{i + 1}'] = jnp.zeros((b,), dtype=jnp.float32)
        gc_dims = [(d, d // 2), (d // 2, d // 4), (d // 4, 1)]
        for i, (a, b) in enumerate(gc_dims):
            inp[f'gc_w{i + 1}'] = w(ks[5 + i], a, b)
            inp[f'gc_b{i + 1}'] = jnp.zeros((b,), dtype=jnp.float32)
        inp['adaptive_range'] = jnp.full((1,), 0.2, dtype=jnp.float32)
        return inp
    _L1_ffn_all = _L1_ffn_setup()
    _L1_ffn_in = {k: v for k, v in _L1_ffn_all.items() if k in ('cn_w1', 'cn_b1', 'cn_w2', 'cn_b2', 'cn_w3', 'cn_b3', 'cn_w4', 'cn_b4', 'gc_w1', 'gc_b1', 'gc_w2', 'gc_b2', 'gc_w3', 'gc_b3', 'adaptive_range')}
    del _L1_ffn_all
    return {'x': x, 'ctx_1024': ctx_1024, 'L0_xattn_Wq': _L0_xattn_in['Wq'], 'L0_xattn_bq': _L0_xattn_in['bq'], 'L0_xattn_Wk': _L0_xattn_in['Wk'], 'L0_xattn_bk': _L0_xattn_in['bk'], 'L0_xattn_Wv': _L0_xattn_in['Wv'], 'L0_xattn_bv': _L0_xattn_in['bv'], 'L0_xattn_Wo': _L0_xattn_in['Wo'], 'L0_xattn_bo': _L0_xattn_in['bo'], 'L0_ffn_w_router': _L0_ffn_in['w_router'], 'L0_ffn_Wg': _L0_ffn_in['Wg'], 'L0_ffn_Wu': _L0_ffn_in['Wu'], 'L0_ffn_Wd': _L0_ffn_in['Wd'], 'L0_ffn_sg': _L0_ffn_in['sg'], 'L0_ffn_su': _L0_ffn_in['su'], 'L0_ffn_sd': _L0_ffn_in['sd'], 'L1_attn_W_qkv': _L1_attn_in['W_qkv'], 'L1_xattn_ln_media_w': _L1_xattn_in['ln_media_w'], 'L1_xattn_ln_media_b': _L1_xattn_in['ln_media_b'], 'L1_xattn_ln_lat_w': _L1_xattn_in['ln_lat_w'], 'L1_xattn_ln_lat_b': _L1_xattn_in['ln_lat_b'], 'L1_xattn_Wq': _L1_xattn_in['Wq'], 'L1_xattn_bq': _L1_xattn_in['bq'], 'L1_xattn_Wkv': _L1_xattn_in['Wkv'], 'L1_xattn_bkv': _L1_xattn_in['bkv'], 'L1_xattn_Wout': _L1_xattn_in['Wout'], 'L1_xattn_bout': _L1_xattn_in['bout'], 'L1_ffn_cn_w1': _L1_ffn_in['cn_w1'], 'L1_ffn_cn_b1': _L1_ffn_in['cn_b1'], 'L1_ffn_cn_w2': _L1_ffn_in['cn_w2'], 'L1_ffn_cn_b2': _L1_ffn_in['cn_b2'], 'L1_ffn_cn_w3': _L1_ffn_in['cn_w3'], 'L1_ffn_cn_b3': _L1_ffn_in['cn_b3'], 'L1_ffn_cn_w4': _L1_ffn_in['cn_w4'], 'L1_ffn_cn_b4': _L1_ffn_in['cn_b4'], 'L1_ffn_gc_w1': _L1_ffn_in['gc_w1'], 'L1_ffn_gc_b1': _L1_ffn_in['gc_b1'], 'L1_ffn_gc_w2': _L1_ffn_in['gc_w2'], 'L1_ffn_gc_b2': _L1_ffn_in['gc_b2'], 'L1_ffn_gc_w3': _L1_ffn_in['gc_w3'], 'L1_ffn_gc_b3': _L1_ffn_in['gc_b3'], 'L1_ffn_adaptive_range': _L1_ffn_in['adaptive_range']}

def reference(x, ctx_1024, L0_xattn_Wq, L0_xattn_bq, L0_xattn_Wk, L0_xattn_bk, L0_xattn_Wv, L0_xattn_bv, L0_xattn_Wo, L0_xattn_bo, L0_ffn_w_router, L0_ffn_Wg, L0_ffn_Wu, L0_ffn_Wd, L0_ffn_sg, L0_ffn_su, L0_ffn_sd, L1_attn_W_qkv, L1_xattn_ln_media_w, L1_xattn_ln_media_b, L1_xattn_ln_lat_w, L1_xattn_ln_lat_b, L1_xattn_Wq, L1_xattn_bq, L1_xattn_Wkv, L1_xattn_bkv, L1_xattn_Wout, L1_xattn_bout, L1_ffn_cn_w1, L1_ffn_cn_b1, L1_ffn_cn_w2, L1_ffn_cn_b2, L1_ffn_cn_w3, L1_ffn_cn_b3, L1_ffn_cn_w4, L1_ffn_cn_b4, L1_ffn_gc_w1, L1_ffn_gc_b1, L1_ffn_gc_w2, L1_ffn_gc_b2, L1_ffn_gc_w3, L1_ffn_gc_b3, L1_ffn_adaptive_range):
    import jax
    import jax.numpy as jnp

    def _L0_attn_ref(x):
        import jax, jax.numpy as jnp
        import numpy as np
        EPS = 1e-08
        norms = jnp.linalg.norm(x, axis=-1)
        dots = jnp.einsum('bil,bjl->bij', x, x)
        sim = dots / jnp.maximum(norms[:, :, None] * norms[:, None, :], EPS)
        atten = jax.nn.softmax(sim, axis=-1)
        out = jnp.einsum('bij,bjl->bil', atten, x) + x
        return out

    def _L0_xattn_ref(query, key_, value, Wq, bq, Wk, bk, Wv, bv, Wo, bo):
        import jax, jax.numpy as jnp
        import numpy as np
        D_MODEL = 128
        NUM_HEADS = 16
        HEAD_DIM = D_MODEL // NUM_HEADS
        B, S = (2, 256)

        def _split_heads(x):
            b, s, _ = x.shape
            return x.reshape(b, s, NUM_HEADS, HEAD_DIM).transpose(0, 2, 1, 3)
        Q = _split_heads(query @ Wq + bq)
        K = _split_heads(key_ @ Wk + bk)
        V = _split_heads(value @ Wv + bv)
        scale = 1.0 / jnp.sqrt(jnp.asarray(HEAD_DIM, query.dtype))
        scores = jnp.einsum('bhqd,bhkd->bhqk', Q, K) * scale
        attn = jax.nn.softmax(scores, axis=-1)
        out = jnp.einsum('bhqk,bhkd->bhqd', attn, V)
        concat = out.transpose(0, 2, 1, 3).reshape(query.shape[0], -1, D_MODEL)
        return concat @ Wo + bo

    def _L0_ffn_ref(x, w_router, Wg, Wu, Wd, sg, su, sd):
        import jax, jax.numpy as jnp
        import numpy as np
        B, S, D, H, E, K = (2, 256, 128, 256, 8, 2)
        b, s, d = x.shape
        xf = x.reshape(-1, d)
        logits = jnp.einsum('td,ed->te', xf, w_router)
        probs = jax.nn.softmax(logits, axis=-1)
        topw, topi = jax.lax.top_k(probs, K)
        topw = topw / jnp.sum(topw, axis=-1, keepdims=True)
        comb = jnp.sum(topw[..., None] * jax.nn.one_hot(topi, E, dtype=xf.dtype), axis=1)
        shared = jnp.einsum('th,dh->td', jax.nn.silu(jnp.einsum('td,hd->th', xf, sg)) * jnp.einsum('td,hd->th', xf, su), sd)
        h1 = jax.nn.silu(jnp.einsum('td,ehd->teh', xf, Wg))
        h2 = jnp.einsum('td,ehd->teh', xf, Wu)
        eo = jnp.einsum('teh,edh->ted', h1 * h2, Wd)
        routed = jnp.einsum('te,ted->td', comb, eo)
        return (routed + shared).reshape(b, s, d)

    def _L1_attn_ref(x, W_qkv):
        import jax, jax.numpy as jnp
        import numpy as np
        NUM_HEADS = 16
        EPS = 1e-06
        L2_EPS = 1e-12

        def _l2_normalize(x):
            n = jnp.linalg.norm(x, axis=-1, keepdims=True)
            return x / jnp.maximum(n, L2_EPS)
        b, n, dim = x.shape
        h = NUM_HEADS
        d = dim // h
        scale = d ** (-0.5)
        qkv = x @ W_qkv.T
        q, k, v = jnp.split(qkv, 3, axis=-1)
        to_heads = lambda t: t.reshape(b, n, h, d).transpose(0, 2, 1, 3)
        q, k, v = (to_heads(q), to_heads(k), to_heads(v))
        q = jax.nn.softplus(_l2_normalize(q))
        k = jax.nn.softplus(_l2_normalize(k))
        kv = jnp.einsum('bhnd,bhnc->bhdc', k, v) * scale
        ksum = jnp.sum(k, axis=2) + EPS
        norm = 1.0 / jnp.einsum('bhnd,bhd->bhn', q, ksum)
        out = jnp.einsum('bhnd,bhdc,bhn->bhnc', q, kv, norm)
        return out.transpose(0, 2, 1, 3).reshape(b, n, dim)

    def _L1_xattn_ref(x, latents, ln_media_w, ln_media_b, ln_lat_w, ln_lat_b, Wq, bq, Wkv, bkv, Wout, bout):
        import jax, jax.numpy as jnp
        import numpy as np
        DIM = 128
        HEADS = 16
        DIM_HEAD = 64
        INNER = HEADS * DIM_HEAD

        def _layernorm(x, w, b, eps=1e-05):
            mu = jnp.mean(x, axis=-1, keepdims=True)
            var = jnp.var(x, axis=-1, keepdims=True)
            return (x - mu) * jax.lax.rsqrt(var + eps) * w + b
        scale = DIM_HEAD ** (-0.5)
        x = _layernorm(x, ln_media_w, ln_media_b)
        lat = _layernorm(latents, ln_lat_w, ln_lat_b)
        q = lat @ Wq + bq
        kv_in = jnp.concatenate([x, lat], axis=1)
        kv = kv_in @ Wkv + bkv
        k, v = jnp.split(kv, 2, axis=-1)
        split = lambda t: t.reshape(t.shape[0], t.shape[1], HEADS, DIM_HEAD).transpose(0, 2, 1, 3)
        q, k, v = (split(q), split(k), split(v))
        sim = jnp.einsum('bhid,bhjd->bhij', q * scale, k)
        sim = sim - jax.lax.stop_gradient(jnp.max(sim, axis=-1, keepdims=True))
        attn = jax.nn.softmax(sim, axis=-1)
        out = jnp.einsum('bhij,bhjd->bhid', attn, v)
        out = out.transpose(0, 2, 1, 3).reshape(out.shape[0], out.shape[2], INNER)
        return out @ Wout + bout

    def _L1_ffn_ref(x, cn_w1, cn_b1, cn_w2, cn_b2, cn_w3, cn_b3, cn_w4, cn_b4, gc_w1, gc_b1, gc_w2, gc_b2, gc_w3, gc_b3, adaptive_range):
        import jax, jax.numpy as jnp
        import numpy as np
        B, S, DIM = (4, 512, 128)
        BASE_COUPLING = 0.1
        NUM_CYCLES = 3

        def _gelu(x):
            return jax.nn.gelu(x, approximate=False)

        def _coupling_net(h, w1, b1, w2, b2, w3, b3, w4, b4):
            h = _gelu(h @ w1 + b1)
            h = _gelu(h @ w2 + b2)
            h = _gelu(h @ w3 + b3)
            return jax.nn.sigmoid(h @ w4 + b4)

        def _global_net(h, w1, b1, w2, b2, w3, b3):
            h = _gelu(h @ w1 + b1)
            h = _gelu(h @ w2 + b2)
            return jax.nn.sigmoid(h @ w3 + b3)

        def _twist(x):
            o_r, o_i, p_r, p_i = jnp.split(x, 4, axis=-1)
            return jnp.concatenate([p_r, -p_i, -o_r, o_i], axis=-1)
        global_context = x.mean(axis=1, keepdims=True)
        gf = _global_net(global_context, gc_w1, gc_b1, gc_w2, gc_b2, gc_w3, gc_b3)
        out = x
        for _ in range(NUM_CYCLES):
            tf = _coupling_net(out, cn_w1, cn_b1, cn_w2, cn_b2, cn_w3, cn_b3, cn_w4, cn_b4)
            combined = 0.7 * gf + 0.3 * tf
            coupling = BASE_COUPLING + adaptive_range * (combined - 0.5) * 2.0
            out = out + coupling * _twist(out)
        return out
    x = _layernorm(x + _L0_attn_ref(x), axis=-1)
    x = _layernorm(x + _L0_xattn_ref(x, ctx_1024, ctx_1024, L0_xattn_Wq, L0_xattn_bq, L0_xattn_Wk, L0_xattn_bk, L0_xattn_Wv, L0_xattn_bv, L0_xattn_Wo, L0_xattn_bo), axis=-1)
    x = _layernorm(x + _L0_ffn_ref(x, L0_ffn_w_router, L0_ffn_Wg, L0_ffn_Wu, L0_ffn_Wd, L0_ffn_sg, L0_ffn_su, L0_ffn_sd), axis=-1)
    x = _layernorm(x + _L1_attn_ref(x, L1_attn_W_qkv), axis=-1)
    x = _layernorm(x + _L1_xattn_ref(ctx_1024, x, L1_xattn_ln_media_w, L1_xattn_ln_media_b, L1_xattn_ln_lat_w, L1_xattn_ln_lat_b, L1_xattn_Wq, L1_xattn_bq, L1_xattn_Wkv, L1_xattn_bkv, L1_xattn_Wout, L1_xattn_bout), axis=-1)
    x = _layernorm(x + _L1_ffn_ref(x, L1_ffn_cn_w1, L1_ffn_cn_b1, L1_ffn_cn_w2, L1_ffn_cn_b2, L1_ffn_cn_w3, L1_ffn_cn_b3, L1_ffn_cn_w4, L1_ffn_cn_b4, L1_ffn_gc_w1, L1_ffn_gc_b1, L1_ffn_gc_w2, L1_ffn_gc_b2, L1_ffn_gc_w3, L1_ffn_gc_b3, L1_ffn_adaptive_range), axis=-1)
    return x

_drawn_inputs = setup_inputs


def setup_inputs(seed=0):
    import zlib

    import numpy as np

    out = dict(_drawn_inputs(seed))
    spreads = {'L0_xattn_bq': (0.0, 0.1),
     'L0_xattn_bk': (0.0, 2.0),
     'L0_xattn_bv': (0.0, 0.1),
     'L0_xattn_bo': (0.0, 0.1),
     'L1_xattn_ln_media_w': (1.0, 0.6),
     'L1_xattn_ln_media_b': (0.0, 0.424),
     'L1_xattn_ln_lat_w': (1.0, 0.2),
     'L1_xattn_ln_lat_b': (0.0, 0.1),
     'L1_xattn_bq': (0.0, 0.655),
     'L1_xattn_bkv': (0.0, 0.1),
     'L1_xattn_bout': (0.0, 0.1),
     'L1_ffn_cn_b1': (0.0, 0.8),
     'L1_ffn_cn_b2': (0.0, 2.0),
     'L1_ffn_cn_b3': (0.0, 2.0),
     'L1_ffn_gc_b1': (0.0, 2.0),
     'L1_ffn_gc_b2': (0.0, 0.8)}
    factors = {'L1_ffn_cn_w1': 8.0,
     'L1_ffn_cn_w2': 6.687,
     'L1_ffn_cn_w3': 5.928,
     'L1_ffn_cn_w4': 5.663,
     'L1_ffn_gc_w1': 44.592,
     'L1_ffn_gc_w2': 5.487,
     'L1_ffn_gc_w3': 33.912}
    for name, (base, spread) in spreads.items():
        noise = np.random.default_rng([zlib.crc32(name.encode()), seed]).standard_normal(out[name].shape)
        drawn = base * np.exp(spread * noise) if base else spread * noise
        out[name] = jnp.asarray(drawn.astype(out[name].dtype))
    for name, factor in factors.items():
        out[name] = (out[name] * factor).astype(out[name].dtype)
    return out
```

```python
from contextlib import ExitStack

import concourse.bass as bass
from concourse import mybir

F32 = mybir.dt.float32
F32R = mybir.dt.float32r
U32 = mybir.dt.uint32
ACT = mybir.ActivationFunctionType
ALU = mybir.AluOpType
AX = mybir.AxisListType

P = 128
B, S, D = 4, 512, 128
NT = S // P
TILES = B * NT
CK = 77
NH = 16
DH = D // NH
DW = 64
INNER = NH * DW
NHP = NH // 2
PAIRS = B * NHP
KEYS = S + CK
KEYS_PAD = KEYS + 1
KB = (KEYS + P - 1) // P
E, HID = 8, 256
EXPERTS = E + 1
HB = HID // P
CYCLES = 3
LN_EPS = 1e-5
COS_EPS = 1e-8
L2_EPS = 1e-12
KSUM_EPS = 1e-6
LN_SCALE = 65536.0
SCALE_N = DH ** -0.5
SCALE_W = DW ** -0.5

LN_KEYS = ([("A", b) for b in range(B)] + [("media", 0)] + [("B", b) for b in range(B)]
           + [("C", b) for b in range(B)] + [("D", b) for b in range(B)] + [("lat", b) for b in range(B)]
           + [("E", b) for b in range(B)] + [("F", b) for b in range(B)])
LN = {key: n for n, key in enumerate(LN_KEYS)}


def lane_a_tasks():
    t = [("xT", "A", b) for b in range(B)] + [("rb", b) for b in range(B)]
    t += [("ctxT",), ("mediaT",)]
    for b in range(B):
        t += [("xT", "B", b), ("qT0", b)]
    for tt in range(TILES):
        t += [("pT", tt, 0), ("pT", tt, 2)]
        if tt % NT == 1 and tt > NT:
            t += [("cT", tt // NT - 1)]
    t += [("cT", B - 1)]
    t += [("xT", "C", b) for b in range(B)]
    t += [("xT", "D", b) for b in range(B)] + [("qT", b) for b in range(B)]
    t += [("latT", b) for b in range(B)]
    t += [("xT", "F", b) for b in range(B)] + [("gn", n) for n in range(3)]
    for c in range(CYCLES):
        for layer in range(4):
            t += [("cn", c, layer, b) for b in range(B)]
    return {key: n for n, key in enumerate(t)}


def lane_v_tasks():
    t = [("oA", b) for b in range(B)]
    t += [("k0",), ("v0",), ("cb0",), ("cb1",)]
    for tt in range(TILES):
        t += [("pT", tt, 1), ("pT", tt, 3)]
        if tt % NT == 2 and tt > NT:
            t += [("yB", tt // NT - 1)]
    t += [("yB", B - 1)]
    t += [("router", b) for b in range(B)]
    t += [("down", b, e) for b in range(B) for e in range(EXPERTS)]
    t += [("kv", b) for b in range(B)] + [("oD", b, h) for b in range(B) for h in range(2)]
    for c in range(CYCLES):
        t += [("twist", c, b) for b in range(B)]
    t += [("back", b) for b in range(B)]
    return {key: n for n, key in enumerate(t)}


LA, LV = lane_a_tasks(), lane_v_tasks()

SLOTS = 2 * KB
STEPS = PAIRS
MAX_UNITS = {0: [0], 1: [1, 2], 2: [3, 4], 3: [5], 4: [6, 7], 5: [8, 9]}


def step_tasks(p):
    t = {}
    if p + 2 < PAIRS:
        t[0], t[3], t[5] = [("Q", p + 2)], [("K", p + 2)], [("Kt", p + 2)]
    if p + 1 < PAIRS:
        t[6] = [("c", p + 1)]
    b, hp = divmod(p, NHP)
    if b + 1 < B and hp < KB:
        t[2] = [("V", b + 1, 2 * hp)]
        t[7] = [("V", b + 1, 2 * hp + 1)]
    if p:
        t[8] = [("oT", p - 1)]
    if b and hp == 0:
        t[9] = [("yE", b - 1)]
    return t


def splits(tasks, slot):
    now = [(key, 0) for key in tasks.get(slot, []) if key[0] in ("Q", "K", "Kt")]
    return ([(key, 1) for key in tasks.get(slot - 1, []) if key[0] in ("Q", "K")] + now
            + [(key, 1) for key, _ in now if key[0] == "Kt"])


PROLOGUE = ([("V", 0, u) for u in range(2 * KB)] + [("Q", 0), ("K", 0), ("Kt", 0), ("Q", 1), ("K", 1), ("Kt", 1)]
            + [("c", 0)])
EPILOGUE = [("oT", PAIRS - 1), ("yE", B - 1)]


def proj_tasks():
    t = list(PROLOGUE)
    for p in range(STEPS):
        for slot in range(SLOTS):
            t += step_tasks(p).get(slot, [])
    return {key: n for n, key in enumerate(t + EPILOGUE)}


PJ = proj_tasks()


def decoder(nc, x, ctx, wq0, bq0, wk0, bk0, wv0, bv0, wo0, bo0, w_router, w_g, w_u, w_d, s_g, s_u, s_d, w_qkv,
            med_w, med_b, lat_w, lat_b, wq1, bq1, wkv1, bkv1, wout1, bout1,
            cw1, cb1_, cw2, cb2_, cw3, cb3_, cw4, cb4_, gw1, gb1, gw2, gb2, gw3, gb3, arange, out):
    es = ExitStack()
    with es:
        def sb(name, shape, dt=F32):
            return es.enter_context(nc.sbuf_tensor(name, shape, dt))

        def sem(name):
            return es.enter_context(nc.semaphore(name))

        X_EVEN, X_ODD = sb("X_EVEN", [P, TILES, D]), sb("X_ODD", [P, TILES, D])
        XS = {"0": X_EVEN, "A": X_ODD, "B": X_EVEN, "C": X_ODD, "D": X_EVEN, "E": X_ODD}
        XT = sb("XT", [P, B, S])
        Y = sb("Y", [P, B, NT, D])
        BIG = sb("BIG", [P, 6656])
        REG = sb("REG", [P, 6400])
        st = sb("st", [P, 2, NT, 6])
        mv = sb("mv", [P, len(LN), NT, 2])
        ve = sb("ve", [P, len(LN), NT])
        rs = sb("rs", [P, len(LN), NT])
        ident = sb("ident", [P, P])
        ones = sb("ones", [P, P])
        half_neg = sb("half_neg", [P, NT])
        zero1 = sb("zero1", [P, 1])
        eps1 = sb("eps1", [P, 1])
        lnb = sb("lnb", [P, 1])
        hmask = sb("hmask", [P, NH])
        hmask_s = sb("hmask_s", [P, NH])
        iota = sb("iota", [P, E])
        twist = sb("twist", [P, P])
        ctx_sb = sb("ctx_sb", [CK, B, D])
        wq0s, wk0s, wv0s, wo0s = (sb(n, [P, P]) for n in ("wq0s", "wk0s", "wv0s", "wo0s"))
        b0s = sb("b0s", [P, 3])
        bo0s = sb("bo0s", [P, D])
        wqkvT = sb("wqkvT", [P, 3, P])
        wrT = sb("wrT", [P, E])
        lnw = sb("lnw", [P, 4])
        wq1s = sb("wq1s", [P, INNER])
        wout1s = sb("wout1s", [P, INNER // P, D])
        b1s = sb("b1s", [P, 3, INNER // P])
        bout1s = sb("bout1s", [P, D])
        CB0, CB1 = bo0s, bout1s
        bv0b = sb("bv0b", [P, P])
        cn1, cn2, cn3, cn4 = sb("cn1", [P, P]), sb("cn2", [P, 64]), sb("cn3", [64, 32]), sb("cn4", [32, P])
        gn1, gn2, gn3 = sb("gn1", [P, 64]), sb("gn2", [64, 32]), sb("gn3", [32, P])
        cnb, gnb = sb("cnb", [P, 4]), sb("gnb", [P, 3])
        w4col = sb("w4col", [32, 2])
        ar1 = sb("ar1", [P, 1])
        ss = sb("ss", [P, TILES])
        rn = sb("rn", [P, TILES])
        rsum = sb("rsum", [P, TILES])
        rinv = sb("rinv", [P, TILES])
        v0x = sb("v0x", [CK, B, NH, DH + 1])
        mx0 = sb("mx0", [P, 2, NH])
        r0 = sb("r0", [P, 2, NH])
        lg = sb("lg", [P, B, NT, E])
        top = sb("top", [P, B, NT, E])
        topi = sb("topi", [P, B, NT, E], U32)
        topf = sb("topf", [P, B, NT, 2])
        dl = sb("dl", [P, B, NT])
        th0 = sb("th0", [P, B, NT])
        wtop = sb("wtop", [P, B, 2, NT])
        eq = sb("eq", [P, 2, NT, E])
        comb = sb("comb", [P, B, NT, E])
        kse = sb("kse", [P, B])
        gsum = sb("gsum", [P, B])
        gact1, gact2 = sb("gact1", [64, B]), sb("gact2", [32, B])
        gth = sb("gth", [P, B])
        cA, cB = sb("cA", [P, 1]), sb("cB", [P, B])
        cbias = sb("cbias", [P, 2])
        MEDT = sb("MEDT", [P, B, KEYS_PAD - S])
        QA = [[sb(f"QA{r}{h}", [P, S], F32R) for h in range(2)] for r in range(3)]
        KA = [[sb(f"KA{r}{h}", [P, KEYS_PAD], F32R) for h in range(2)] for r in range(3)]
        QB = [[sb(f"QB{r}{h}", [P, S], F32R) for h in range(2)] for r in range(3)]
        KBt = [[sb(f"KB{r}{h}", [P, KEYS_PAD], F32R) for h in range(2)] for r in range(3)]
        mxm = sb("mxm", [P, 2, 2, NT])
        mxt = sb("mxt", [P, 2, 2, NT])
        cmx = sb("cmx", [P, 2, 2, NT])
        crow = sb("crow", [2 * NT, 2, P])
        rden = sb("rden", [P, 2, NT])

        VXA = sb("VXA", [P, 2, KB, NH, DW + 1])

        NW = HB * EXPERTS * D
        vflat = VXA[:].rearrange("p a j h d -> p (a j h d)")
        wgT, wuT, wdT = (vflat[:, NW * n:NW * n + NW].rearrange("p (k d) -> p k d", d=P) for n in range(3))
        DG = Y[:].rearrange("p b t d -> p b (t d)")
        RBv = BIG[:, 0:2048].rearrange("p (b n) -> p b n", b=B)
        EX = BIG[:, 2048:6144].rearrange("p (r t n) -> p r t n", r=2, t=NT)
        GX = REG[:, 0:1024].rearrange("p (r n) -> p r n", r=2)
        SM = BIG[:, 0:2 * NH * CK].rearrange("p (r n) -> p r n", r=2)
        PT0 = BIG[0:CK, 2560:2560 + 2 * NH * P].rearrange("p (r h n) -> p r h n", r=2, h=NH)
        QT0 = vflat[:, 3 * NW:3 * NW + 2048].rearrange("p (b n) -> p b n", b=B)
        ctxT, k0T = (vflat[:, 3 * NW + n:3 * NW + n + B * CK].rearrange("p (b k) -> p b k", b=B) for n in (2432, 2432 + B * CK))
        ctxn = BIG[0:CK, 2560:2560 + B * D].rearrange("p (b d) -> p b d", b=B)
        KBD = REG[:, 0:B * NH * CK].rearrange("p (b h k) -> p b h k", b=B, h=NH)
        bv1b = REG[:, 0:NHP * P].rearrange("p (c n) -> p c n", c=NHP)
        C0, C0T = Y, XT
        SG = BIG[:, 0:2048].rearrange("p (r n) -> p r n", r=4)
        HX = BIG[:, 2048:5120].rearrange("p (r k n) -> p r k n", r=3, k=HB)
        QK = BIG[:, 0:4096].rearrange("p (b t n) -> p b t n", b=B, t=NT)
        VXv = REG[:, 2048:2048 + B * NT * (D + 1)].rearrange("p (b t n) -> p b t n", b=B, t=NT)
        KVB = BIG[:, 4096:4096 + B * (D + NH)].rearrange("p (b n) -> p b n", b=B)
        SSQ = BIG[:, 4672:4672 + B * 128].rearrange("p (b n) -> p b n", b=B)
        SQ = REG[:, 0:1024].rearrange("p (r t n) -> p r t n", r=2, t=2)
        QTD = XT
        LAT, LATT = Y, XT
        PX = BIG[:, 0:2048].rearrange("p (r n) -> p r n", r=4)
        CT = BIG[:, 2048:2048 + 2 * NT * P].rearrange("p (r t n) -> p r t n", r=2, t=NT)
        OT = REG[:, 0:NHP * S].rearrange("p (c n) -> p c n", c=NHP)
        wkv1s = REG[:, 6400 - 2 * INNER:6400]
        FS = XT
        H1 = BIG[:, 0:2048].rearrange("p (b n) -> p b n", b=B)
        H2 = BIG[0:64, 2048:4096].rearrange("p (b n) -> p b n", b=B)
        H3 = BIG[0:32, 4096:6144].rearrange("p (b n) -> p b n", b=B)
        TH = REG[:, 0:2048].rearrange("p (b n) -> p b n", b=B)
        CP = REG[:, 2048:4096].rearrange("p (b n) -> p b n", b=B)

        PS = es.enter_context(nc.psum_tensor("PS", [P, 8, 512], F32))

        def bank_a(n):
            return PS[:, 4 + n % 2, :]

        def bank_v(n):
            return PS[:, 6 + n % 2, :]

        x_in = [sem(f"x_in{b}") for b in range(B)]
        ctx_in, w0_in, moe_in, qkv_in, perc_in, cn_in, wkv_in = (sem(n) for n in ("ctx_in", "w0_in", "moe_in", "qkv_in", "perc_in", "cn_in", "wkv_in"))
        consts = sem("consts")
        a_full, a_free, v_full, v_free = (sem(n) for n in ("a_full", "a_free", "v_full", "v_free"))
        var_ready, rstd_ready, x_ready = sem("var_ready"), sem("rstd_ready"), sem("x_ready")
        dve_seq, act_seq = sem("dve_seq"), sem("act_seq")
        sq_ready, ss_ready, rn_ready, diag_ready = (sem(n) for n in ("sq_ready", "ss_ready", "rn_ready", "diag_ready"))
        dots_ready, sim_ready, exp_ready = sem("dots_ready"), sem("sim_ready"), sem("exp_ready")
        xr_ready = sem("xr_ready")
        kbd_ready, bvb_ready = sem("kbd_ready"), sem("bvb_ready")
        s0_ready, s0_sub, p0_ready, pv0_full, pv0_free = (sem(n) for n in ("s0_ready", "s0_sub", "p0_ready", "pv0_full", "pv0_free"))
        dl_ready, th_ready = sem("dl_ready"), sem("th_ready")
        g_ready, u_ready, silu_ready, h_ready = (sem(n) for n in ("g_ready", "u_ready", "silu_ready", "h_ready"))
        qkv_ready, qk_copied, vx_ready, sqq_ready, ssq_ready, lnorm_ready, qkn_ready, kvb_ready = (
            sem(n) for n in ("qkv_ready", "qk_copied", "vx_ready", "sqq_ready", "ssq_ready", "lnorm_ready", "qkn_ready", "kvb_ready"))
        pj_full, pj_free, hi_ready, lo_ready = (sem(n) for n in ("pj_full", "pj_free", "hi_ready", "lo_ready"))
        mu_full, mu_free, cm_ready = (sem(n) for n in ("mu_full", "mu_free", "cm_ready"))
        c_in = [sem(f"c_in{r}") for r in range(3)]
        sw_ready, pw_ready, pv_ready, on_ready = (sem(n) for n in ("sw_ready", "pw_ready", "pv_ready", "on_ready"))
        gs_ready, coef_ready, state_ready, out_sem = (sem(n) for n in ("gs_ready", "coef_ready", "state_ready", "out_sem"))

        block = es.enter_context(nc.Block())

        N_W0, N_MOE, N_QKV, N_PERC, N_CN = 16 * 8, 16 * 6, 16 * 2, 16 * 10, 16 * 15
        N_CONST = 17
        N_POOL = 22

        def xtile(k, b):
            return XS[k][:, NT * b:NT * b + NT, :]

        @block.sync
        def _(sp):
            for b in range(B):
                sp.dma_start(XS["0"][:, NT * b:NT * b + NT, :], x[b].rearrange("(t p) d -> p t d", p=P)).then_inc(x_in[b], 16)
            sp.dma_start(ctx_sb[:], ctx.rearrange("b k d -> k b d")).then_inc(ctx_in, 16)
            for dst, src in ((wq0s, wq0), (wk0s, wk0), (wv0s, wv0), (wo0s, wo0)):
                sp.dma_start(dst[:], src).then_inc(w0_in, 16)
            for n, src in enumerate((bq0, bk0, bv0)):
                sp.dma_start(b0s[:, n:n + 1], src.rearrange("(p a) -> p a", a=1)).then_inc(w0_in, 16)
            sp.dma_start(bo0s[:], bo0.partition_broadcast(P)).then_inc(w0_in, 16)
            ne = HB * E * P
            for dst, src, shared in ((wgT, w_g, s_g), (wuT, w_u, s_u), (wdT, w_d, s_d)):
                flat = dst.rearrange("p k d -> p (k d)")
                sp.dma_start(flat[:, 0:ne], src).then_inc(moe_in, 16)
                sp.dma_start(flat[:, ne:], shared).then_inc(moe_in, 16)
            sp.dma_start(wqkvT[:].rearrange("p k d -> p (k d)"), w_qkv).then_inc(qkv_in, 16)
            sp.dma_start(wrT[:], w_router).then_inc(qkv_in, 16)
            for n, src in enumerate((med_w, med_b, lat_w, lat_b)):
                sp.dma_start(lnw[:, n:n + 1], src.rearrange("(p a) -> p a", a=1)).then_inc(perc_in, 16)
            sp.dma_start(wq1s[:], wq1).then_inc(perc_in, 16)
            sp.dma_start(wout1s[:], wout1).then_inc(perc_in, 16)
            sp.dma_start(b1s[:, 0, :], bq1).then_inc(perc_in, 16)
            sp.dma_start(b1s[:, 1, :], bkv1[:, 0:NHP]).then_inc(perc_in, 16)
            sp.dma_start(b1s[:, 2, :], bkv1[:, NHP:2 * NHP]).then_inc(perc_in, 16)
            sp.dma_start(bout1s[:], bout1.partition_broadcast(P)).then_inc(perc_in, 16)
            for dst, src in ((cn1, cw1), (cn2, cw2), (cn3, cw3), (gn1, gw1), (gn2, gw2)):
                sp.dma_start(dst[:], src).then_inc(cn_in, 16)
            sp.dma_start(w4col[:, 0:1], cw4).then_inc(cn_in, 16)
            sp.dma_start(w4col[:, 1:2], gw3).then_inc(cn_in, 16)
            for n, src in enumerate((cb1_, cb2_, cb3_)):
                sp.dma_start(cnb[0:src.shape[0], n:n + 1], src.rearrange("(p a) -> p a", a=1)).then_inc(cn_in, 16)
            sp.dma_start(cnb[:, 3:4], cb4_.partition_broadcast(P)).then_inc(cn_in, 16)
            for n, src in enumerate((gb1, gb2)):
                sp.dma_start(gnb[0:src.shape[0], n:n + 1], src.rearrange("(p a) -> p a", a=1)).then_inc(cn_in, 16)
            sp.dma_start(gnb[:, 2:3], gb3.partition_broadcast(P)).then_inc(cn_in, 16)
            sp.dma_start(ar1[:], arange.partition_broadcast(P)).then_inc(cn_in, 16)
            sp.wait_ge(s0_ready, TILES)
            sp.dma_start(wkv1s, wkv1).then_inc(wkv_in, 16)
            for p in range(PAIRS):
                r = p % 3
                sp.wait_ge(pj_free, PJ["c", p] + 1)
                for h in range(2):
                    row = DW * (1 - h)
                    sp.dma_start(QB[r][h][row:row + 1, :].bitcast(F32).rearrange("a (t n) -> a t n", t=NT),
                                 crow[NT * h:NT * h + NT, p % 2, :]).then_inc(c_in[r], 16)
            for b in range(B):
                sp.wait_ge(x_ready, LN["F", b] + 1)
                sp.dma_start(out[b].rearrange("(t p) d -> p t d", p=P), XS["0"][:, NT * b:NT * b + NT, :]).then_inc(out_sem, 16)
            sp.wait_ge(out_sem, 16 * B)

        @block.gpsimd
        def _(pool):
            pool.memset(ident[:], 0.0).then_inc(consts, 1)
            pool.memset(ones[:], 1.0).then_inc(consts, 1)
            pool.memset(half_neg[:], -0.5).then_inc(consts, 1)
            pool.memset(eps1[:], LN_EPS).then_inc(consts, 1)
            pool.memset(lnb[:], 0.5 * 11.090354888959125).then_inc(consts, 1)
            pool.memset(zero1[:], 0.0).then_inc(consts, 1)
            pool.memset(hmask[:], 1.0).then_inc(consts, 1)
            pool.memset(twist[:], 0.0).then_inc(consts, 1)
            pool.memset(v0x[:], 1.0).then_inc(consts, 1)
            pool.iota(topi[:, 0, 0, :], pattern=[[1, E]], base=0, channel_multiplier=0).then_inc(consts, 1)
            pool.wait_ge(consts, 10)
            pool.affine_select(out=ident[:], in_=ident[:], compare_op=ALU.not_equal, fill=1.0, base=0,
                               pattern=[[-1, P]], channel_multiplier=1).then_inc(consts, 1)
            pool.affine_select(out=hmask[:], in_=hmask[:], compare_op=ALU.is_ge, fill=0.0, base=0,
                               pattern=[[-DH, NH]], channel_multiplier=1).then_inc(consts, 1)
            pool.wait_ge(consts, 12)
            pool.affine_select(out=hmask[:], in_=hmask[:], compare_op=ALU.is_ge, fill=0.0, base=DH - 1,
                               pattern=[[DH, NH]], channel_multiplier=-1).then_inc(consts, 1)
            for n, (fill, off) in enumerate(((1.0, -64), (-1.0, -64), (-1.0, 64), (1.0, 64))):
                cols = twist[:, 32 * n:32 * n + 32]
                pool.affine_select(out=cols, in_=cols, compare_op=ALU.not_equal, fill=fill, base=off - 32 * n,
                                   pattern=[[-1, 32]], channel_multiplier=1).then_inc(consts, 1)
            setup = [0]

            def settled(ins):
                setup[0] += 1
                ins.then_inc(bvb_ready, 1)
                pool.wait_ge(bvb_ready, setup[0])

            def last_layers():
                pool.wait_ge(cn_in, N_CN)
                settled(pool.tensor_copy(cn4[:], w4col[:, 0:1].broadcast_to([32, P])))
                settled(pool.tensor_copy(gn3[:], w4col[:, 1:2].broadcast_to([32, P])))

            def rstd(key):
                n = LN[key]
                rows = CK if key[0] == "media" else P
                pool.wait_ge(var_ready, n + 1)
                pool.tensor_tensor(rs[0:rows, n, :], ve[0:rows, n, :], half_neg[0:rows, 0:NT], ALU.pow).then_inc(rstd_ready, 1)

            for b in range(B):
                pool.wait_ge(ss_ready, b + 1)
                pool.tensor_tensor(rn[:, NT * b:NT * b + NT], ss[:, NT * b:NT * b + NT], half_neg[:, 0:NT], ALU.pow).then_inc(rn_ready, 1)
            pool.wait_ge(w0_in, N_W0)
            settled(pool.tensor_copy(bv0b[:], b0s[:, 2:3].broadcast_to([P, P])))
            for r in range(3):
                for h in range(2):
                    lo = DW * (1 - h)
                    settled(pool.memset(QB[r][h][lo:lo + DW, :].bitcast(F32), 0.0))
                    settled(pool.memset(KBt[r][h][lo:lo + DW, :].bitcast(F32), 0.0))
            for r in range(3):
                for h in range(2):
                    lo = DW * (1 - h)
                    settled(pool.memset(KBt[r][h][lo:lo + 1, :].bitcast(F32), 1.0))
            for b in range(B):
                rstd(("A", b))
            rstd(("media", 0))
            pool.wait_ge(v_free, LV["cb0",] + 1)
            for b in range(B):
                pool.wait_ge(a_full, LA["xT", "B", b] + 1)
                pool.tensor_tensor(xtile("A", b), xtile("A", b), CB0[:].unsqueeze(1).broadcast_to([P, NT, D]), ALU.add).then_inc(xr_ready, 1)
            for stage in "BCD":
                for b in range(B):
                    rstd((stage, b))
            pool.wait_ge(v_free, LV["cb1",] + 1)
            for b in range(B):
                rstd(("lat", b))
                pool.wait_ge(x_ready, LN["lat", b] + 1)
                pool.tensor_tensor(xtile("D", b), xtile("D", b), CB1[:].unsqueeze(1).broadcast_to([P, NT, D]), ALU.add).then_inc(xr_ready, 1)
            last_layers()
            settled(pool.memset(VXA[:], 1.0))

            for p in range(STEPS):
                if p % NHP == 1 and p > 1:
                    rstd(("E", p // NHP - 1))
            rstd(("E", B - 1))
            for b in range(B):
                rstd(("F", b))

        @block.scalar
        def _(act):
            def evac(key, dst, rows=P, cols=512, func=ACT.Copy, shape=None, **kw):
                n = LA[key]
                act.wait_ge(a_full, n + 1)
                src = bank_a(n)[0:rows, 0:cols]
                if shape:
                    src = src.rearrange(shape[0], **shape[1])
                act.activation(dst, src, func, **kw).then_inc(a_free, 1)

            act.wait_ge(consts, N_CONST)
            for b in range(B):
                act.wait_ge(x_in[b], 16)
                for t in range(NT):
                    tt = NT * b + t
                    act.activation(BIG[:, 2048 + 128 * tt:2048 + 128 * tt + 128], XS["0"][:, tt, :], ACT.Square,
                                   accum_out=ss[:, tt:tt + 1]).then_inc(sq_ready, 1)
            for b in range(B):
                evac(("xT", "A", b), XT[:, b, :])
            for b in range(B):
                evac(("rb", b), RBv[:, b, :])
                for j in range(NT):
                    act.wait_ge(sim_ready, NT * b + j + 1)
                    act.activation(EX[:, b % 2, j, :], EX[:, b % 2, j, :], ACT.Exp,
                                   accum_out=rsum[:, NT * b + j:NT * b + j + 1]).then_inc(exp_ready, 1)
            evac(("ctxT",), ctxT[:].rearrange("p b k -> p (b k)"), cols=B * CK)
            act.wait_ge(perc_in, N_PERC)
            evac(("mediaT",), MEDT[:, :, 0:CK], cols=B * CK, shape=("p (b k) -> p b k", {"k": CK}),
                 func=ACT.Identity, scale=lnw[:, 0:1], bias=lnw[:, 1:2])
            for b in range(B):
                evac(("xT", "B", b), XT[:, b, :])
                evac(("qT0", b), QT0[:, b, :], func=ACT.Identity, bias=b0s[:, 0:1])

            def exp0(tt):
                act.wait_ge(s0_sub, tt + 1)
                act.activation(SM[:, tt % 2, :], SM[:, tt % 2, :], ACT.Exp, scale=SCALE_N).then_inc(p0_ready, 1)

            exp0(0)
            for tt in range(TILES):
                if tt >= 2:
                    act.wait_ge(pv0_full, tt - 1)
                evac(("pT", tt, 0), PT0[:, tt % 2, 0:4, :].rearrange("p h n -> p (h n)"), rows=CK)
                evac(("pT", tt, 2), PT0[:, tt % 2, 8:12, :].rearrange("p h n -> p (h n)"), rows=CK)
                if tt + 1 < TILES:
                    exp0(tt + 1)
                if tt % NT == 1 and tt > NT:
                    evac(("cT", tt // NT - 1), C0T[:, tt // NT - 1, :])
            evac(("cT", B - 1), C0T[:, B - 1, :])
            for b in range(B):
                evac(("xT", "C", b), XT[:, b, :])
                act.wait_ge(dl_ready, b + 1)
                act.activation(th0[:, b, :], dl[:, b, :], ACT.Tanh, scale=0.5).then_inc(th_ready, 1)
            for n in range(B * EXPERTS * HB):
                act.wait_ge(g_ready, n + 1)
                if n >= 4:
                    act.wait_ge(h_ready, n - 3)
                act.activation(SG[:, n % 4, :], PS[:, n % 2, :], ACT.Silu).then_inc(silu_ready, 1)
            for b in range(B):
                evac(("xT", "D", b), XT[:, b, :])
            act.wait_ge(h_ready, B * EXPERTS * HB)
            act.wait_ge(v_full, LV["down", B - 1, E] + 1)
            for b in range(B):
                act.wait_ge(qkv_ready, NT * (b + 1))
                act.activation(QK[:, b], PS[:, 0:NT, 0:2 * D], ACT.Copy).then_inc(qk_copied, 1)
                act.wait_ge(qk_copied, b + 1)
                if b >= 1:
                    act.wait_ge(ssq_ready, b)
                act.activation(SQ[:, 0].rearrange("p t n -> p (t n)"), QK[:, b].rearrange("p t n -> p (t n)")[:, 0:512], ACT.Square).then_inc(sqq_ready, 1)
                act.activation(SQ[:, 1].rearrange("p t n -> p (t n)"), QK[:, b].rearrange("p t n -> p (t n)")[:, 512:1024], ACT.Square).then_inc(sqq_ready, 1)
            for b in range(B):
                act.wait_ge(ssq_ready, b + 1)
                act.activation(SSQ[:, b], SSQ[:, b], ACT.Ln, scale=LN_SCALE).then_inc(act_seq, 1)
                act.wait_ge(act_seq, 3 * b + 1)
                act.activation(SSQ[:, b], SSQ[:, b], ACT.Exp, scale=-0.5, bias=lnb[:]).then_inc(lnorm_ready, 1)
                act.wait_ge(qkn_ready, b + 1)
                qk = QK[:, b].rearrange("p t n -> p (t n)")
                act.activation(qk, qk, ACT.Exp).then_inc(act_seq, 1)
                act.wait_ge(act_seq, 3 * b + 2)
                act.activation(qk, qk, ACT.Ln, bias=ones[:, 0:1]).then_inc(act_seq, 1)
            for b in range(B):
                evac(("qT", b), QTD[:, b, :])
            for b in range(B):
                evac(("latT", b), LATT[:, b, :], func=ACT.Identity, scale=lnw[:, 2:3], bias=lnw[:, 3:4])
            act.activation(MEDT[:, :, CK:CK + 1], MEDT[:, :, CK - 1:CK], ACT.Copy).then_inc(act_seq, 1)

            def hi(key, h):
                kind, p = key
                r, hp = p % 3, p % NHP
                n = PJ[key]
                own, other = slice(DW * h, DW * h + DW), slice(DW * (1 - h), DW * (1 - h) + DW)
                act.wait_ge(pj_full, n + 1)
                if p >= 3 and kind == "Q" and h == 0:
                    act.wait_ge(sw_ready, SLOTS * (p - 2))
                if kind == "Q":
                    dsts, width, bias = (QA[r][h][own, :], QB[r][h][own, :]), S, b1s[own, 0, hp:hp + 1]
                elif kind == "K":
                    dsts, width, bias = (KA[r][h][own, 0:S], KA[r][h][other, 0:S]), S, b1s[own, 1, hp:hp + 1]
                else:
                    dsts, width, bias = (KA[r][h][own, S:KEYS_PAD], KA[r][h][other, S:KEYS_PAD]), KEYS_PAD - S, b1s[own, 1, hp:hp + 1]
                for dst in dsts:
                    act.activation(dst, PS[own, 6 + n % 2, 0:width], ACT.Identity, bias=bias).then_inc(hi_ready, 1)

            act.wait_ge(a_full, LA["latT", B - 1] + 1)
            for p in range(2):
                for kind in ("Q", "K", "Kt"):
                    for h in range(2):
                        hi((kind, p), h)
            for p in range(STEPS):
                tasks = step_tasks(p)
                for slot in range(SLOTS):
                    g = SLOTS * p + slot
                    j = slot % KB
                    rows = min(P, KEYS - P * j)
                    act.wait_ge(sw_ready, g + 1)
                    if g >= 4:
                        act.wait_ge(pv_ready, g - 3)
                    act.activation(PX[0:rows, g % 4, :], PS[0:rows, g % 2, :], ACT.Exp, scale=SCALE_W).then_inc(pw_ready, 1)
                    for key, h in splits(tasks, slot):
                        hi(key, h)
            for b in range(B):
                evac(("xT", "F", b), FS[:, b, :])
            act.wait_ge(cn_in, N_CN)
            act.wait_ge(coef_ready, 1)
            evac(("gn", 0), gact1[:], rows=64, cols=B, func=ACT.Gelu, scale=1.0 / S, bias=gnb[0:64, 0:1])
            evac(("gn", 1), gact2[:], rows=32, cols=B, func=ACT.Gelu, bias=gnb[0:32, 1:2])
            evac(("gn", 2), gth[:], cols=B, func=ACT.Tanh, scale=0.5, bias=cbias[:, 1:2])
            for c in range(CYCLES):
                for layer, (dst, rows, func, scale, bias) in enumerate((
                        (H1, P, ACT.Gelu, 1.0, cnb[:, 0:1]), (H2, 64, ACT.Gelu, 1.0, cnb[0:64, 1:2]),
                        (H3, 32, ACT.Gelu, 1.0, cnb[0:32, 2:3]), (TH, P, ACT.Tanh, 0.5, cbias[:, 0:1]))):
                    for b in range(B):
                        if layer == 3 and c:
                            act.wait_ge(state_ready, B * (c - 1) + b + 1)
                        evac(("cn", c, layer, b), dst[0:rows, b, :], rows=rows, func=func, scale=scale, bias=bias)

        @block.vector
        def _(dve):
            count = [0]

            def link(ins):
                count[0] += 1
                ins.then_inc(dve_seq, 1)
                dve.wait_ge(dve_seq, count[0])

            def norm_stats(key, src, rows=P):
                n = LN[key]
                for t in range(NT):
                    ins = dve.bn_stats(out=st[0:rows, n % 2, t, :], in_=src[0:rows, t, :])
                link(ins)
                for t in range(NT):
                    ins = dve.bn_aggr(out=mv[0:rows, n, t, :], in_=st[0:rows, n % 2, t, :])
                link(ins)
                dve.tensor_scalar_add(ve[0:rows, n, :], mv[0:rows, n, :, 1], LN_EPS).then_inc(var_ready, 1)

            def norm_apply(key, src, dst, rows=P):
                n = LN[key]
                dve.wait_ge(rstd_ready, n + 1)
                for t in range(NT):
                    ins = dve.tensor_scalar(dst[0:rows, t, :], src[0:rows, t, :], mv[0:rows, n, t, 0:1], rs[0:rows, n, t:t + 1],
                                            ALU.subtract, ALU.mult)
                ins.then_inc(x_ready, 1)

            def norm(key, src, dst, rows=P):
                norm_stats(key, src, rows)
                norm_apply(key, src, dst, rows)

            dve.wait_ge(consts, N_CONST)
            dve.tensor_copy(iota[:], topi[:, 0, 0, :])
            link(dve.tensor_scalar_mul(hmask_s[:], hmask[:], SCALE_N))
            for b in range(B):
                dve.wait_ge(sq_ready, NT * (b + 1))
                cols = slice(NT * b, NT * b + NT)
                dve.tensor_scalar_max(ss[:, cols], ss[:, cols], 1e-37).then_inc(ss_ready, 1)
            for b in range(B):
                dve.wait_ge(rn_ready, b + 1)
                dve.tensor_tensor(DG[:, b, :].rearrange("p (t n) -> p t n", t=NT), ident[:].unsqueeze(1).broadcast_to([P, NT, P]),
                                  rn[:, NT * b:NT * b + NT].unsqueeze(2).broadcast_to([P, NT, P]), ALU.mult).then_inc(diag_ready, 1)

            def sims(b):
                for j in range(NT):
                    n = NT * b + j
                    dve.wait_ge(a_free, LA["rb", b] + 1)
                    link(dve.tensor_scalar(GX[:, n % 2, :], RBv[:, b, :], rn[:, n:n + 1], 1.0 / COS_EPS, ALU.mult, ALU.min))
                    dve.wait_ge(dots_ready, n + 1)
                    dve.wait_ge(sq_ready, TILES)
                    if b >= 2:
                        dve.wait_ge(v_full, LV["oA", b - 2] + 1)
                    dve.tensor_tensor(EX[:, b % 2, j, :], PS[:, j, :], GX[:, n % 2, :], ALU.mult).then_inc(sim_ready, 1)

            def out_a(b):
                n = LV["oA", b]
                cols = slice(NT * b, NT * b + NT)
                dve.wait_ge(exp_ready, NT * (b + 1))
                link(dve.reciprocal(rinv[:, cols], rsum[:, cols]))
                dve.wait_ge(v_full, n + 1)
                for t in range(NT):
                    ins = dve.scalar_tensor_tensor(Y[:, b, t, :], bank_v(n)[:, P * t:P * t + P], rinv[:, NT * b + t:NT * b + t + 1],
                                                   XS["0"][:, NT * b + t, :], ALU.mult, ALU.add)
                ins.then_inc(v_free, 1)
                dve.wait_ge(v_free, n + 1)
                link(dve.tensor_tensor(Y[:, b], Y[:, b], xtile("0", b), ALU.add))
                norm(("A", b), Y[:, b], xtile("A", b))

            sims(0)
            for b in range(B):
                if b + 1 < B:
                    sims(b + 1)
                out_a(b)
            dve.wait_ge(ctx_in, 16)
            norm(("media", 0), ctx_sb, ctxn, rows=CK)
            n = LV["k0",]
            dve.wait_ge(v_full, n + 1)
            dve.wait_ge(w0_in, N_W0)
            dve.tensor_scalar_add(k0T[:].rearrange("p b k -> p (b k)"), bank_v(n)[:, 0:B * CK], b0s[:, 1:2]).then_inc(v_free, 1)
            n = LV["v0",]
            dve.wait_ge(v_full, n + 1)
            dve.tensor_copy(v0x[:, :, :, 0:DH], bank_v(n)[0:CK, :].rearrange("p (b h d) -> p b h d", b=B, h=NH)).then_inc(v_free, 1)
            n = LV["cb0",]
            dve.wait_ge(v_full, n + 1)
            dve.tensor_tensor(CB0[:], bank_v(n)[:, 0:D], bo0s[:], ALU.add).then_inc(v_free, 1)
            dve.wait_ge(perc_in, N_PERC)
            dve.tensor_copy(bv1b, b1s[:, 2, :].unsqueeze(2).broadcast_to([P, NHP, P])).then_inc(kbd_ready, 1)
            n = LV["cb1",]
            dve.wait_ge(v_full, n + 1)
            dve.tensor_tensor(CB1[:], bank_v(n)[:, 0:D], bout1s[:], ALU.add).then_inc(v_free, 1)
            for b in range(B):
                dve.tensor_tensor(KBD[:, b], k0T[:, b, :].unsqueeze(1).broadcast_to([P, NH, CK]),
                                  hmask[:].unsqueeze(2).broadcast_to([P, NH, CK]), ALU.mult).then_inc(kbd_ready, 1)

            def max_sub(tt):
                r = tt % 2
                dve.wait_ge(s0_ready, tt + 1)
                wide = PS[:, 0:2, 0:6 * CK].rearrange("p a (h k) -> p a h k", k=CK)
                rest = PS[:, 2, 0:4 * CK].rearrange("p (h k) -> p h k", k=CK)
                dve.tensor_reduce(mx0[:, r, 0:12].rearrange("p (a h) -> p a h", a=2), wide, AX.X, ALU.max)
                link(dve.tensor_reduce(mx0[:, r, 12:16], rest, AX.X, ALU.max))
                if tt >= 2:
                    dve.wait_ge(v_full, LV["pT", tt - 2, 3] + 1)
                    dve.wait_ge(a_full, LA["pT", tt - 2, 2] + 1)
                sm = SM[:, r, :].rearrange("p (h k) -> p h k", k=CK)
                dve.tensor_tensor(sm[:, 0:12, :].rearrange("p (a h) k -> p a h k", a=2), wide,
                                  mx0[:, r, 0:12].rearrange("p (a h) -> p a h", a=2).unsqueeze(3).broadcast_to([P, 2, 6, CK]), ALU.subtract)
                dve.tensor_tensor(sm[:, 12:16, :], rest, mx0[:, r, 12:16].unsqueeze(2).broadcast_to([P, 4, CK]),
                                  ALU.subtract).then_inc(s0_sub, 1)

            def y_b(b):
                n = LV["yB", b]
                dve.wait_ge(v_full, n + 1)
                dve.wait_ge(xr_ready, b + 1)
                dve.tensor_tensor(Y[:, b], bank_v(n).rearrange("p (t d) -> p t d", t=NT), xtile("A", b), ALU.add).then_inc(v_free, 1)
                dve.wait_ge(v_free, n + 1)
                norm(("B", b), Y[:, b], xtile("B", b))

            def divide0(tt):
                b, t = divmod(tt, NT)
                dve.wait_ge(pv0_full, tt + 1)
                o = PS[:, 3, 0:NH * (DH + 1)].rearrange("p (h d) -> p h d", h=NH)
                link(dve.reciprocal(r0[:, tt % 2, :], o[:, :, DH]))
                dve.tensor_tensor(C0[:, b, t, :].rearrange("p (h d) -> p h d", h=NH), o[:, :, 0:DH],
                                  r0[:, tt % 2, :].unsqueeze(2).broadcast_to([P, NH, DH]), ALU.mult).then_inc(pv0_free, 1)

            max_sub(0)
            for tt in range(TILES):
                if tt + 1 < TILES:
                    max_sub(tt + 1)
                if tt >= 2:
                    dve.wait_ge(pv0_full, tt - 1)
                for g in (1, 3):
                    n = LV["pT", tt, g]
                    dve.wait_ge(v_full, n + 1)
                    dve.tensor_copy(PT0[:, tt % 2, 4 * g:4 * g + 4, :].rearrange("p h n -> p (h n)"), bank_v(n)[0:CK, :]).then_inc(v_free, 1)
                if tt:
                    divide0(tt - 1)
                if tt % NT == 2 and tt > NT:
                    y_b(tt // NT - 1)
            divide0(TILES - 1)
            y_b(B - 1)
            for b in range(B):
                n = LV["router", b]
                dve.wait_ge(v_full, n + 1)
                dve.tensor_copy(lg[:, b].rearrange("p t e -> p (t e)"), bank_v(n)[:, 0:NT * E]).then_inc(v_free, 1)
                dve.wait_ge(v_free, n + 1)
                for t in range(NT):
                    ins = dve.max(top[:, b, t, :], lg[:, b, t, :])
                link(ins)
                dve.tensor_tensor(dl[:, b, :], top[:, b, :, 1], top[:, b, :, 0], ALU.subtract).then_inc(dl_ready, 1)
                for t in range(NT):
                    ins = dve.max_index(topi[:, b, t, :], top[:, b, t, :], lg[:, b, t, :])
                link(ins)
                link(dve.tensor_copy(topf[:, b], topi[:, b, :, 0:2]))
                dve.wait_ge(th_ready, b + 1)
                dve.tensor_scalar(wtop[:, b, 0, :], th0[:, b, :], -0.5, 0.5, ALU.mult, ALU.add)
                dve.tensor_scalar(wtop[:, b, 1, :], th0[:, b, :], 0.5, 0.5, ALU.mult, ALU.add)
                for i in range(2):
                    ins = dve.tensor_tensor(eq[:, i], iota[:].unsqueeze(1).broadcast_to([P, NT, E]),
                                            topf[:, b, :, i].unsqueeze(2).broadcast_to([P, NT, E]), ALU.is_equal)
                link(ins)
                for i in range(2):
                    ins = dve.tensor_tensor(eq[:, i], eq[:, i], wtop[:, b, i, :].unsqueeze(2).broadcast_to([P, NT, E]), ALU.mult)
                link(ins)
                link(dve.tensor_tensor(comb[:, b], eq[:, 0], eq[:, 1], ALU.add))

            def gate(n):
                e_all, k = divmod(n, HB)
                dve.wait_ge(silu_ready, n + 1)
                dve.wait_ge(u_ready, n + 1)
                if e_all >= 3:
                    dve.wait_ge(v_full, LV["down", (e_all - 3) // EXPERTS, (e_all - 3) % EXPERTS] + 1)
                dve.tensor_tensor(HX[:, e_all % 3, k, :], PS[:, 2 + n % 2, :], SG[:, n % 4, :], ALU.mult).then_inc(h_ready, 1)

            def accumulate(e_all):
                b, e = divmod(e_all, EXPERTS)
                n = LV["down", b, e]
                dve.wait_ge(v_full, n + 1)
                if e == E:
                    dve.tensor_tensor(Y[:, b], bank_v(n).rearrange("p (t d) -> p t d", t=NT), Y[:, b], ALU.add).then_inc(v_free, 1)
                else:
                    for t in range(NT):
                        ins = dve.scalar_tensor_tensor(Y[:, b, t, :], bank_v(n)[:, P * t:P * t + P], comb[:, b, t, e:e + 1],
                                                       XS["B"][:, NT * b + t, :] if e == 0 else Y[:, b, t, :], ALU.mult, ALU.add)
                    ins.then_inc(v_free, 1)
                dve.wait_ge(v_free, n + 1)
                if e == E:
                    norm(("C", b), Y[:, b], xtile("C", b))

            for k in range(HB):
                gate(k)
            for e_all in range(B * EXPERTS):
                if e_all + 1 < B * EXPERTS:
                    for k in range(HB):
                        gate(HB * (e_all + 1) + k)
                accumulate(e_all)
            dve.memset(VXv[:, :, :, D:D + 1], 1.0)
            for b in range(B):
                dve.wait_ge(qk_copied, b + 1)
                dve.tensor_copy(VXv[:, b, :, 0:D], PS[:, 0:NT, 2 * D:3 * D]).then_inc(vx_ready, 1)
                dve.wait_ge(sqq_ready, 2 * b + 2)
                link(dve.tensor_reduce(SSQ[:, b], SQ.rearrange("p r t (h d) -> p (r t h) d", d=DH), AX.X, ALU.add))
                dve.tensor_scalar_max(SSQ[:, b], SSQ[:, b], L2_EPS ** 2).then_inc(ssq_ready, 1)
            for b in range(B):
                dve.wait_ge(lnorm_ready, b + 1)
                qk = QK[:, b].rearrange("p t (h d) -> p (t h) d", d=DH)
                dve.tensor_tensor(qk, qk, SSQ[:, b].unsqueeze(2).broadcast_to([P, NT * 2 * NH, DH]), ALU.mult).then_inc(qkn_ready, 1)
            for b in range(B):
                n = LV["kv", b]
                dve.wait_ge(v_full, n + 1)
                kv = bank_v(n)
                dve.tensor_tensor(KVB[:, b, 0:D].rearrange("p (h d) -> p h d", h=NH), kv[:, 0:D].rearrange("p (h d) -> p h d", h=NH),
                                  hmask_s[:].unsqueeze(2).broadcast_to([P, NH, DH]), ALU.mult)
                dve.tensor_scalar_add(kse[:, b:b + 1], kv[:, D:D + 1], KSUM_EPS).then_inc(v_free, 1)
                dve.wait_ge(v_free, n + 1)
                dve.tensor_scalar_mul(KVB[:, b, D:D + NH], hmask[:], kse[:, b:b + 1]).then_inc(kvb_ready, 1)
            for b in range(B):
                for h in range(2):
                    n = LV["oD", b, h]
                    dve.wait_ge(v_full, n + 1)
                    o = bank_v(n)[:, 0:2 * (D + NH)].rearrange("p (t n) -> p t n", t=2)
                    rec = eq[:, :, :, :].rearrange("p a t e -> p (a t e)")[:, 0:2 * NH].rearrange("p (t h) -> p t h", t=2)
                    link(dve.reciprocal(rec, o[:, :, D:D + NH]))
                    for t in range(2):
                        ins = dve.tensor_tensor(Y[:, b, 2 * h + t, :].rearrange("p (h d) -> p h d", h=NH),
                                                o[:, t, 0:D].rearrange("p (h d) -> p h d", h=NH),
                                                rec[:, t, :].unsqueeze(2).broadcast_to([P, NH, DH]), ALU.mult)
                    ins.then_inc(v_free, 1)
                    dve.wait_ge(v_free, n + 1)
                link(dve.tensor_tensor(Y[:, b], Y[:, b], xtile("C", b), ALU.add))
                norm(("D", b), Y[:, b], xtile("D", b))
            for b in range(B):
                dve.wait_ge(x_ready, LN["D", b] + 1)
                if b == 0:
                    dve.wait_ge(v_full, LV["oD", B - 1, 1] + 1)
                norm(("lat", b), xtile("D", b), LAT[:, b])

            def lo(key, h):
                kind, p = key
                r, hp = p % 3, p % NHP
                n = PJ[key]
                dve.wait_ge(hi_ready, 12 * p + {"Q": 0, "K": 4, "Kt": 8}[kind] + 2 * h + 2)
                rows, other = slice(DW * h, DW * h + DW), slice(DW * (1 - h), DW * (1 - h) + DW)
                if kind == "Q":
                    lead, dst, width, bias = QA[r][h][rows, :], QA[r][h][other, :], S, b1s[rows, 0, hp:hp + 1]
                elif kind == "K":
                    lead, dst, width, bias = KA[r][h][rows, 0:S], KBt[r][h][rows, 0:S], S, b1s[rows, 1, hp:hp + 1]
                else:
                    width = KEYS_PAD - S
                    lead, dst, bias = KA[r][h][rows, S:KEYS_PAD], KBt[r][h][rows, S:KEYS_PAD], b1s[rows, 1, hp:hp + 1]
                ins = dve.scalar_tensor_tensor(dst, PS[rows, 6 + n % 2, 0:width], bias, lead.bitcast(F32), ALU.add, ALU.subtract)
                ins.then_inc(lo_ready if h == 0 else pj_free, 1)

            def value(key):
                _, b, u = key
                n = PJ[key]
                j, half = divmod(u, 2)
                rows = min(P, KEYS - P * j)
                dve.wait_ge(pj_full, n + 1)
                dve.tensor_copy(VXA[0:rows, b % 2, j, 8 * half:8 * half + 8, 0:DW],
                                PS[0:rows, 6 + n % 2, :].rearrange("p (h d) -> p h d", h=8)).then_inc(pj_free, 1)

            def c_rows(key):
                p = key[1]
                n = PJ[key]
                dve.wait_ge(pj_full, n + 1)
                if p >= 2:
                    dve.wait_ge(c_in[(p - 2) % 3], 32 * ((p - 2) // 3 + 1))
                dve.tensor_scalar_mul(crow[:, p % 2, :], PS[0:2 * NT, 6 + n % 2, 0:P], -1.0).then_inc(pj_free, 1)

            def task(key):
                kind = key[0]
                n = PJ[key]
                if kind == "V":
                    value(key)
                elif kind == "c":
                    c_rows(key)
                elif kind == "oT":
                    dve.wait_ge(pj_full, n + 1)
                    dve.tensor_copy(OT[:, key[1] % NHP, :], PS[:, 6 + n % 2, :]).then_inc(pj_free, 1)
                else:
                    b = key[1]
                    dve.wait_ge(pj_full, n + 1)
                    dve.wait_ge(xr_ready, B + b + 1)
                    dve.tensor_tensor(Y[:, b], PS[:, 6 + n % 2, :].rearrange("p (t d) -> p t d", t=NT), xtile("D", b), ALU.add).then_inc(pj_free, 1)
                    dve.wait_ge(pj_free, n + 1)
                    norm(("E", b), Y[:, b], xtile("E", b))

            def maxima(p, u):
                h, m = divmod(u, 5)
                g = 10 * p + u
                dve.wait_ge(mu_full, g + 1)
                if m < NT:
                    dve.tensor_reduce(mxm[:, p % 2, h, m:m + 1], PS[:, 2 + g % 2, :], AX.X, ALU.max).then_inc(mu_free, 1)
                else:
                    dve.tensor_reduce(mxt[:, p % 2, h, :], PS[:, 2 + g % 2, 0:NT * (KEYS_PAD - S)].rearrange("p (t k) -> p t k", t=NT),
                                      AX.X, ALU.max).then_inc(mu_free, 1)
                    dve.wait_ge(mu_free, g + 1)
                    dve.tensor_tensor(cmx[:, p % 2, h, :], mxm[:, p % 2, h, :], mxt[:, p % 2, h, :], ALU.max).then_inc(cm_ready, 1)

            def head_out(head):
                p, h = divmod(head, 2)
                b = p // NHP
                o = PS[:, 4 + head % 2, 0:NT * (DW + 1)].rearrange("p (t d) -> p t d", t=NT)
                dve.wait_ge(pv_ready, KB * (head + 1))
                link(dve.reciprocal(rden[:, head % 2, :], o[:, :, DW]))
                if p >= 2:
                    dve.wait_ge(pj_full, PJ["oT", p - 2] + 1)
                dve.tensor_tensor(CT[:, p % 2, :, DW * h:DW * h + DW], o[:, :, 0:DW],
                                  rden[:, head % 2, :].unsqueeze(2).broadcast_to([P, NT, DW]), ALU.mult).then_inc(on_ready, 1)

            for key in PROLOGUE[:2 * KB]:
                dve.wait_ge(bvb_ready, N_POOL)
                task(key)
            for key in PROLOGUE[2 * KB:-1]:
                for h in range(2):
                    lo(key, h)
            for u in range(10):
                maxima(0, u)
            task(("c", 0))
            for p in range(STEPS):
                tasks = step_tasks(p)
                for slot in range(SLOTS):
                    if p + 1 < PAIRS:
                        for u in MAX_UNITS.get(slot, []):
                            maxima(p + 1, u)
                    if slot == 0 and p:
                        head_out(2 * p - 1)
                    if slot == KB:
                        head_out(2 * p)
                    for key, h in splits(tasks, slot - 1):
                        lo(key, h)
                    for key in tasks.get(slot, []):
                        if key[0] not in ("Q", "K", "Kt"):
                            task(key)
            head_out(2 * PAIRS - 1)
            for key in EPILOGUE:
                task(key)
            dve.wait_ge(cn_in, N_CN)
            dve.tensor_scalar_mul(cbias[:, 0:1], cnb[:, 3:4], 0.5)
            dve.tensor_scalar_mul(cA[:], ar1[:], 0.3)
            dve.tensor_scalar_mul(cbias[:, 1:2], gnb[:, 2:3], 0.5).then_inc(coef_ready, 1)
            for b in range(B):
                dve.wait_ge(a_free, LA["xT", "F", b] + 1)
                dve.tensor_reduce(gsum[:, b:b + 1], FS[:, b, :], AX.X, ALU.add).then_inc(gs_ready, 1)
            dve.wait_ge(a_free, LA["gn", 2] + 1)
            link(dve.tensor_scalar(cB[:], gth[:], ar1[:], 0.7, ALU.mult, ALU.mult))
            link(dve.tensor_scalar_add(cB[:], cB[:], 0.1))
            for c in range(CYCLES):
                for b in range(B):
                    dve.wait_ge(a_free, LA["cn", c, 3, b] + 1)
                    link(dve.tensor_scalar(CP[:, b, :], TH[:, b, :], cA[:], cB[:, b:b + 1], ALU.mult, ALU.add))
                    n = LV["twist", c, b]
                    dve.wait_ge(v_full, n + 1)
                    dve.tensor_tensor(CP[:, b, :], CP[:, b, :], bank_v(n), ALU.mult).then_inc(v_free, 1)
                    dve.wait_ge(v_free, n + 1)
                    dve.tensor_tensor(FS[:, b, :], FS[:, b, :], CP[:, b, :], ALU.add).then_inc(state_ready, 1)
            for b in range(B):
                n = LV["back", b]
                dve.wait_ge(v_full, n + 1)
                dve.tensor_tensor(Y[:, b], bank_v(n).rearrange("p (t d) -> p t d", t=NT), xtile("E", b), ALU.add).then_inc(v_free, 1)
                dve.wait_ge(v_free, n + 1)
                norm(("F", b), Y[:, b], xtile("0", b))

        @block.tensor
        def _(pe):
            def lane_a(key, emit):
                n = LA[key]
                if n >= 2:
                    pe.wait_ge(a_free, n - 1)
                emit(bank_a(n)).then_inc(a_full, 1)

            def lane_v(key, emit):
                n = LV[key]
                if n >= 2:
                    pe.wait_ge(v_free, n - 1)
                emit(bank_v(n)).then_inc(v_full, 1)

            def mm(dst, lhsT, rhs, start=True, stop=True, **kw):
                return pe.matmul(dst, lhsT, rhs, start=start, stop=stop, **kw)

            def transposes(srcs, rows=P):
                def emit(bank):
                    for n, src in enumerate(srcs):
                        ins = pe.transpose(bank[0:src.shape[1], rows * n:rows * n + rows], src, ident[0:rows, 0:rows])
                    return ins
                return emit

            def tiles_of(x3):
                return [x3[:, t, :] for t in range(NT)]

            pe.wait_ge(consts, N_CONST)
            for b in range(B):
                pe.wait_ge(x_in[b], 16)
                lane_a(("xT", "A", b), transposes(tiles_of(xtile("0", b))))

            def dots(b):
                pe.wait_ge(diag_ready, b + 1)
                lane_a(("rb", b), lambda bank: mm(bank, ones[:], DG[:, b, :]))
                pe.wait_ge(a_free, LA["xT", "A", b] + 1)
                for j in range(NT):
                    if b:
                        pe.wait_ge(sim_ready, NT * (b - 1) + j + 1)
                    mm(PS[:, j, :], XT[:, b, P * j:P * j + P], XT[:, b, :]).then_inc(dots_ready, 1)

            def out_a(b):
                pe.wait_ge(exp_ready, NT * (b + 1))

                def emit(bank):
                    for i in range(NT):
                        for j in range(NT):
                            ins = mm(bank[:, P * i:P * i + P], EX[:, b % 2, j, P * i:P * i + P], XS["0"][:, NT * b + j, :],
                                     start=j == 0, stop=j == NT - 1)
                    return ins
                lane_v(("oA", b), emit)

            dots(0)
            for b in range(B):
                if b + 1 < B:
                    dots(b + 1)
                out_a(b)
            pe.wait_ge(ctx_in, 16)
            lane_a(("ctxT",), transposes([ctx_sb[:, b, :] for b in range(B)], rows=CK))
            pe.wait_ge(a_free, LA["ctxT",] + 1)
            pe.wait_ge(w0_in, N_W0)
            lane_v(("k0",), lambda bank: mm(bank[:, 0:B * CK], wk0s[:], ctxT[:].rearrange("p b k -> p (b k)")))

            def v0(bank):
                for b in range(B):
                    ins = mm(bank[0:CK, D * b:D * b + D], ctxT[:, b, :], wv0s[:])
                return ins
            lane_v(("v0",), v0)
            pe.wait_ge(bvb_ready, 1)
            lane_v(("cb0",), lambda bank: mm(bank[:, 0:D], bv0b[:], wo0s[:]))
            pe.wait_ge(perc_in, N_PERC)
            pe.wait_ge(kbd_ready, 1)

            def cb1(bank):
                for c in range(NHP):
                    ins = mm(bank[:, 0:D], bv1b[:, c, :], wout1s[:, c, :], start=c == 0, stop=c == NHP - 1)
                return ins
            lane_v(("cb1",), cb1)
            pe.wait_ge(x_ready, LN["media", 0] + 1)
            lane_a(("mediaT",), transposes([ctxn[:, b, :] for b in range(B)], rows=CK))
            for b in range(B):
                pe.wait_ge(x_ready, LN["A", b] + 1)
                lane_a(("xT", "B", b), transposes(tiles_of(xtile("A", b))))
                pe.wait_ge(a_free, LA["xT", "B", b] + 1)
                lane_a(("qT0", b), lambda bank: mm(bank, wq0s[:], XT[:, b, :]))

            def scores0(tt):
                b, t = divmod(tt, NT)
                pe.wait_ge(a_free, LA["qT0", b] + 1)
                pe.wait_ge(kbd_ready, b + 2)
                if tt:
                    pe.wait_ge(s0_sub, tt)
                for n, (h0, hn) in enumerate(((0, 6), (6, 6), (12, 4))):
                    ins = mm(PS[:, n, 0:hn * CK], QT0[:, b, P * t:P * t + P], KBD[:, b, h0:h0 + hn, :].rearrange("p h k -> p (h k)"))
                ins.then_inc(s0_ready, 1)

            def turn0(tt):
                pe.wait_ge(p0_ready, tt + 1)
                sm = SM[:, tt % 2, :].rearrange("p (h k) -> p h k", k=CK)
                for g in range(4):
                    lane = lane_a if g % 2 == 0 else lane_v
                    lane(("pT", tt, g), transposes([sm[:, 4 * g + i, :] for i in range(4)]))

            def weigh0(tt):
                b = tt // NT
                pe.wait_ge(a_free, LA["pT", tt, 2] + 1)
                pe.wait_ge(v_free, LV["pT", tt, 3] + 1)
                if tt:
                    pe.wait_ge(pv0_free, tt)
                for h in range(NH):
                    ins = mm(PS[:, 3, (DH + 1) * h:(DH + 1) * (h + 1)], PT0[:, tt % 2, h, :], v0x[:, b, h, :])
                ins.then_inc(pv0_full, 1)

            def c_t(b):
                pe.wait_ge(pv0_free, NT * b + NT)
                lane_a(("cT", b), transposes([C0[:, b, t, :] for t in range(NT)]))

            def y_b(b):
                pe.wait_ge(a_free, LA["cT", b] + 1)

                def emit(bank):
                    for t in range(NT):
                        ins = mm(bank[:, P * t:P * t + P], C0T[:, b, P * t:P * t + P], wo0s[:])
                    return ins
                lane_v(("yB", b), emit)

            scores0(0)
            for tt in range(TILES):
                if tt + 1 < TILES:
                    scores0(tt + 1)
                turn0(tt)
                if tt:
                    weigh0(tt - 1)
                if tt % NT == 1 and tt > NT:
                    c_t(tt // NT - 1)
                if tt % NT == 2 and tt > NT:
                    y_b(tt // NT - 1)
            weigh0(TILES - 1)
            c_t(B - 1)
            pe.wait_ge(moe_in, N_MOE)
            pe.wait_ge(qkv_in, N_QKV)
            y_b(B - 1)
            for b in range(B):
                pe.wait_ge(x_ready, LN["B", b] + 1)
                lane_a(("xT", "C", b), transposes(tiles_of(xtile("B", b))))
                pe.wait_ge(a_free, LA["xT", "C", b] + 1)

                def router(bank):
                    for t in range(NT):
                        ins = mm(bank[:, E * t:E * t + E], XT[:, b, P * t:P * t + P], wrT[:])
                    return ins
                lane_v(("router", b), router)
            pe.wait_ge(s0_sub, TILES)

            def up(e_all):
                b, e = divmod(e_all, EXPERTS)
                for k in range(HB):
                    n = HB * e_all + k
                    if n >= 2:
                        pe.wait_ge(silu_ready, n - 1)
                    mm(PS[:, n % 2, :], wgT[:, HB * e + k, :], XT[:, b, :]).then_inc(g_ready, 1)
                    if n >= 2:
                        pe.wait_ge(h_ready, n - 1)
                    mm(PS[:, 2 + n % 2, :], wuT[:, HB * e + k, :], XT[:, b, :]).then_inc(u_ready, 1)

            def down(e_all):
                b, e = divmod(e_all, EXPERTS)
                pe.wait_ge(h_ready, HB * (e_all + 1))

                def emit(bank):
                    for t in range(NT):
                        for k in range(HB):
                            ins = mm(bank[:, P * t:P * t + P], HX[:, e_all % 3, k, P * t:P * t + P], wdT[:, HB * e + k, :],
                                     start=k == 0, stop=k == HB - 1)
                    return ins
                lane_v(("down", b, e), emit)

            up(0)
            for e_all in range(B * EXPERTS):
                if e_all + 1 < B * EXPERTS:
                    up(e_all + 1)
                down(e_all)
            pe.wait_ge(silu_ready, B * EXPERTS * HB)
            for b in range(B):
                pe.wait_ge(x_ready, LN["C", b] + 1)
                lane_a(("xT", "D", b), transposes(tiles_of(xtile("C", b))))
            for b in range(B):
                pe.wait_ge(a_free, LA["xT", "D", b] + 1)
                if b:
                    pe.wait_ge(vx_ready, b)
                for t in range(NT):
                    mm(PS[:, t, 0:3 * D], XT[:, b, P * t:P * t + P], wqkvT[:].rearrange("p k n -> p (k n)")).then_inc(qkv_ready, 1)
            for b in range(B):
                pe.wait_ge(act_seq, 3 * b + 3)
                lane_a(("qT", b), transposes([QK[:, b, t, 0:D] for t in range(NT)]))

                def kv(bank):
                    for t in range(NT):
                        ins = mm(bank[:, 0:D + 1], QK[:, b, t, D:2 * D], VXv[:, b, t, :], start=t == 0, stop=t == NT - 1)
                    return ins
                lane_v(("kv", b), kv)
            for b in range(B):
                pe.wait_ge(a_free, LA["qT", b] + 1)
                pe.wait_ge(kvb_ready, b + 1)
                for h in range(2):
                    def emit(bank):
                        for t in range(2):
                            tt = 2 * h + t
                            ins = mm(bank[:, (D + NH) * t:(D + NH) * (t + 1)], QTD[:, b, P * tt:P * tt + P], KVB[:, b, :])
                        return ins
                    lane_v(("oD", b, h), emit)
            for b in range(B):
                pe.wait_ge(x_ready, LN["lat", b] + 1)
                lane_a(("latT", b), transposes(tiles_of(LAT[:, b])))
            pe.wait_ge(v_free, LV["oD", B - 1, 1] + 1)
            pe.wait_ge(vx_ready, B)
            pe.wait_ge(act_seq, 3 * B + 1)
            pe.wait_ge(bvb_ready, N_POOL)
            pe.wait_ge(a_free, LA["latT", B - 1] + 1)
            pe.wait_ge(wkv_in, 16)

            def s_wide(p, slot):
                g = SLOTS * p + slot
                h, j = divmod(slot, KB)
                r, rows = p % 3, min(P, KEYS - P * j)
                if slot == 0:
                    pe.wait_ge(c_in[r], 32 * (p // 3 + 1))
                if g >= 2:
                    pe.wait_ge(pw_ready, g - 1)
                dst = PS[0:rows, g % 2, :]
                mm(dst, KA[r][h][:, P * j:P * j + rows], QA[r][h][:], stop=False)
                mm(dst, KBt[r][h][:, P * j:P * j + rows], QB[r][h][:], start=False).then_inc(sw_ready, 1)

            def pv(g):
                p, slot = divmod(g, SLOTS)
                h, j = divmod(slot, KB)
                b, hp = divmod(p, NHP)
                head = 2 * p + h
                rows = min(P, KEYS - P * j)
                pe.wait_ge(pw_ready, g + 1)
                if j == 0 and head >= 2:
                    pe.wait_ge(on_ready, head - 1)
                if j == 0 and hp == 0 and h == 0:
                    pe.wait_ge(pj_free, PJ["V", b, 2 * KB - 1] + 1)
                for t in range(NT):
                    ins = mm(PS[:, 4 + head % 2, (DW + 1) * t:(DW + 1) * (t + 1)], PX[0:rows, g % 4, P * t:P * t + P],
                             VXA[0:rows, b % 2, j, 2 * hp + h, :], start=j == 0 and t == 0, stop=j == KB - 1, skip_group_check=True)
                ins.then_inc(pv_ready, 1)

            def max_unit(p, u):
                h, m = divmod(u, 5)
                g, r = 10 * p + u, p % 3
                if u == 0:
                    pe.wait_ge(hi_ready, 12 * (p + 1))
                    pe.wait_ge(pj_free, PJ["Kt", p] + 1)
                if g >= 2:
                    pe.wait_ge(mu_free, g - 1)
                if m < NT:
                    mm(PS[:, 2 + g % 2, :], QA[r][h][:, P * m:P * m + P], KA[r][h][:, 0:S]).then_inc(mu_full, 1)
                else:
                    w = KEYS_PAD - S
                    for t in range(NT):
                        ins = mm(PS[:, 2 + g % 2, w * t:w * t + w], QA[r][h][:, P * t:P * t + P], KA[r][h][:, S:KEYS_PAD])
                    ins.then_inc(mu_full, 1)

            def task(key):
                n = PJ[key]
                if n >= 2:
                    pe.wait_ge(pj_free, n - 1)
                bank = PS[:, 6 + n % 2, :]
                kind = key[0]
                if kind == "Q":
                    b, hp = divmod(key[1], NHP)
                    ins = mm(bank, wq1s[:, P * hp:P * hp + P], LATT[:, b, :])
                elif kind == "K":
                    b, hp = divmod(key[1], NHP)
                    ins = mm(bank, wkv1s[:, P * hp:P * hp + P], LATT[:, b, :])
                elif kind == "Kt":
                    b, hp = divmod(key[1], NHP)
                    ins = mm(bank[:, 0:KEYS_PAD - S], wkv1s[:, P * hp:P * hp + P], MEDT[:, b, :])
                elif kind == "V":
                    _, b, u = key
                    j, half = divmod(u, 2)
                    rows = min(P, KEYS - P * j)
                    keys = LATT[:, b, P * j:P * j + P] if j < NT else MEDT[:, b, 0:CK]
                    ins = mm(bank[0:rows, :], keys, wkv1s[:, INNER + 512 * half:INNER + 512 * half + 512])
                elif kind == "c":
                    p = key[1]
                    pe.wait_ge(cm_ready, 2 * (p + 1))
                    ins = pe.transpose(bank[0:2 * NT, 0:P], cmx[:, p % 2].rearrange("p h t -> p (h t)"), ident[:])
                elif kind == "oT":
                    p = key[1]
                    pe.wait_ge(on_ready, 2 * (p + 1))
                    for t in range(NT):
                        ins = pe.transpose(bank[:, P * t:P * t + P], CT[:, p % 2, t, :], ident[:])
                else:
                    b = key[1]
                    pe.wait_ge(pj_free, PJ["oT", NHP * b + NHP - 1] + 1)
                    for t in range(NT):
                        for c in range(NHP):
                            ins = mm(bank[:, P * t:P * t + P], OT[:, c, P * t:P * t + P], wout1s[:, c, :], start=c == 0, stop=c == NHP - 1)
                ins.then_inc(pj_full, 1)

            for key in PROLOGUE[:-1]:
                task(key)
            for u in range(10):
                max_unit(0, u)
            task(("c", 0))
            for p in range(STEPS):
                tasks = step_tasks(p)
                for slot in range(SLOTS):
                    s_wide(p, slot)
                    if p + 1 < PAIRS:
                        for u in MAX_UNITS.get(slot, []):
                            max_unit(p + 1, u)
                    if SLOTS * p + slot:
                        pv(SLOTS * p + slot - 1)
                    for key in tasks.get(slot, []):
                        task(key)
            pv(SLOTS * STEPS - 1)
            for key in EPILOGUE:
                task(key)
            pe.wait_ge(cn_in, N_CN)
            pe.wait_ge(pj_free, len(PJ))
            pe.wait_ge(bvb_ready, N_POOL)
            for b in range(B):
                pe.wait_ge(x_ready, LN["E", b] + 1)
                lane_a(("xT", "F", b), transposes(tiles_of(xtile("E", b))))
            pe.wait_ge(gs_ready, B)
            lane_a(("gn", 0), lambda bank: mm(bank[0:64, 0:B], gn1[:], gsum[:]))
            pe.wait_ge(a_free, LA["gn", 0] + 1)
            lane_a(("gn", 1), lambda bank: mm(bank[0:32, 0:B], gn2[:], gact1[:]))
            pe.wait_ge(a_free, LA["gn", 1] + 1)
            lane_a(("gn", 2), lambda bank: mm(bank[:, 0:B], gn3[:], gact2[:]))
            for c in range(CYCLES):
                for layer, (w, src, rows) in enumerate(((cn1, FS, P), (cn2, H1, 64), (cn3, H2, 32), (cn4, H3, P))):
                    for b in range(B):
                        if layer == 0 and c:
                            pe.wait_ge(state_ready, B * (c - 1) + b + 1)
                        if layer:
                            pe.wait_ge(a_free, LA["cn", c, layer - 1, b] + 1)
                        lane_a(("cn", c, layer, b), lambda bank: mm(bank[0:rows, :], w[:], src[:, b, :]))
                for b in range(B):
                    lane_v(("twist", c, b), lambda bank: mm(bank, twist[:], FS[:, b, :]))
            for b in range(B):
                pe.wait_ge(state_ready, B * (CYCLES - 1) + b + 1)
                lane_v(("back", b), transposes([FS[:, b, P * t:P * t + P] for t in range(NT)]))


_INS = ["x", "ctx_1024", "L0_xattn_Wq", "L0_xattn_bq", "L0_xattn_Wk", "L0_xattn_bk", "L0_xattn_Wv", "L0_xattn_bv",
        "L0_xattn_Wo", "L0_xattn_bo", "L0_ffn_w_router", "L0_ffn_Wg", "L0_ffn_Wu", "L0_ffn_Wd", "L0_ffn_sg",
        "L0_ffn_su", "L0_ffn_sd", "L1_attn_W_qkv", "L1_xattn_ln_media_w", "L1_xattn_ln_media_b", "L1_xattn_ln_lat_w",
        "L1_xattn_ln_lat_b", "L1_xattn_Wq", "L1_xattn_bq", "L1_xattn_Wkv", "L1_xattn_bkv", "L1_xattn_Wout",
        "L1_xattn_bout", "L1_ffn_cn_w1", "L1_ffn_cn_b1", "L1_ffn_cn_w2", "L1_ffn_cn_b2", "L1_ffn_cn_w3",
        "L1_ffn_cn_b3", "L1_ffn_cn_w4", "L1_ffn_cn_b4", "L1_ffn_gc_w1", "L1_ffn_gc_b1", "L1_ffn_gc_w2",
        "L1_ffn_gc_b2", "L1_ffn_gc_w3", "L1_ffn_gc_b3", "L1_ffn_adaptive_range"]


def kernel(**inputs):
    import numpy as np
    import concourse.bacc as bacc
    from concourse.bass_utils import run_bass_kernel_spmd

    nc = bacc.Bacc("TRN2", target_bir_lowering=False, num_devices=1)
    arrays, args = {}, []
    def blocks(w):
        return w.reshape(-1, P, w.shape[-1]).transpose(1, 0, 2)

    layout = {
        "L0_ffn_Wg": lambda w: w.transpose(2, 0, 1).reshape(D, -1), "L0_ffn_Wu": lambda w: w.transpose(2, 0, 1).reshape(D, -1),
        "L0_ffn_sg": lambda w: w.T, "L0_ffn_su": lambda w: w.T,
        "L0_ffn_Wd": lambda w: blocks(w.transpose(0, 2, 1).reshape(-1, D)).reshape(P, -1),
        "L0_ffn_sd": lambda w: blocks(w.T).reshape(P, -1),
        "L0_ffn_w_router": lambda w: w.T, "L1_attn_W_qkv": lambda w: w.T,
        "L1_xattn_bq": lambda w: w.reshape(-1, P).T, "L1_xattn_bkv": lambda w: w.reshape(-1, P).T,
        "L1_xattn_Wout": blocks,
    }
    for name in _INS:
        a = np.asarray(inputs[name])
        a = np.ascontiguousarray(layout[name](a) if name in layout else a)
        arrays[f"in_{name}"] = a
        args.append(nc.dram_tensor(f"in_{name}", a.shape, mybir.dt.from_np(a.dtype), kind="ExternalInput").ap())
    args.append(nc.dram_tensor("out", (B, S, D), F32, kind="ExternalOutput").ap())
    decoder(nc, *args)
    r = run_bass_kernel_spmd(nc, [arrays], core_ids=[0])
    return r.results[0]["out"]
```

```python
from contextlib import ExitStack

import concourse.bass as bass
from concourse import mybir

F32 = mybir.dt.float32
F32R = mybir.dt.float32r
U32 = mybir.dt.uint32
ACT = mybir.ActivationFunctionType
ALU = mybir.AluOpType
AX = mybir.AxisListType

P = 128
B, S, D = 4, 512, 128
NT = S // P
TILES = B * NT
CK = 77
NH = 16
DH = D // NH
DW = 64
INNER = NH * DW
NHP = NH // 2
PAIRS = B * NHP
KEYS = S + CK
KEYS_PAD = KEYS + 1
KB = (KEYS + P - 1) // P
E, HID = 8, 256
EXPERTS = E + 1
HB = HID // P
CYCLES = 3
LN_EPS = 1e-5
COS_EPS = 1e-8
L2_EPS = 1e-12
KSUM_EPS = 1e-6
LN_SCALE = 65536.0
SCALE_N = DH ** -0.5
SCALE_W = DW ** -0.5

D_NORMS = [("D", 0), ("D", 1), ("lat", 0), ("D", 2), ("lat", 1), ("D", 3), ("lat", 2), ("lat", 3)]
LN_KEYS = ([("A", b) for b in range(B)] + [("media", 0)] + [("B", b) for b in range(B)]
           + [("C", b) for b in range(B)] + D_NORMS
           + [("E", b) for b in range(B)] + [("F", b) for b in range(B)])
LN = {key: n for n, key in enumerate(LN_KEYS)}


def between0(tt):
    b, t = divmod(tt, NT)
    work = []
    if t == 1 and b:
        work += [("cT", b - 1)]
    if t == 1 and b + 1 < B:
        work += [("x", b + 1)]
    if t == 2 and b + 1 < B:
        work += [("q", b + 1)]
    if t == 2 and b:
        work += [("y", b - 1)]
    if tt == 3:
        work += [("media", 0)]
    if t == 0 and b >= 2:
        work += [("xC", b - 2)]
    if t == 1 and b >= 2:
        work += [("route", b - 2)]
    return work


LAST_ROUTER = 3
BIAS_ROW = 5


def lane_a_tasks():
    t = [("xT", "A", b) for b in range(B)] + [("rb", b) for b in range(B)]
    t += [("ctxT",), ("xT", "B", 0), ("qT0", 0)]
    for tt in range(TILES):
        t += [("pT", tt, 0), ("pT", tt, 2)]
        for kind, b in between0(tt):
            t += {"cT": [("cT", b)], "x": [("xT", "B", b)], "q": [("qT0", b)], "media": [("mediaT",)], "xC": [("xT", "C", b)]}.get(kind, [])
    t += [("xT", "C", B - 2), ("cT", B - 1), ("xT", "C", B - 1)]
    t += [("xT", "D", b) for b in range(B)] + [("qT", b) for b in range(B)]
    t += [("latT", b) for b in range(B)]
    t += [("xT", "F", b) for b in range(B)]
    for c in range(CYCLES):
        for layer in range(4):
            t += [("cn", c, layer, b) for b in range(B)]
            if c == 0 and layer < 3:
                t += [("gn", layer)]
    return {key: n for n, key in enumerate(t)}


def lane_v_tasks():
    t = [("oA", 0), ("oA", 1), ("k0",), ("v0",), ("cb0",), ("oA", 2), ("oA", 3)]
    for tt in range(TILES):
        t += [("pT", tt, 1), ("pT", tt, 3)]
        for kind, b in between0(tt):
            t += {"y": [("yB", b)], "route": [("router", b)]}.get(kind, [])
    t += [("yB", B - 1), ("router", B - 2)]
    for e_all in range(B * EXPERTS):
        t += [("down", e_all // EXPERTS, e_all % EXPERTS)]
        if e_all == LAST_ROUTER:
            t += [("router", B - 1)]
        if e_all == BIAS_ROW:
            t += [("cb1",)]
    t += [("kv", b) for b in range(B)] + [("oD", b, h) for b in range(B) for h in range(2)]
    for c in range(CYCLES):
        for b in range(B):
            if c == CYCLES - 1 and b >= 2:
                t += [("back", b - 2)]
            t += [("twist", c, b)]
    t += [("back", b) for b in range(B - 2, B)]
    return {key: n for n, key in enumerate(t)}


LA, LV = lane_a_tasks(), lane_v_tasks()

SLOTS = 2 * KB
STEPS = PAIRS
MAX_UNITS = {0: [0], 1: [1, 2], 2: [3, 4], 3: [5], 4: [6, 7], 5: [8, 9]}


def step_tasks(p):
    t = {}
    if p + 2 < PAIRS:
        t[0], t[3], t[5] = [("Q", p + 2)], [("K", p + 2)], [("Kt", p + 2)]
    if p + 1 < PAIRS:
        t[6] = [("c", p + 1)]
    b, hp = divmod(p, NHP)
    if b + 1 < B and hp < KB:
        t[2] = [("V", b + 1, 2 * hp)]
        t[7] = [("V", b + 1, 2 * hp + 1)]
    if p:
        t[8] = [("oT", p - 1)]
    if b and hp == 0:
        t[9] = [("yE", b - 1)]
    return t


def splits(tasks, slot):
    now = [(key, 0) for key in tasks.get(slot, []) if key[0] in ("Q", "K", "Kt")]
    return ([(key, 1) for key in tasks.get(slot - 1, []) if key[0] in ("Q", "K")] + now
            + [(key, 1) for key, _ in now if key[0] == "Kt"])


PROLOGUE = ([("Q", 0), ("K", 0), ("Kt", 0), ("V", 0, 0), ("V", 0, 1), ("max", 0), ("max", 1), ("V", 0, 2), ("max", 2),
             ("max", 3), ("V", 0, 3), ("max", 4), ("max", 5), ("V", 0, 4), ("max", 6), ("max", 7), ("V", 0, 5), ("max", 8),
             ("max", 9), ("c", 0), ("Q", 1), ("V", 0, 6), ("K", 1), ("V", 0, 7), ("Kt", 1), ("V", 0, 8), ("V", 0, 9)])
EPILOGUE = [("oT", PAIRS - 1), ("yE", B - 1)]


def proj_tasks():
    t = [key for key in PROLOGUE if key[0] != "max"]
    for p in range(STEPS):
        for slot in range(SLOTS):
            t += step_tasks(p).get(slot, [])
    return {key: n for n, key in enumerate(t + EPILOGUE)}


PJ = proj_tasks()


def decoder(nc, x, ctx, wq0, bq0, wk0, bk0, wv0, bv0, wo0, bo0, w_router, w_g, w_u, w_d, s_g, s_u, s_d, w_qkv,
            med_w, med_b, lat_w, lat_b, wq1, bq1, wkv1, bkv1, wout1, bout1,
            cw1, cb1_, cw2, cb2_, cw3, cb3_, cw4, cb4_, gw1, gb1, gw2, gb2, gw3, gb3, arange, out):
    es = ExitStack()
    with es:
        def sb(name, shape, dt=F32):
            return es.enter_context(nc.sbuf_tensor(name, shape, dt))

        def sem(name):
            return es.enter_context(nc.semaphore(name))

        X_EVEN = sb("X_EVEN", [P, TILES, D])
        x_odd_at = nc.sbuf_base
        X_ODD = sb("X_ODD", [P, TILES, D])
        XS = {"0": X_EVEN, "A": X_ODD, "B": X_EVEN, "C": X_ODD, "D": X_EVEN, "E": X_ODD}
        xt_at = nc.sbuf_base
        XT = sb("XT", [P, B, S])
        Y = sb("Y", [P, B, NT, D])
        big_at = nc.sbuf_base
        BIG = sb("BIG", [P, 6656])
        reg_at = nc.sbuf_base
        REG = sb("REG", [P, 6400])
        wq1_at = nc.sbuf_base
        wq1s = sb("wq1s", [P, INNER])
        medt_at = nc.sbuf_base
        MEDT = sb("MEDT", [P, B, KEYS_PAD - S])
        st = sb("st", [P, 2, NT, 6])
        mv = sb("mv", [P, len(LN), NT, 2])
        ve = sb("ve", [P, len(LN), NT])
        rs = sb("rs", [P, len(LN), NT])
        ident = sb("ident", [P, P])
        ones = sb("ones", [P, P])
        half_neg = sb("half_neg", [P, NT])
        lnb = sb("lnb", [P, 1])
        hmask = sb("hmask", [P, NH])
        hmask_s = sb("hmask_s", [P, NH])
        iota = sb("iota", [P, E])
        twist = sb("twist", [P, P])
        ctx_sb = sb("ctx_sb", [CK, B, D])
        wq0s, wk0s, wv0s, wo0s = (sb(n, [P, P]) for n in ("wq0s", "wk0s", "wv0s", "wo0s"))
        b0s = sb("b0s", [P, 3])
        bo0s = sb("bo0s", [P, D])
        wqkvT = sb("wqkvT", [P, 3, P])
        wrT = sb("wrT", [P, E])
        lnw = sb("lnw", [P, 4])
        wout1s = sb("wout1s", [P, INNER // P, D])
        b1s = sb("b1s", [P, 3, INNER // P])
        bout1s = sb("bout1s", [P, D])
        CB0, CB1 = bo0s, bout1s
        bv0b = sb("bv0b", [P, P])
        cn1, cn2, cn3, cn4 = (sb(n, [P, P]) for n in ("cn1", "cn2", "cn3", "cn4"))
        gn1, gn2, gn3 = sb("gn1", [P, 64]), sb("gn2", [64, 32]), sb("gn3", [32, P])
        cnb, gnb = sb("cnb", [P, 4]), sb("gnb", [P, 3])
        w4col = sb("w4col", [32, 2])
        ar1 = sb("ar1", [P, 1])
        ss = sb("ss", [P, TILES])
        rn = sb("rn", [P, TILES])
        rsum = sb("rsum", [P, TILES])
        rinv = sb("rinv", [P, TILES])
        v0x = sb("v0x", [CK, B, NH, DH + 1])
        mx0 = sb("mx0", [P, 2, NH])
        r0 = sb("r0", [P, 2, NH])
        lg = sb("lg", [P, B, NT, E])
        top = sb("top", [P, B, NT, E])
        topi = sb("topi", [P, B, NT, E], U32)
        topf = sb("topf", [P, B, NT, 2])
        dl = sb("dl", [P, B, NT])
        th0 = sb("th0", [P, B, NT])
        wtop = sb("wtop", [P, B, 2, NT])
        eq = sb("eq", [P, 2, NT, E])
        comb = sb("comb", [P, B, NT, E])
        kse = sb("kse", [P, B])
        gsum = sb("gsum", [P, B])
        gact1, gact2 = sb("gact1", [64, B]), sb("gact2", [32, B])
        gth = sb("gth", [P, B])
        cA, cB = sb("cA", [P, 1]), sb("cB", [P, B])
        cbias = sb("cbias", [P, 2])
        QA = [[sb(f"QA{r}{h}", [P, S], F32R) for h in range(2)] for r in range(3)]
        KA = [[sb(f"KA{r}{h}", [P, KEYS_PAD], F32R) for h in range(2)] for r in range(3)]
        QB = [[sb(f"QB{r}{h}", [P, S], F32R) for h in range(2)] for r in range(3)]
        KBt = [[sb(f"KB{r}{h}", [P, KEYS_PAD], F32R) for h in range(2)] for r in range(3)]
        mxm = sb("mxm", [P, 2, 2, NT])
        mxt = sb("mxt", [P, 2, 2, NT])
        cmx = sb("cmx", [P, 2, 2, NT])
        crow = sb("crow", [2 * NT, 2, P])
        rden = sb("rden", [P, 2, NT])

        vxa_at = nc.sbuf_base
        VXA = sb("VXA", [P, 2, KB, NH, DW + 1])

        NW = HB * EXPERTS * D
        vflat = VXA[:].rearrange("p a j h d -> p (a j h d)")
        up_weights = vflat[:, 0:2 * NW].rearrange("p (a k d) -> p a k d", a=2, d=P)
        wgT, wuT, wdT = (vflat[:, NW * n:NW * n + NW].rearrange("p (k d) -> p k d", d=P) for n in range(3))

        def over(name, at, shape):
            return nc.alloc_sbuf_tensor_at(name, shape, F32R, offset=at)

        UPHI = over("UPHI", reg_at, [P, 2, EXPERTS * HB, P])
        UPLO = over("UPLO", vxa_at, [P, 2, EXPERTS * HB, P])
        XHI = over("XHI", reg_at + 4 * (6400 - 2 * S), [P, 2, S])
        XLO = over("XLO", xt_at, [P, B, S])
        WQHI, WQLO = over("WQHI", big_at + 4 * 5184, [P, INNER]), over("WQLO", wq1_at, [P, INNER])
        MEDHI, MEDLO = over("MEDHI", big_at + 4 * 6208, [P, B, KEYS_PAD - S]), over("MEDLO", medt_at, [P, B, KEYS_PAD - S])
        WKVHI, WKVLO = over("WKVHI", big_at + 4 * 3072, [P, 2 * INNER]), over("WKVLO", reg_at + 4 * (6400 - 2 * INNER), [P, 2 * INNER])
        LATHI, LATLO = over("LATHI", x_odd_at, [P, B, S]), over("LATLO", xt_at, [P, B, S])
        DG = Y[:].rearrange("p b t d -> p b (t d)")
        RBv = BIG[:, 0:2048].rearrange("p (b n) -> p b n", b=B)
        EX = BIG[:, 2048:6144].rearrange("p (r t n) -> p r t n", r=2, t=NT)
        GX = REG[:, 0:1024].rearrange("p (r n) -> p r n", r=2)
        SM = BIG[:, 0:2 * NH * CK].rearrange("p (r n) -> p r n", r=2)
        PT0 = BIG[0:CK, 2560:2560 + 2 * NH * P].rearrange("p (r h n) -> p r h n", r=2, h=NH)
        QT0 = vflat[:, 3 * NW:3 * NW + 2048].rearrange("p (b n) -> p b n", b=B)
        ctxT, k0T = (vflat[:, 3 * NW + n:3 * NW + n + B * CK].rearrange("p (b k) -> p b k", b=B) for n in (2048, 2048 + B * CK))
        ctxn = vflat[0:CK, 3 * NW + 2048 + 2 * B * CK:3 * NW + 2048 + 2 * B * CK + B * D].rearrange("p (b d) -> p b d", b=B)
        KBD = REG[:, 0:B * NH * CK].rearrange("p (b h k) -> p b h k", b=B, h=NH)
        bv1b = BIG[:, 5120:5120 + NHP * P].rearrange("p (c n) -> p c n", c=NHP)
        C0, C0T = Y, XT
        SG = BIG[:, 0:2048].rearrange("p (r n) -> p r n", r=4)
        HX = BIG[:, 2048:5120].rearrange("p (r k n) -> p r k n", r=3, k=HB)
        QK = BIG[:, 0:4096].rearrange("p (b t n) -> p b t n", b=B, t=NT)
        VXv = REG[:, 2048:2048 + B * NT * (D + 1)].rearrange("p (b t n) -> p b t n", b=B, t=NT)
        KVB = BIG[:, 4096:4096 + B * (D + NH)].rearrange("p (b n) -> p b n", b=B)
        SSQ = BIG[:, 4672:4672 + B * 128].rearrange("p (b n) -> p b n", b=B)
        SQ = REG[:, 0:1024].rearrange("p (r t n) -> p r t n", r=2, t=2)
        QTD = XT
        LAT, LATT = Y, XT
        PX = BIG[:, 0:2048].rearrange("p (r n) -> p r n", r=4)
        CT = BIG[:, 2048:2048 + 2 * NT * P].rearrange("p (r t n) -> p r t n", r=2, t=NT)
        OT = REG[:, 0:NHP * S].rearrange("p (c n) -> p c n", c=NHP)
        wkv1s = REG[:, 6400 - 2 * INNER:6400]
        FS = XT
        H1 = BIG[:, 0:2048].rearrange("p (b n) -> p b n", b=B)
        H2 = BIG[:, 2048:4096].rearrange("p (b n) -> p b n", b=B)
        H3 = BIG[:, 4096:6144].rearrange("p (b n) -> p b n", b=B)
        TH = REG[:, 0:2048].rearrange("p (b n) -> p b n", b=B)
        CP = REG[:, 2048:4096].rearrange("p (b n) -> p b n", b=B)

        PS = es.enter_context(nc.psum_tensor("PS", [P, 8, 512], F32))

        def bank_a(n):
            return PS[:, 4 + n % 2, :]

        def bank_v(n):
            return PS[:, 6 + n % 2, :]

        x_in = [sem(f"x_in{b}") for b in range(B)]
        ctx_in, w0_in, moe_in, qkv_in, perc_in, cn_in, wkv_in = (sem(n) for n in ("ctx_in", "w0_in", "moe_in", "qkv_in", "perc_in", "cn_in", "wkv_in"))
        consts = sem("consts")
        a_full, a_free, v_full, v_free = (sem(n) for n in ("a_full", "a_free", "v_full", "v_free"))
        var_ready, rstd_ready, x_ready = sem("var_ready"), sem("rstd_ready"), sem("x_ready")
        dve_seq, act_seq = sem("dve_seq"), sem("act_seq")
        sq_ready, ss_ready, rn_ready, diag_ready = (sem(n) for n in ("sq_ready", "ss_ready", "rn_ready", "diag_ready"))
        dots_ready, sim_ready, exp_ready = sem("dots_ready"), sem("sim_ready"), sem("exp_ready")
        xr_ready = sem("xr_ready")
        wide_hi, wide_lo, lathi_ready, latlo_ready, med_ready = (sem(n) for n in ("wide_hi", "wide_lo", "lathi_ready", "latlo_ready", "med_ready"))
        uphi_ready, uplo_ready, xhi_ready, xlo_ready = (sem(n) for n in ("uphi_ready", "uplo_ready", "xhi_ready", "xlo_ready"))
        kbd_ready, kbd_more, bv1_ready, bvb_ready = (sem(n) for n in ("kbd_ready", "kbd_more", "bv1_ready", "bvb_ready"))
        s0_ready, s0_sub, p0_ready, pv0_full, pv0_free = (sem(n) for n in ("s0_ready", "s0_sub", "p0_ready", "pv0_full", "pv0_free"))
        dl_ready, th_ready = sem("dl_ready"), sem("th_ready")
        g_ready, u_ready, silu_ready, h_ready = (sem(n) for n in ("g_ready", "u_ready", "silu_ready", "h_ready"))
        qkv_ready, qk_copied, vx_ready, sqq_ready, ssq_ready, lnorm_ready, qkn_ready, kvb_ready = (
            sem(n) for n in ("qkv_ready", "qk_copied", "vx_ready", "sqq_ready", "ssq_ready", "lnorm_ready", "qkn_ready", "kvb_ready"))
        pj_full, pj_free, hi_ready, lo_ready = (sem(n) for n in ("pj_full", "pj_free", "hi_ready", "lo_ready"))
        mu_full, mu_free, cm_ready = (sem(n) for n in ("mu_full", "mu_free", "cm_ready"))
        c_in = [sem(f"c_in{r}") for r in range(3)]
        sw_ready, pw_ready, pv_ready, on_ready = (sem(n) for n in ("sw_ready", "pw_ready", "pv_ready", "on_ready"))
        gs_ready, coef_ready, state_ready, out_sem = (sem(n) for n in ("gs_ready", "coef_ready", "state_ready", "out_sem"))

        block = es.enter_context(nc.Block())

        N_W0, N_MOE, N_QKV, N_PERC, N_CN = 16 * 8, 16 * 6, 16 * 2, 16 * 10, 16 * 15
        WIDE = ([(wq1s[:, 512 * n:512 * n + 512], WQHI[:, 512 * n:512 * n + 512], WQLO[:, 512 * n:512 * n + 512]) for n in range(2)]
                + [(MEDT[:], MEDHI[:], MEDLO[:])]
                + [(wkv1s[:, 512 * n:512 * n + 512], WKVHI[:, 512 * n:512 * n + 512], WKVLO[:, 512 * n:512 * n + 512]) for n in range(4)])
        N_CONST = 19
        N_POOL = 22
        N_E_OPERANDS = 20

        def xtile(k, b):
            return XS[k][:, NT * b:NT * b + NT, :]

        @block.sync
        def _(sp):
            for b in range(B):
                sp.dma_start(XS["0"][:, NT * b:NT * b + NT, :], x[b].rearrange("(t p) d -> p t d", p=P)).then_inc(x_in[b], 16)
            sp.dma_start(ctx_sb[:], ctx.rearrange("b k d -> k b d")).then_inc(ctx_in, 16)
            for dst, src in ((wq0s, wq0), (wk0s, wk0), (wv0s, wv0), (wo0s, wo0)):
                sp.dma_start(dst[:], src).then_inc(w0_in, 16)
            for n, src in enumerate((bq0, bk0, bv0)):
                sp.dma_start(b0s[:, n:n + 1], src.rearrange("(p a) -> p a", a=1)).then_inc(w0_in, 16)
            sp.dma_start(bo0s[:], bo0.partition_broadcast(P)).then_inc(w0_in, 16)
            ne = HB * E * P
            for dst, src, shared in ((wgT, w_g, s_g), (wuT, w_u, s_u), (wdT, w_d, s_d)):
                flat = dst.rearrange("p k d -> p (k d)")
                sp.dma_start(flat[:, 0:ne], src).then_inc(moe_in, 16)
                sp.dma_start(flat[:, ne:], shared).then_inc(moe_in, 16)
            sp.dma_start(wqkvT[:].rearrange("p k d -> p (k d)"), w_qkv).then_inc(qkv_in, 16)
            sp.dma_start(wrT[:], w_router).then_inc(qkv_in, 16)
            for n, src in enumerate((med_w, med_b, lat_w, lat_b)):
                sp.dma_start(lnw[:, n:n + 1], src.rearrange("(p a) -> p a", a=1)).then_inc(perc_in, 16)
            sp.dma_start(wq1s[:], wq1).then_inc(perc_in, 16)
            sp.dma_start(wout1s[:], wout1).then_inc(perc_in, 16)
            sp.dma_start(b1s[:, 0, :], bq1).then_inc(perc_in, 16)
            sp.dma_start(b1s[:, 1, :], bkv1[:, 0:NHP]).then_inc(perc_in, 16)
            sp.dma_start(b1s[:, 2, :], bkv1[:, NHP:2 * NHP]).then_inc(perc_in, 16)
            sp.dma_start(bout1s[:], bout1.partition_broadcast(P)).then_inc(perc_in, 16)
            sp.wait_ge(consts, N_CONST)
            for dst, src in ((cn1, cw1), (cn2, cw2), (cn3, cw3), (gn1, gw1), (gn2, gw2)):
                sp.dma_start(dst[0:src.shape[0], 0:src.shape[1]], src).then_inc(cn_in, 16)
            sp.dma_start(w4col[:, 0:1], cw4).then_inc(cn_in, 16)
            sp.dma_start(w4col[:, 1:2], gw3).then_inc(cn_in, 16)
            for n, src in enumerate((cb1_, cb2_, cb3_)):
                sp.dma_start(cnb[0:src.shape[0], n:n + 1], src.rearrange("(p a) -> p a", a=1)).then_inc(cn_in, 16)
            sp.dma_start(cnb[:, 3:4], cb4_.partition_broadcast(P)).then_inc(cn_in, 16)
            for n, src in enumerate((gb1, gb2)):
                sp.dma_start(gnb[0:src.shape[0], n:n + 1], src.rearrange("(p a) -> p a", a=1)).then_inc(cn_in, 16)
            sp.dma_start(gnb[:, 2:3], gb3.partition_broadcast(P)).then_inc(cn_in, 16)
            sp.dma_start(ar1[:], arange.partition_broadcast(P)).then_inc(cn_in, 16)
            sp.wait_ge(u_ready, B * EXPERTS * HB)
            sp.dma_start(wkv1s, wkv1).then_inc(wkv_in, 16)
            for p in range(PAIRS):
                r = p % 3
                sp.wait_ge(pj_free, PJ["c", p] + 1)
                for h in range(2):
                    row = DW * (1 - h)
                    sp.dma_start(QB[r][h][row:row + 1, :].bitcast(F32).rearrange("a (t n) -> a t n", t=NT),
                                 crow[NT * h:NT * h + NT, p % 2, :]).then_inc(c_in[r], 16)
            for b in range(B):
                sp.wait_ge(x_ready, LN["F", b] + 1)
                sp.dma_start(out[b].rearrange("(t p) d -> p t d", p=P), XS["0"][:, NT * b:NT * b + NT, :]).then_inc(out_sem, 16)
            sp.wait_ge(out_sem, 16 * B)

        @block.gpsimd
        def _(pool):
            pool.memset(ident[:], 0.0).then_inc(consts, 1)
            pool.memset(ones[:], 1.0).then_inc(consts, 1)
            pool.memset(half_neg[:], -0.5).then_inc(consts, 1)
            pool.memset(cnb[:], 0.0).then_inc(consts, 1)
            pool.memset(lnb[:], 0.5 * 11.090354888959125).then_inc(consts, 1)
            for w in (cn2, cn3, cn4):
                pool.memset(w[:], 0.0).then_inc(consts, 1)
            pool.memset(hmask[:], 1.0).then_inc(consts, 1)
            pool.memset(twist[:], 0.0).then_inc(consts, 1)
            pool.memset(v0x[:], 1.0).then_inc(consts, 1)
            pool.iota(topi[:, 0, 0, :], pattern=[[1, E]], base=0, channel_multiplier=0).then_inc(consts, 1)
            pool.wait_ge(consts, 12)
            pool.affine_select(out=ident[:], in_=ident[:], compare_op=ALU.not_equal, fill=1.0, base=0,
                               pattern=[[-1, P]], channel_multiplier=1).then_inc(consts, 1)
            pool.affine_select(out=hmask[:], in_=hmask[:], compare_op=ALU.is_ge, fill=0.0, base=0,
                               pattern=[[-DH, NH]], channel_multiplier=1).then_inc(consts, 1)
            pool.wait_ge(consts, 14)
            pool.affine_select(out=hmask[:], in_=hmask[:], compare_op=ALU.is_ge, fill=0.0, base=DH - 1,
                               pattern=[[DH, NH]], channel_multiplier=-1).then_inc(consts, 1)
            for n, (fill, off) in enumerate(((1.0, -64), (-1.0, -64), (-1.0, 64), (1.0, 64))):
                cols = twist[:, 32 * n:32 * n + 32]
                pool.affine_select(out=cols, in_=cols, compare_op=ALU.not_equal, fill=fill, base=off - 32 * n,
                                   pattern=[[-1, 32]], channel_multiplier=1).then_inc(consts, 1)
            setup = [0]

            def settled(ins):
                setup[0] += 1
                ins.then_inc(bvb_ready, 1)
                pool.wait_ge(bvb_ready, setup[0])

            def last_layers():
                pool.wait_ge(cn_in, N_CN)
                settled(pool.tensor_copy(cn4[0:32, :], w4col[:, 0:1].broadcast_to([32, P])))
                settled(pool.tensor_copy(gn3[:], w4col[:, 1:2].broadcast_to([32, P])))

            def rstd(key):
                n = LN[key]
                rows = CK if key[0] == "media" else P
                pool.wait_ge(var_ready, n + 1)
                pool.tensor_tensor(rs[0:rows, n, :], ve[0:rows, n, :], half_neg[0:rows, 0:NT], ALU.pow).then_inc(rstd_ready, 1)

            for b in range(B):
                pool.wait_ge(ss_ready, b + 1)
                pool.tensor_tensor(rn[:, NT * b:NT * b + NT], ss[:, NT * b:NT * b + NT], half_neg[:, 0:NT], ALU.pow).then_inc(rn_ready, 1)
            pool.wait_ge(w0_in, N_W0)
            settled(pool.tensor_copy(bv0b[:], b0s[:, 2:3].broadcast_to([P, P])))
            for r in range(3):
                for h in range(2):
                    lo = DW * (1 - h)
                    settled(pool.memset(QB[r][h][lo:lo + DW, :].bitcast(F32), 0.0))
                    settled(pool.memset(KBt[r][h][lo:lo + DW, :].bitcast(F32), 0.0))
            for r in range(3):
                for h in range(2):
                    lo = DW * (1 - h)
                    settled(pool.memset(KBt[r][h][lo:lo + 1, :].bitcast(F32), 1.0))
            for b in range(B):
                rstd(("A", b))
            rstd(("media", 0))
            pool.wait_ge(v_free, LV["k0",] + 1)
            for b in range(1, B):
                pool.tensor_tensor(KBD[:, b], k0T[:, b, :].unsqueeze(1).broadcast_to([P, NH, CK]),
                                   hmask[:].unsqueeze(2).broadcast_to([P, NH, CK]), ALU.mult).then_inc(kbd_more, 1)
            pool.wait_ge(v_free, LV["cb0",] + 1)
            def residual0(b):
                pool.wait_ge(a_full, LA["xT", "B", b] + 1)
                pool.tensor_tensor(xtile("A", b), xtile("A", b), CB0[:].unsqueeze(1).broadcast_to([P, NT, D]), ALU.add).then_inc(xr_ready, 1)

            for b in range(B - 1):
                residual0(b)
            def split_x(b):
                pool.wait_ge(xhi_ready, b + 1)
                pool.wait_ge(v_full, LV["router", b] + 1)
                pool.tensor_tensor(XLO[:, b, :], XT[:, b, :], XHI[:, b % 2, :].bitcast(F32), ALU.subtract).then_inc(xlo_ready, 1)

            def split_w(e):
                pool.wait_ge(uphi_ready, e + 1)
                blocks = slice(HB * e, HB * e + HB)
                pool.tensor_tensor(UPLO[:, :, blocks, :], up_weights[:, :, blocks, :], UPHI[:, :, blocks, :].bitcast(F32),
                                   ALU.subtract).then_inc(uplo_ready, 1)

            def split_wide(n):
                whole, lead, rest = WIDE[n]
                pool.wait_ge(wide_hi, n + 1)
                pool.tensor_tensor(rest, whole, lead.bitcast(F32), ALU.subtract).then_inc(wide_lo, 1)

            def split_lat(b):
                pool.wait_ge(lathi_ready, b + 1)
                pool.tensor_tensor(LATLO[:, b, :], LATT[:, b, :], LATHI[:, b, :].bitcast(F32), ALU.subtract).then_inc(latlo_ready, 1)

            rstd(("B", 0))
            residual0(B - 1)
            split_x(0)
            rstd(("B", 1))
            split_x(1)
            rstd(("B", 2))
            for e in range(EXPERTS):
                split_w(e)
                if e == 2:
                    rstd(("B", 3))
            for b in range(B):
                rstd(("C", b))
                if b < 2:
                    split_x(b + 2)
                if b == 0:
                    for n in range(3):
                        split_wide(n)
            pool.wait_ge(v_full, LV["down", B - 1, E] + 1)
            settled(pool.memset(VXA[:, :, :, :, DW:DW + 1], 1.0))
            for key in D_NORMS:
                rstd(key)
                if key == ("D", 3):
                    split_wide(3)
                elif key == ("lat", 2):
                    split_wide(4)
                    split_lat(0)
            split_wide(5)
            split_wide(6)
            for b in range(1, B):
                split_lat(b)
            pool.wait_ge(v_free, LV["cb1",] + 1)
            for b in range(B):
                pool.wait_ge(x_ready, LN["lat", b] + 1)
                pool.tensor_tensor(xtile("D", b), xtile("D", b), CB1[:].unsqueeze(1).broadcast_to([P, NT, D]), ALU.add).then_inc(xr_ready, 1)
            last_layers()

            for p in range(STEPS):
                if p % NHP == 1 and p > 1:
                    rstd(("E", p // NHP - 1))
            rstd(("E", B - 1))
            for b in range(B):
                rstd(("F", b))

        @block.scalar
        def _(act):
            def evac(key, dst, rows=P, cols=512, func=ACT.Copy, shape=None, **kw):
                n = LA[key]
                act.wait_ge(a_full, n + 1)
                src = bank_a(n)[0:rows, 0:cols]
                if shape:
                    src = src.rearrange(shape[0], **shape[1])
                act.activation(dst, src, func, **kw).then_inc(a_free, 1)

            act.wait_ge(consts, N_CONST)
            for b in range(B):
                act.wait_ge(x_in[b], 16)
                for t in range(NT):
                    tt = NT * b + t
                    act.activation(BIG[:, 2048 + 128 * tt:2048 + 128 * tt + 128], XS["0"][:, tt, :], ACT.Square,
                                   accum_out=ss[:, tt:tt + 1]).then_inc(sq_ready, 1)
            for b in range(B):
                evac(("xT", "A", b), XT[:, b, :])
            for b in range(B):
                evac(("rb", b), RBv[:, b, :])
                if b == B - 1:
                    evac(("ctxT",), ctxT[:].rearrange("p b k -> p (b k)"), cols=B * CK)
                for j in range(NT):
                    act.wait_ge(sim_ready, NT * b + j + 1)
                    act.activation(EX[:, b % 2, j, :], EX[:, b % 2, j, :], ACT.Exp,
                                   accum_out=rsum[:, NT * b + j:NT * b + j + 1]).then_inc(exp_ready, 1)

            def input0(b):
                evac(("xT", "B", b), XT[:, b, :])

            def queries0(b):
                evac(("qT0", b), QT0[:, b, :], func=ACT.Identity, bias=b0s[:, 0:1])

            def exp0(tt):
                act.wait_ge(s0_sub, tt + 1)
                act.activation(SM[:, tt % 2, :], SM[:, tt % 2, :], ACT.Exp, scale=SCALE_N).then_inc(p0_ready, 1)

            def exp_top(b):
                act.wait_ge(dl_ready, b + 1)
                act.activation(th0[:, b, :], dl[:, b, :], ACT.Exp).then_inc(th_ready, 1)

            input0(0)
            def split_x(b):
                act.wait_ge(a_free, LA["xT", "C", b] + 1)
                if b >= 2:
                    act.wait_ge(u_ready, HB * EXPERTS * (b - 1))
                act.activation(XHI[:, b % 2, :], XT[:, b, :], ACT.Copy).then_inc(xhi_ready, 1)

            queries0(0)
            exp0(0)
            for tt in range(TILES):
                if tt >= 2:
                    act.wait_ge(pv0_full, tt - 1)
                evac(("pT", tt, 0), PT0[:, tt % 2, 0:4, :].rearrange("p h n -> p (h n)"), rows=CK)
                evac(("pT", tt, 2), PT0[:, tt % 2, 8:12, :].rearrange("p h n -> p (h n)"), rows=CK)
                if tt + 1 < TILES:
                    exp0(tt + 1)
                for kind, b in between0(tt):
                    if kind == "cT":
                        evac(("cT", b), C0T[:, b, :])
                    elif kind == "x":
                        input0(b)
                    elif kind == "q":
                        queries0(b)
                    elif kind == "media":
                        act.wait_ge(perc_in, N_PERC)
                        evac(("mediaT",), MEDT[:, :, 0:CK], cols=B * CK, shape=("p (b k) -> p b k", {"k": CK}),
                             func=ACT.Identity, scale=lnw[:, 0:1], bias=lnw[:, 1:2])
                        act.wait_ge(a_free, LA["mediaT",] + 1)
                        act.activation(MEDT[:, :, CK:CK + 1], MEDT[:, :, CK - 1:CK], ACT.Copy).then_inc(med_ready, 1)
                    elif kind == "xC":
                        evac(("xT", "C", b), XT[:, b, :])
                        split_x(b)
                for kind, b in between0(tt - 1):
                    if kind == "route":
                        exp_top(b)
            act.wait_ge(moe_in, N_MOE)
            act.wait_ge(s0_ready, TILES)
            for e in range(EXPERTS):
                blocks = slice(HB * e, HB * e + HB)
                act.activation(UPHI[:, :, blocks, :], up_weights[:, :, blocks, :], ACT.Copy).then_inc(uphi_ready, 1)
                if e == 1:
                    evac(("xT", "C", B - 2), XT[:, B - 2, :])
                    evac(("cT", B - 1), C0T[:, B - 1, :])
            def split_wide(n):
                act.activation(WIDE[n][1], WIDE[n][0], ACT.Copy).then_inc(wide_hi, 1)

            for n in range(B * EXPERTS * HB):
                act.wait_ge(g_ready, n + 1)
                if n >= 4:
                    act.wait_ge(h_ready, n - 3)
                act.activation(SG[:, n % 4, :], PS[:, n % 2, :], ACT.Silu).then_inc(silu_ready, 1)
                if n == HB:
                    exp_top(B - 2)
                if n == HB * EXPERTS:
                    split_x(2)
                if n == HB * EXPERTS + 2:
                    act.wait_ge(v_full, LV["cb1",] + 1)
                    act.wait_ge(med_ready, 1)
                    for m in range(3):
                        split_wide(m)
                if n == 2 * HB * EXPERTS:
                    split_x(3)
                if n == HB * (LAST_ROUTER + 2) - 1:
                    evac(("xT", "C", B - 1), XT[:, B - 1, :])
                    exp_top(B - 1)
            for b in range(B):
                evac(("xT", "D", b), XT[:, b, :])
            act.wait_ge(h_ready, B * EXPERTS * HB)
            act.wait_ge(v_full, LV["down", B - 1, E] + 1)
            for b in range(B):
                for t in range(NT):
                    act.wait_ge(qkv_ready, NT * b + t + 1)
                    act.activation(QK[:, b, t, :], PS[:, t, 0:2 * D], ACT.Copy).then_inc(qk_copied, 1)
                act.wait_ge(qk_copied, NT * (b + 1))
                if b >= 1:
                    act.wait_ge(ssq_ready, b)
                for half in range(2):
                    act.activation(SQ[:, half].rearrange("p t n -> p (t n)"), QK[:, b].rearrange("p t n -> p (t n)")[:, 512 * half:512 * half + 512],
                                   ACT.Square).then_inc(sqq_ready, 1)
            for b in range(B):
                act.wait_ge(ssq_ready, b + 1)
                act.activation(SSQ[:, b], SSQ[:, b], ACT.Ln, scale=LN_SCALE).then_inc(act_seq, 1)
            for b in range(B):
                act.wait_ge(act_seq, b + 1)
                act.activation(SSQ[:, b], SSQ[:, b], ACT.Exp, scale=-0.5, bias=lnb[:]).then_inc(lnorm_ready, 1)
            for b in range(B):
                act.wait_ge(qkn_ready, b + 1)
                qk = QK[:, b].rearrange("p t n -> p (t n)")
                act.activation(qk, qk, ACT.Exp).then_inc(act_seq, 1)
            for b in range(B):
                act.wait_ge(act_seq, B + b + 1)
                qk = QK[:, b].rearrange("p t n -> p (t n)")
                act.activation(qk, qk, ACT.Ln, bias=ones[:, 0:1]).then_inc(act_seq, 1)
            for b in range(B):
                evac(("qT", b), QTD[:, b, :])
            act.wait_ge(v_full, LV["oD", B - 1, 1] + 1)
            act.wait_ge(wkv_in, 16)
            for n in range(3, 7):
                split_wide(n)
            for b in range(B):
                evac(("latT", b), LATT[:, b, :], func=ACT.Identity, scale=lnw[:, 2:3], bias=lnw[:, 3:4])
                act.wait_ge(a_free, LA["latT", b] + 1)
                act.activation(LATHI[:, b, :], LATT[:, b, :], ACT.Copy).then_inc(lathi_ready, 1)

            def hi(key, h):
                kind, p = key
                r, hp = p % 3, p % NHP
                n = PJ[key]
                own, other = slice(DW * h, DW * h + DW), slice(DW * (1 - h), DW * (1 - h) + DW)
                act.wait_ge(pj_full, n + 1)
                if p >= 3 and kind == "Q" and h == 0:
                    act.wait_ge(sw_ready, SLOTS * (p - 2))
                if kind == "Q":
                    dsts, width, bias = (QA[r][h][own, :], QB[r][h][own, :]), S, b1s[own, 0, hp:hp + 1]
                elif kind == "K":
                    dsts, width, bias = (KA[r][h][own, 0:S], KA[r][h][other, 0:S]), S, b1s[own, 1, hp:hp + 1]
                else:
                    dsts, width, bias = (KA[r][h][own, S:KEYS_PAD], KA[r][h][other, S:KEYS_PAD]), KEYS_PAD - S, b1s[own, 1, hp:hp + 1]
                for dst in dsts:
                    act.activation(dst, PS[own, 6 + n % 2, 0:width], ACT.Identity, bias=bias).then_inc(hi_ready, 1)

            act.wait_ge(a_full, LA["latT", B - 1] + 1)
            for p in range(2):
                for kind in ("Q", "K", "Kt"):
                    for h in range(2):
                        hi((kind, p), h)
            for p in range(STEPS):
                tasks = step_tasks(p)
                for slot in range(SLOTS):
                    g = SLOTS * p + slot
                    j = slot % KB
                    rows = min(P, KEYS - P * j)
                    act.wait_ge(sw_ready, g + 1)
                    if g >= 4:
                        act.wait_ge(pv_ready, g - 3)
                    act.activation(PX[0:rows, g % 4, :], PS[0:rows, g % 2, :], ACT.Exp, scale=SCALE_W).then_inc(pw_ready, 1)
                    for key, h in splits(tasks, slot):
                        hi(key, h)
            for b in range(B):
                evac(("xT", "F", b), FS[:, b, :])
            act.wait_ge(cn_in, N_CN)
            act.wait_ge(coef_ready, 1)
            global_layers = ((gact1[:], 64, ACT.Gelu, 1.0 / S, gnb[0:64, 0:1]), (gact2[:], 32, ACT.Gelu, 1.0, gnb[0:32, 1:2]),
                             (gth[:], P, ACT.Tanh, 0.5, cbias[:, 1:2]))
            for c in range(CYCLES):
                for layer, (dst, func, scale, bias) in enumerate((
                        (H1, ACT.Gelu, 1.0, cnb[:, 0:1]), (H2, ACT.Gelu, 1.0, cnb[:, 1:2]),
                        (H3, ACT.Gelu, 1.0, cnb[:, 2:3]), (TH, ACT.Tanh, 0.5, cbias[:, 0:1]))):
                    for b in range(B):
                        if layer == 3 and c:
                            act.wait_ge(state_ready, B * (c - 1) + b + 1)
                        evac(("cn", c, layer, b), dst[:, b, :], func=func, scale=scale, bias=bias)
                    if c == 0 and layer < 3:
                        gdst, rows, func, scale, bias = global_layers[layer]
                        evac(("gn", layer), gdst, rows=rows, cols=B, func=func, scale=scale, bias=bias)

        @block.vector
        def _(dve):
            count = [0]

            def link(ins):
                count[0] += 1
                ins.then_inc(dve_seq, 1)
                dve.wait_ge(dve_seq, count[0])

            def norm_stats(key, src, rows=P):
                n = LN[key]
                for t in range(NT):
                    ins = dve.bn_stats(out=st[0:rows, n % 2, t, :], in_=src[0:rows, t, :])
                link(ins)
                for t in range(NT):
                    ins = dve.bn_aggr(out=mv[0:rows, n, t, :], in_=st[0:rows, n % 2, t, :])
                link(ins)
                dve.tensor_scalar_add(ve[0:rows, n, :], mv[0:rows, n, :, 1], LN_EPS).then_inc(var_ready, 1)

            def norm_apply(key, src, dst, rows=P):
                n = LN[key]
                dve.wait_ge(rstd_ready, n + 1)
                for t in range(NT):
                    ins = dve.tensor_scalar(dst[0:rows, t, :], src[0:rows, t, :], mv[0:rows, n, t, 0:1], rs[0:rows, n, t:t + 1],
                                            ALU.subtract, ALU.mult)
                ins.then_inc(x_ready, 1)

            def norm(key, src, dst, rows=P):
                norm_stats(key, src, rows)
                norm_apply(key, src, dst, rows)

            dve.wait_ge(consts, N_CONST)
            dve.tensor_copy(iota[:], topi[:, 0, 0, :])
            link(dve.tensor_scalar_mul(hmask_s[:], hmask[:], SCALE_N))
            for b in range(B):
                dve.wait_ge(sq_ready, NT * (b + 1))
                cols = slice(NT * b, NT * b + NT)
                dve.tensor_scalar_max(ss[:, cols], ss[:, cols], 1e-37).then_inc(ss_ready, 1)
            for b in range(B):
                dve.wait_ge(rn_ready, b + 1)
                dve.tensor_tensor(DG[:, b, :].rearrange("p (t n) -> p t n", t=NT), ident[:].unsqueeze(1).broadcast_to([P, NT, P]),
                                  rn[:, NT * b:NT * b + NT].unsqueeze(2).broadcast_to([P, NT, P]), ALU.mult).then_inc(diag_ready, 1)

            def sims(b):
                for j in range(NT):
                    n = NT * b + j
                    dve.wait_ge(a_free, LA["rb", b] + 1)
                    link(dve.tensor_scalar(GX[:, n % 2, :], RBv[:, b, :], rn[:, n:n + 1], 1.0 / COS_EPS, ALU.mult, ALU.min))
                    dve.wait_ge(dots_ready, n + 1)
                    dve.wait_ge(sq_ready, TILES)
                    if b >= 2:
                        dve.wait_ge(v_full, LV["oA", b - 2] + 1)
                    dve.tensor_tensor(EX[:, b % 2, j, :], PS[:, j, :], GX[:, n % 2, :], ALU.mult).then_inc(sim_ready, 1)

            def out_a(b):
                n = LV["oA", b]
                cols = slice(NT * b, NT * b + NT)
                dve.wait_ge(exp_ready, NT * (b + 1))
                link(dve.reciprocal(rinv[:, cols], rsum[:, cols]))
                dve.wait_ge(v_full, n + 1)
                for t in range(NT):
                    ins = dve.scalar_tensor_tensor(Y[:, b, t, :], bank_v(n)[:, P * t:P * t + P], rinv[:, NT * b + t:NT * b + t + 1],
                                                   XS["0"][:, NT * b + t, :], ALU.mult, ALU.add)
                ins.then_inc(v_free, 1)
                dve.wait_ge(v_free, n + 1)
                link(dve.tensor_tensor(Y[:, b], Y[:, b], xtile("0", b), ALU.add))
                norm_stats(("A", b), Y[:, b])

            sims(0)
            def context0():
                n = LV["k0",]
                dve.wait_ge(v_full, n + 1)
                dve.wait_ge(w0_in, N_W0)
                dve.tensor_scalar_add(k0T[:].rearrange("p b k -> p (b k)"), bank_v(n)[:, 0:B * CK], b0s[:, 1:2]).then_inc(v_free, 1)
                dve.wait_ge(v_free, n + 1)
                dve.tensor_tensor(KBD[:, 0], k0T[:, 0, :].unsqueeze(1).broadcast_to([P, NH, CK]),
                                  hmask[:].unsqueeze(2).broadcast_to([P, NH, CK]), ALU.mult).then_inc(kbd_ready, 1)
                n = LV["v0",]
                dve.wait_ge(v_full, n + 1)
                dve.tensor_copy(v0x[:, :, :, 0:DH], bank_v(n)[0:CK, :].rearrange("p (b h d) -> p b h d", b=B, h=NH)).then_inc(v_free, 1)
                n = LV["cb0",]
                dve.wait_ge(v_full, n + 1)
                dve.tensor_tensor(CB0[:], bank_v(n)[:, 0:D], bo0s[:], ALU.add).then_inc(v_free, 1)

            for b in range(B):
                if b + 1 < B:
                    sims(b + 1)
                if b:
                    norm_apply(("A", b - 1), Y[:, b - 1], xtile("A", b - 1))
                if b == 2:
                    context0()
                out_a(b)
            dve.wait_ge(ctx_in, 16)
            norm_stats(("media", 0), ctx_sb, rows=CK)
            norm_apply(("A", B - 1), Y[:, B - 1], xtile("A", B - 1))
            norm_apply(("media", 0), ctx_sb, ctxn, rows=CK)

            def max_sub(tt):
                r = tt % 2
                dve.wait_ge(s0_ready, tt + 1)
                wide = PS[:, 0:2, 0:6 * CK].rearrange("p a (h k) -> p a h k", k=CK)
                rest = PS[:, 2, 0:4 * CK].rearrange("p (h k) -> p h k", k=CK)
                dve.tensor_reduce(mx0[:, r, 0:12].rearrange("p (a h) -> p a h", a=2), wide, AX.X, ALU.max)
                link(dve.tensor_reduce(mx0[:, r, 12:16], rest, AX.X, ALU.max))
                if tt >= 2:
                    dve.wait_ge(v_full, LV["pT", tt - 2, 3] + 1)
                    dve.wait_ge(a_full, LA["pT", tt - 2, 2] + 1)
                sm = SM[:, r, :].rearrange("p (h k) -> p h k", k=CK)
                dve.tensor_tensor(sm[:, 0:12, :].rearrange("p (a h) k -> p a h k", a=2), wide,
                                  mx0[:, r, 0:12].rearrange("p (a h) -> p a h", a=2).unsqueeze(3).broadcast_to([P, 2, 6, CK]), ALU.subtract)
                dve.tensor_tensor(sm[:, 12:16, :], rest, mx0[:, r, 12:16].unsqueeze(2).broadcast_to([P, 4, CK]),
                                  ALU.subtract).then_inc(s0_sub, 1)

            def y_b(b):
                n = LV["yB", b]
                dve.wait_ge(v_full, n + 1)
                dve.wait_ge(xr_ready, b + 1)
                dve.tensor_tensor(Y[:, b], bank_v(n).rearrange("p (t d) -> p t d", t=NT), xtile("A", b), ALU.add).then_inc(v_free, 1)
                dve.wait_ge(v_free, n + 1)
                norm_stats(("B", b), Y[:, b])

            def divide0(tt):
                b, t = divmod(tt, NT)
                dve.wait_ge(pv0_full, tt + 1)
                o = PS[:, 3, 0:NH * (DH + 1)].rearrange("p (h d) -> p h d", h=NH)
                link(dve.reciprocal(r0[:, tt % 2, :], o[:, :, DH]))
                dve.tensor_tensor(C0[:, b, t, :].rearrange("p (h d) -> p h d", h=NH), o[:, :, 0:DH],
                                  r0[:, tt % 2, :].unsqueeze(2).broadcast_to([P, NH, DH]), ALU.mult).then_inc(pv0_free, 1)

            def route(b):
                n = LV["router", b]
                dve.wait_ge(v_full, n + 1)
                dve.tensor_copy(lg[:, b].rearrange("p t e -> p (t e)"), bank_v(n)[:, 0:NT * E]).then_inc(v_free, 1)
                dve.wait_ge(v_free, n + 1)
                for t in range(NT):
                    ins = dve.max(top[:, b, t, :], lg[:, b, t, :])
                link(ins)
                dve.tensor_tensor(dl[:, b, :], top[:, b, :, 1], top[:, b, :, 0], ALU.subtract).then_inc(dl_ready, 1)
                for t in range(NT):
                    ins = dve.max_index(topi[:, b, t, :], top[:, b, t, :], lg[:, b, t, :])
                link(ins)
                link(dve.tensor_copy(topf[:, b], topi[:, b, :, 0:2]))

            def combine(b):
                dve.wait_ge(th_ready, b + 1)
                link(dve.tensor_scalar_add(wtop[:, b, 0, :], th0[:, b, :], 1.0))
                link(dve.reciprocal(wtop[:, b, 0, :], wtop[:, b, 0, :]))
                dve.tensor_tensor(wtop[:, b, 1, :], th0[:, b, :], wtop[:, b, 0, :], ALU.mult)
                for i in range(2):
                    ins = dve.tensor_tensor(eq[:, i], iota[:].unsqueeze(1).broadcast_to([P, NT, E]),
                                            topf[:, b, :, i].unsqueeze(2).broadcast_to([P, NT, E]), ALU.is_equal)
                link(ins)
                for i in range(2):
                    ins = dve.tensor_tensor(eq[:, i], eq[:, i], wtop[:, b, i, :].unsqueeze(2).broadcast_to([P, NT, E]), ALU.mult)
                link(ins)
                link(dve.tensor_tensor(comb[:, b], eq[:, 0], eq[:, 1], ALU.add))

            max_sub(0)
            for tt in range(TILES):
                if tt + 1 < TILES:
                    max_sub(tt + 1)
                if tt >= 2:
                    dve.wait_ge(pv0_full, tt - 1)
                for g in (1, 3):
                    n = LV["pT", tt, g]
                    dve.wait_ge(v_full, n + 1)
                    dve.tensor_copy(PT0[:, tt % 2, 4 * g:4 * g + 4, :].rearrange("p h n -> p (h n)"), bank_v(n)[0:CK, :]).then_inc(v_free, 1)
                if tt:
                    divide0(tt - 1)
                if tt % NT == 3 and tt > NT:
                    norm_apply(("B", tt // NT - 1), Y[:, tt // NT - 1], xtile("B", tt // NT - 1))
                for kind, b in between0(tt):
                    if kind == "y":
                        y_b(b)
                    elif kind == "route":
                        route(b)
                for kind, b in between0(tt - 1):
                    if kind == "route":
                        combine(b)
            divide0(TILES - 1)

            def gate(n):
                e_all, k = divmod(n, HB)
                dve.wait_ge(silu_ready, n + 1)
                dve.wait_ge(u_ready, n + 1)
                if e_all >= 3:
                    dve.wait_ge(v_full, LV["down", (e_all - 3) // EXPERTS, (e_all - 3) % EXPERTS] + 1)
                dve.tensor_tensor(HX[:, e_all % 3, k, :], PS[:, 2 + n % 2, :], SG[:, n % 4, :], ALU.mult).then_inc(h_ready, 1)

            def accumulate(e_all):
                b, e = divmod(e_all, EXPERTS)
                n = LV["down", b, e]
                dve.wait_ge(v_full, n + 1)
                if e == E:
                    dve.tensor_tensor(Y[:, b], bank_v(n).rearrange("p (t d) -> p t d", t=NT), Y[:, b], ALU.add).then_inc(v_free, 1)
                else:
                    for t in range(NT):
                        ins = dve.scalar_tensor_tensor(Y[:, b, t, :], bank_v(n)[:, P * t:P * t + P], comb[:, b, t, e:e + 1],
                                                       XS["B"][:, NT * b + t, :] if e == 0 else Y[:, b, t, :], ALU.mult, ALU.add)
                    ins.then_inc(v_free, 1)
                dve.wait_ge(v_free, n + 1)
                if e == E:
                    norm(("C", b), Y[:, b], xtile("C", b))

            for k in range(HB):
                gate(k)
            y_b(B - 1)
            route(B - 2)
            for e_all in range(B * EXPERTS):
                if e_all + 1 < B * EXPERTS:
                    for k in range(HB):
                        gate(HB * (e_all + 1) + k)
                accumulate(e_all)
                if e_all == 0:
                    norm_apply(("B", B - 1), Y[:, B - 1], xtile("B", B - 1))
                    combine(B - 2)
                    dve.wait_ge(perc_in, N_PERC)
                    dve.tensor_copy(bv1b, b1s[:, 2, :].unsqueeze(2).broadcast_to([P, NHP, P])).then_inc(bv1_ready, 1)
                if e_all == LAST_ROUTER:
                    route(B - 1)
                    combine(B - 1)
                if e_all == BIAS_ROW:
                    n = LV["cb1",]
                    dve.wait_ge(v_full, n + 1)
                    dve.tensor_tensor(CB1[:], bank_v(n)[:, 0:D], bout1s[:], ALU.add).then_inc(v_free, 1)
            dve.memset(VXv[:, :, :, D:D + 1], 1.0)
            for b in range(B):
                for t in range(NT):
                    dve.wait_ge(qk_copied, NT * b + t + 1)
                    dve.tensor_copy(VXv[:, b, t, 0:D], PS[:, t, 2 * D:3 * D]).then_inc(vx_ready, 1)
                dve.wait_ge(sqq_ready, 2 * b + 2)
                link(dve.tensor_reduce(SSQ[:, b], SQ.rearrange("p r t (h d) -> p (r t h) d", d=DH), AX.X, ALU.add))
                dve.tensor_scalar_max(SSQ[:, b], SSQ[:, b], L2_EPS ** 2).then_inc(ssq_ready, 1)
            for b in range(B):
                dve.wait_ge(lnorm_ready, b + 1)
                qk = QK[:, b].rearrange("p t (h d) -> p (t h) d", d=DH)
                dve.tensor_tensor(qk, qk, SSQ[:, b].unsqueeze(2).broadcast_to([P, NT * 2 * NH, DH]), ALU.mult).then_inc(qkn_ready, 1)
            for b in range(B):
                n = LV["kv", b]
                dve.wait_ge(v_full, n + 1)
                kv = bank_v(n)
                dve.tensor_tensor(KVB[:, b, 0:D].rearrange("p (h d) -> p h d", h=NH), kv[:, 0:D].rearrange("p (h d) -> p h d", h=NH),
                                  hmask_s[:].unsqueeze(2).broadcast_to([P, NH, DH]), ALU.mult)
                dve.tensor_scalar_add(kse[:, b:b + 1], kv[:, D:D + 1], KSUM_EPS).then_inc(v_free, 1)
                dve.wait_ge(v_free, n + 1)
                dve.tensor_scalar_mul(KVB[:, b, D:D + NH], hmask[:], kse[:, b:b + 1]).then_inc(kvb_ready, 1)
            def out_d(b):
                for h in range(2):
                    n = LV["oD", b, h]
                    dve.wait_ge(v_full, n + 1)
                    o = bank_v(n)[:, 0:2 * (D + NH)].rearrange("p (t n) -> p t n", t=2)
                    rec = eq[:, :, :, :].rearrange("p a t e -> p (a t e)")[:, 0:2 * NH].rearrange("p (t h) -> p t h", t=2)
                    link(dve.reciprocal(rec, o[:, :, D:D + NH]))
                    for t in range(2):
                        ins = dve.tensor_tensor(Y[:, b, 2 * h + t, :].rearrange("p (h d) -> p h d", h=NH),
                                                o[:, t, 0:D].rearrange("p (h d) -> p h d", h=NH),
                                                rec[:, t, :].unsqueeze(2).broadcast_to([P, NH, DH]), ALU.mult)
                    ins.then_inc(v_free, 1)
                    dve.wait_ge(v_free, n + 1)
                link(dve.tensor_tensor(Y[:, b], Y[:, b], xtile("C", b), ALU.add))

            def apply_d(key):
                kind, b = key
                if kind == "D":
                    norm_apply(key, Y[:, b], xtile("D", b))
                else:
                    norm_apply(key, xtile("D", b), LAT[:, b])

            for i, key in enumerate(D_NORMS):
                kind, b = key
                if kind == "D":
                    out_d(b)
                    norm_stats(key, Y[:, b])
                else:
                    dve.wait_ge(x_ready, LN["D", b] + 1)
                    norm_stats(key, xtile("D", b))
                if i:
                    apply_d(D_NORMS[i - 1])
            apply_d(D_NORMS[-1])

            def lo(key, h):
                kind, p = key
                r, hp = p % 3, p % NHP
                n = PJ[key]
                dve.wait_ge(hi_ready, 12 * p + {"Q": 0, "K": 4, "Kt": 8}[kind] + 2 * h + 2)
                rows, other = slice(DW * h, DW * h + DW), slice(DW * (1 - h), DW * (1 - h) + DW)
                if kind == "Q":
                    lead, dst, width, bias = QA[r][h][rows, :], QA[r][h][other, :], S, b1s[rows, 0, hp:hp + 1]
                elif kind == "K":
                    lead, dst, width, bias = KA[r][h][rows, 0:S], KBt[r][h][rows, 0:S], S, b1s[rows, 1, hp:hp + 1]
                else:
                    width = KEYS_PAD - S
                    lead, dst, bias = KA[r][h][rows, S:KEYS_PAD], KBt[r][h][rows, S:KEYS_PAD], b1s[rows, 1, hp:hp + 1]
                ins = dve.scalar_tensor_tensor(dst, PS[rows, 6 + n % 2, 0:width], bias, lead.bitcast(F32), ALU.add, ALU.subtract)
                ins.then_inc(lo_ready if h == 0 else pj_free, 1)

            def value(key):
                _, b, u = key
                n = PJ[key]
                j, half = divmod(u, 2)
                rows = min(P, KEYS - P * j)
                dve.wait_ge(pj_full, n + 1)
                dve.tensor_copy(VXA[0:rows, b % 2, j, 8 * half:8 * half + 8, 0:DW],
                                PS[0:rows, 6 + n % 2, :].rearrange("p (h d) -> p h d", h=8)).then_inc(pj_free, 1)

            def c_rows(key):
                p = key[1]
                n = PJ[key]
                dve.wait_ge(pj_full, n + 1)
                if p >= 2:
                    dve.wait_ge(c_in[(p - 2) % 3], 32 * ((p - 2) // 3 + 1))
                dve.tensor_scalar_mul(crow[:, p % 2, :], PS[0:2 * NT, 6 + n % 2, 0:P], -1.0).then_inc(pj_free, 1)

            def task(key):
                kind = key[0]
                n = PJ[key]
                if kind == "V":
                    value(key)
                elif kind == "c":
                    c_rows(key)
                elif kind == "oT":
                    dve.wait_ge(pj_full, n + 1)
                    dve.tensor_copy(OT[:, key[1] % NHP, :], PS[:, 6 + n % 2, :]).then_inc(pj_free, 1)
                else:
                    b = key[1]
                    dve.wait_ge(pj_full, n + 1)
                    dve.wait_ge(xr_ready, B + b + 1)
                    dve.tensor_tensor(Y[:, b], PS[:, 6 + n % 2, :].rearrange("p (t d) -> p t d", t=NT), xtile("D", b), ALU.add).then_inc(pj_free, 1)
                    dve.wait_ge(pj_free, n + 1)
                    norm(("E", b), Y[:, b], xtile("E", b))

            def maxima(p, u):
                h, m = divmod(u, 5)
                g = 10 * p + u
                dve.wait_ge(mu_full, g + 1)
                if m < NT:
                    dve.tensor_reduce(mxm[:, p % 2, h, m:m + 1], PS[:, 2 + g % 2, :], AX.X, ALU.max).then_inc(mu_free, 1)
                else:
                    dve.tensor_reduce(mxt[:, p % 2, h, :], PS[:, 2 + g % 2, 0:NT * (KEYS_PAD - S)].rearrange("p (t k) -> p t k", t=NT),
                                      AX.X, ALU.max).then_inc(mu_free, 1)
                    dve.wait_ge(mu_free, g + 1)
                    dve.tensor_tensor(cmx[:, p % 2, h, :], mxm[:, p % 2, h, :], mxt[:, p % 2, h, :], ALU.max).then_inc(cm_ready, 1)

            def head_out(head):
                p, h = divmod(head, 2)
                b = p // NHP
                o = PS[:, 4 + head % 2, 0:NT * (DW + 1)].rearrange("p (t d) -> p t d", t=NT)
                dve.wait_ge(pv_ready, KB * (head + 1))
                link(dve.reciprocal(rden[:, head % 2, :], o[:, :, DW]))
                if p >= 2:
                    dve.wait_ge(pj_full, PJ["oT", p - 2] + 1)
                dve.tensor_tensor(CT[:, p % 2, :, DW * h:DW * h + DW], o[:, :, 0:DW],
                                  rden[:, head % 2, :].unsqueeze(2).broadcast_to([P, NT, DW]), ALU.mult).then_inc(on_ready, 1)

            dve.wait_ge(bvb_ready, N_E_OPERANDS)
            for key in PROLOGUE:
                if key[0] == "max":
                    maxima(0, key[1])
                elif key[0] in ("Q", "K", "Kt"):
                    for h in range(2):
                        lo(key, h)
                else:
                    task(key)
            for p in range(STEPS):
                tasks = step_tasks(p)
                for slot in range(SLOTS):
                    if p + 1 < PAIRS:
                        for u in MAX_UNITS.get(slot, []):
                            maxima(p + 1, u)
                    if slot == 0 and p:
                        head_out(2 * p - 1)
                    if slot == KB:
                        head_out(2 * p)
                    for key, h in splits(tasks, slot - 1):
                        lo(key, h)
                    for key in tasks.get(slot, []):
                        if key[0] not in ("Q", "K", "Kt"):
                            task(key)
            head_out(2 * PAIRS - 1)
            for key in EPILOGUE:
                task(key)
            dve.wait_ge(cn_in, N_CN)
            dve.tensor_scalar_mul(cbias[:, 0:1], cnb[:, 3:4], 0.5)
            dve.tensor_scalar_mul(cA[:], ar1[:], 0.3)
            dve.tensor_scalar_mul(cbias[:, 1:2], gnb[:, 2:3], 0.5).then_inc(coef_ready, 1)
            for b in range(B):
                dve.wait_ge(a_free, LA["xT", "F", b] + 1)
                dve.tensor_reduce(gsum[:, b:b + 1], FS[:, b, :], AX.X, ALU.add).then_inc(gs_ready, 1)
            dve.wait_ge(a_free, LA["gn", 2] + 1)
            link(dve.tensor_scalar(cB[:], gth[:], ar1[:], 0.7, ALU.mult, ALU.mult))
            link(dve.tensor_scalar_add(cB[:], cB[:], 0.1))
            def back(b):
                n = LV["back", b]
                dve.wait_ge(v_full, n + 1)
                dve.tensor_tensor(Y[:, b], bank_v(n).rearrange("p (t d) -> p t d", t=NT), xtile("E", b), ALU.add).then_inc(v_free, 1)
                dve.wait_ge(v_free, n + 1)
                norm_stats(("F", b), Y[:, b])
                if b:
                    norm_apply(("F", b - 1), Y[:, b - 1], xtile("0", b - 1))

            for c in range(CYCLES):
                for b in range(B):
                    if c == CYCLES - 1 and b >= 2:
                        back(b - 2)
                    dve.wait_ge(a_free, LA["cn", c, 3, b] + 1)
                    link(dve.tensor_scalar(CP[:, b, :], TH[:, b, :], cA[:], cB[:, b:b + 1], ALU.mult, ALU.add))
                    n = LV["twist", c, b]
                    dve.wait_ge(v_full, n + 1)
                    dve.tensor_tensor(CP[:, b, :], CP[:, b, :], bank_v(n), ALU.mult).then_inc(v_free, 1)
                    dve.wait_ge(v_free, n + 1)
                    dve.tensor_tensor(FS[:, b, :], FS[:, b, :], CP[:, b, :], ALU.add).then_inc(state_ready, 1)
            for b in range(B - 2, B):
                back(b)
            norm_apply(("F", B - 1), Y[:, B - 1], xtile("0", B - 1))

        @block.tensor
        def _(pe):
            def lane_a(key, emit):
                n = LA[key]
                if n >= 2:
                    pe.wait_ge(a_free, n - 1)
                emit(bank_a(n)).then_inc(a_full, 1)

            def lane_v(key, emit):
                n = LV[key]
                if n >= 2:
                    pe.wait_ge(v_free, n - 1)
                emit(bank_v(n)).then_inc(v_full, 1)

            def mm(dst, lhsT, rhs, start=True, stop=True, **kw):
                return pe.matmul(dst, lhsT, rhs, start=start, stop=stop, **kw)

            def product(dst, a_hi, a_lo, b_hi, b_lo):
                mm(dst, a_hi, b_hi, stop=False)
                mm(dst, a_hi, b_lo, start=False, stop=False)
                return mm(dst, a_lo, b_hi, start=False)

            def transposes(srcs, rows=P):
                def emit(bank):
                    for n, src in enumerate(srcs):
                        ins = pe.transpose(bank[0:src.shape[1], rows * n:rows * n + rows], src, ident[0:rows, 0:rows])
                    return ins
                return emit

            def tiles_of(x3):
                return [x3[:, t, :] for t in range(NT)]

            pe.wait_ge(consts, N_CONST)
            for b in range(B):
                pe.wait_ge(x_in[b], 16)
                lane_a(("xT", "A", b), transposes(tiles_of(xtile("0", b))))

            def dots(b):
                pe.wait_ge(diag_ready, b + 1)
                lane_a(("rb", b), lambda bank: mm(bank, ones[:], DG[:, b, :]))
                pe.wait_ge(a_free, LA["xT", "A", b] + 1)
                for j in range(NT):
                    if b:
                        pe.wait_ge(sim_ready, NT * (b - 1) + j + 1)
                    mm(PS[:, j, :], XT[:, b, P * j:P * j + P], XT[:, b, :]).then_inc(dots_ready, 1)

            def out_a(b):
                pe.wait_ge(exp_ready, NT * (b + 1))

                def emit(bank):
                    for i in range(NT):
                        for j in range(NT):
                            ins = mm(bank[:, P * i:P * i + P], EX[:, b % 2, j, P * i:P * i + P], XS["0"][:, NT * b + j, :],
                                     start=j == 0, stop=j == NT - 1)
                    return ins
                lane_v(("oA", b), emit)

            def context0():
                pe.wait_ge(ctx_in, 16)
                lane_a(("ctxT",), transposes([ctx_sb[:, b, :] for b in range(B)], rows=CK))
                pe.wait_ge(a_free, LA["ctxT",] + 1)
                pe.wait_ge(w0_in, N_W0)
                lane_v(("k0",), lambda bank: mm(bank[:, 0:B * CK], wk0s[:], ctxT[:].rearrange("p b k -> p (b k)")))

                def v0(bank):
                    for b in range(B):
                        ins = mm(bank[0:CK, D * b:D * b + D], ctxT[:, b, :], wv0s[:])
                    return ins
                lane_v(("v0",), v0)
                pe.wait_ge(bvb_ready, 1)
                lane_v(("cb0",), lambda bank: mm(bank[:, 0:D], bv0b[:], wo0s[:]))

            dots(0)
            for b in range(B):
                if b + 1 < B:
                    dots(b + 1)
                if b == 2:
                    context0()
                out_a(b)

            def input0(b):
                pe.wait_ge(x_ready, LN["A", b] + 1)
                lane_a(("xT", "B", b), transposes(tiles_of(xtile("A", b))))

            def queries0(b):
                pe.wait_ge(a_free, LA["xT", "B", b] + 1)
                lane_a(("qT0", b), lambda bank: mm(bank, wq0s[:], XT[:, b, :]))

            def input_c(b):
                pe.wait_ge(x_ready, LN["B", b] + 1)
                lane_a(("xT", "C", b), transposes(tiles_of(xtile("B", b))))

            def route(b):
                pe.wait_ge(a_free, LA["xT", "C", b] + 1)
                pe.wait_ge(qkv_in, N_QKV)

                def router(bank):
                    for t in range(NT):
                        ins = mm(bank[:, E * t:E * t + E], XT[:, b, P * t:P * t + P], wrT[:])
                    return ins
                lane_v(("router", b), router)

            def scores0(tt):
                b, t = divmod(tt, NT)
                pe.wait_ge(a_free, LA["qT0", b] + 1)
                if b == 0:
                    pe.wait_ge(kbd_ready, 1)
                else:
                    pe.wait_ge(kbd_more, b)
                if tt:
                    pe.wait_ge(s0_sub, tt)
                for n, (h0, hn) in enumerate(((0, 6), (6, 6), (12, 4))):
                    ins = mm(PS[:, n, 0:hn * CK], QT0[:, b, P * t:P * t + P], KBD[:, b, h0:h0 + hn, :].rearrange("p h k -> p (h k)"))
                ins.then_inc(s0_ready, 1)

            def turn0(tt):
                pe.wait_ge(p0_ready, tt + 1)
                sm = SM[:, tt % 2, :].rearrange("p (h k) -> p h k", k=CK)
                for g in range(4):
                    lane = lane_a if g % 2 == 0 else lane_v
                    lane(("pT", tt, g), transposes([sm[:, 4 * g + i, :] for i in range(4)]))

            def weigh0(tt):
                b = tt // NT
                pe.wait_ge(a_free, LA["pT", tt, 2] + 1)
                pe.wait_ge(v_free, LV["pT", tt, 3] + 1)
                if tt:
                    pe.wait_ge(pv0_free, tt)
                for h in range(NH):
                    ins = mm(PS[:, 3, (DH + 1) * h:(DH + 1) * (h + 1)], PT0[:, tt % 2, h, :], v0x[:, b, h, :])
                ins.then_inc(pv0_full, 1)

            def c_t(b):
                pe.wait_ge(pv0_free, NT * b + NT)
                lane_a(("cT", b), transposes([C0[:, b, t, :] for t in range(NT)]))

            def y_b(b):
                pe.wait_ge(a_free, LA["cT", b] + 1)

                def emit(bank):
                    for t in range(NT):
                        ins = mm(bank[:, P * t:P * t + P], C0T[:, b, P * t:P * t + P], wo0s[:])
                    return ins
                lane_v(("yB", b), emit)

            input0(0)
            queries0(0)
            scores0(0)
            for tt in range(TILES):
                if tt + 1 < TILES:
                    scores0(tt + 1)
                turn0(tt)
                if tt:
                    weigh0(tt - 1)
                for kind, b in between0(tt):
                    if kind == "cT":
                        c_t(b)
                    elif kind == "x":
                        input0(b)
                    elif kind == "q":
                        queries0(b)
                    elif kind == "y":
                        y_b(b)
                    elif kind == "media":
                        pe.wait_ge(x_ready, LN["media", 0] + 1)
                        lane_a(("mediaT",), transposes([ctxn[:, b, :] for b in range(B)], rows=CK))
                    elif kind == "xC":
                        input_c(b)
                    elif kind == "route":
                        route(b)
            input_c(B - 2)
            weigh0(TILES - 1)
            c_t(B - 1)
            pe.wait_ge(moe_in, N_MOE)

            def up(e_all):
                b, e = divmod(e_all, EXPERTS)
                if b == 0:
                    pe.wait_ge(uplo_ready, e + 1)
                if e == 0:
                    pe.wait_ge(xlo_ready, b + 1)

                parts = XHI[:, b % 2, :], XLO[:, b, :]
                for k in range(HB):
                    n = HB * e_all + k
                    if n >= 2:
                        pe.wait_ge(silu_ready, n - 1)
                    product(PS[:, n % 2, :], UPHI[:, 0, HB * e + k, :], UPLO[:, 0, HB * e + k, :], *parts).then_inc(g_ready, 1)
                    if n >= 2:
                        pe.wait_ge(h_ready, n - 1)
                    product(PS[:, 2 + n % 2, :], UPHI[:, 1, HB * e + k, :], UPLO[:, 1, HB * e + k, :], *parts).then_inc(u_ready, 1)

            def down(e_all):
                b, e = divmod(e_all, EXPERTS)
                pe.wait_ge(h_ready, HB * (e_all + 1))

                def emit(bank):
                    for t in range(NT):
                        for k in range(HB):
                            ins = mm(bank[:, P * t:P * t + P], HX[:, e_all % 3, k, P * t:P * t + P], wdT[:, HB * e + k, :],
                                     start=k == 0, stop=k == HB - 1)
                    return ins
                lane_v(("down", b, e), emit)

            def bias_row():
                pe.wait_ge(bv1_ready, 1)
                pe.wait_ge(perc_in, N_PERC)

                def emit(bank):
                    for c in range(NHP):
                        ins = mm(bank[:, 0:D], bv1b[:, c, :], wout1s[:, c, :], start=c == 0, stop=c == NHP - 1)
                    return ins
                lane_v(("cb1",), emit)

            pe.wait_ge(s0_sub, TILES)
            up(0)
            y_b(B - 1)
            route(B - 2)
            for e_all in range(B * EXPERTS):
                if e_all + 1 < B * EXPERTS:
                    up(e_all + 1)
                down(e_all)
                if e_all == LAST_ROUTER:
                    input_c(B - 1)
                    route(B - 1)
                if e_all == BIAS_ROW:
                    bias_row()
            pe.wait_ge(silu_ready, B * EXPERTS * HB)
            for b in range(B):
                pe.wait_ge(x_ready, LN["C", b] + 1)
                lane_a(("xT", "D", b), transposes(tiles_of(xtile("C", b))))
            for b in range(B):
                pe.wait_ge(a_free, LA["xT", "D", b] + 1)
                for t in range(NT):
                    if b:
                        pe.wait_ge(vx_ready, NT * (b - 1) + t + 1)
                    mm(PS[:, t, 0:3 * D], XT[:, b, P * t:P * t + P], wqkvT[:].rearrange("p k n -> p (k n)")).then_inc(qkv_ready, 1)
            for b in range(B):
                pe.wait_ge(act_seq, 2 * B + b + 1)
                lane_a(("qT", b), transposes([QK[:, b, t, 0:D] for t in range(NT)]))

                def kv(bank):
                    for t in range(NT):
                        ins = mm(bank[:, 0:D + 1], QK[:, b, t, D:2 * D], VXv[:, b, t, :], start=t == 0, stop=t == NT - 1)
                    return ins
                lane_v(("kv", b), kv)
            for b in range(B):
                pe.wait_ge(a_free, LA["qT", b] + 1)
                pe.wait_ge(kvb_ready, b + 1)
                for h in range(2):
                    def emit(bank):
                        for t in range(2):
                            tt = 2 * h + t
                            ins = mm(bank[:, (D + NH) * t:(D + NH) * (t + 1)], QTD[:, b, P * tt:P * tt + P], KVB[:, b, :])
                        return ins
                    lane_v(("oD", b, h), emit)
            for b in range(B):
                pe.wait_ge(x_ready, LN["lat", b] + 1)
                lane_a(("latT", b), transposes(tiles_of(LAT[:, b])))
            pe.wait_ge(v_free, LV["oD", B - 1, 1] + 1)
            pe.wait_ge(vx_ready, TILES)
            pe.wait_ge(bvb_ready, N_E_OPERANDS)
            pe.wait_ge(a_free, LA["latT", B - 1] + 1)
            pe.wait_ge(wide_lo, 5)

            def s_wide(p, slot):
                g = SLOTS * p + slot
                h, j = divmod(slot, KB)
                r, rows = p % 3, min(P, KEYS - P * j)
                if slot == 0:
                    pe.wait_ge(c_in[r], 32 * (p // 3 + 1))
                if g >= 2:
                    pe.wait_ge(pw_ready, g - 1)
                dst = PS[0:rows, g % 2, :]
                mm(dst, KA[r][h][:, P * j:P * j + rows], QA[r][h][:], stop=False)
                mm(dst, KBt[r][h][:, P * j:P * j + rows], QB[r][h][:], start=False).then_inc(sw_ready, 1)

            def pv(g):
                p, slot = divmod(g, SLOTS)
                h, j = divmod(slot, KB)
                b, hp = divmod(p, NHP)
                head = 2 * p + h
                rows = min(P, KEYS - P * j)
                pe.wait_ge(pw_ready, g + 1)
                if j == 0 and head >= 2:
                    pe.wait_ge(on_ready, head - 1)
                if j == 0 and hp == 0 and h == 0:
                    pe.wait_ge(pj_free, PJ["V", b, 2 * KB - 1] + 1)
                for t in range(NT):
                    ins = mm(PS[:, 4 + head % 2, (DW + 1) * t:(DW + 1) * (t + 1)], PX[0:rows, g % 4, P * t:P * t + P],
                             VXA[0:rows, b % 2, j, 2 * hp + h, :], start=j == 0 and t == 0, stop=j == KB - 1, skip_group_check=True)
                ins.then_inc(pv_ready, 1)

            def max_unit(p, u):
                h, m = divmod(u, 5)
                g, r = 10 * p + u, p % 3
                if u == 0:
                    pe.wait_ge(hi_ready, 12 * (p + 1))
                    pe.wait_ge(pj_free, PJ["Kt", p] + 1)
                if g >= 2:
                    pe.wait_ge(mu_free, g - 1)
                if m < NT:
                    mm(PS[:, 2 + g % 2, :], QA[r][h][:, P * m:P * m + P], KA[r][h][:, 0:S]).then_inc(mu_full, 1)
                else:
                    w = KEYS_PAD - S
                    for t in range(NT):
                        ins = mm(PS[:, 2 + g % 2, w * t:w * t + w], QA[r][h][:, P * t:P * t + P], KA[r][h][:, S:KEYS_PAD])
                    ins.then_inc(mu_full, 1)

            def task(key):
                n = PJ[key]
                if n >= 2:
                    pe.wait_ge(pj_free, n - 1)
                bank = PS[:, 6 + n % 2, :]
                kind = key[0]
                if kind in ("Q", "K", "Kt"):
                    b, hp = divmod(key[1], NHP)
                    pe.wait_ge(latlo_ready, b + 1)
                    cols = slice(P * hp, P * hp + P)
                    if kind == "Q":
                        ins = product(bank, WQHI[:, cols], WQLO[:, cols], LATHI[:, b, :], LATLO[:, b, :])
                    elif kind == "K":
                        ins = product(bank, WKVHI[:, cols], WKVLO[:, cols], LATHI[:, b, :], LATLO[:, b, :])
                    else:
                        ins = product(bank[:, 0:KEYS_PAD - S], WKVHI[:, cols], WKVLO[:, cols], MEDHI[:, b, :], MEDLO[:, b, :])
                elif kind == "V":
                    _, b, u = key
                    pe.wait_ge(latlo_ready, b + 1)
                    pe.wait_ge(wide_lo, 7)
                    j, half = divmod(u, 2)
                    cols = slice(INNER + 512 * half, INNER + 512 * half + 512)
                    rows = min(P, KEYS - P * j)
                    hi, lo = (LATHI[:, b, P * j:P * j + P], LATLO[:, b, P * j:P * j + P]) if j < NT else (MEDHI[:, b, 0:CK], MEDLO[:, b, 0:CK])
                    ins = product(bank[0:rows, :], hi, lo, WKVHI[:, cols], WKVLO[:, cols])
                elif kind == "c":
                    p = key[1]
                    pe.wait_ge(cm_ready, 2 * (p + 1))
                    ins = pe.transpose(bank[0:2 * NT, 0:P], cmx[:, p % 2].rearrange("p h t -> p (h t)"), ident[:])
                elif kind == "oT":
                    p = key[1]
                    pe.wait_ge(on_ready, 2 * (p + 1))
                    for t in range(NT):
                        ins = pe.transpose(bank[:, P * t:P * t + P], CT[:, p % 2, t, :], ident[:])
                else:
                    b = key[1]
                    pe.wait_ge(pj_free, PJ["oT", NHP * b + NHP - 1] + 1)
                    for t in range(NT):
                        for c in range(NHP):
                            ins = mm(bank[:, P * t:P * t + P], OT[:, c, P * t:P * t + P], wout1s[:, c, :], start=c == 0, stop=c == NHP - 1)
                ins.then_inc(pj_full, 1)

            for key in PROLOGUE:
                if key[0] == "max":
                    max_unit(0, key[1])
                else:
                    task(key)
            for p in range(STEPS):
                tasks = step_tasks(p)
                for slot in range(SLOTS):
                    s_wide(p, slot)
                    if p + 1 < PAIRS:
                        for u in MAX_UNITS.get(slot, []):
                            max_unit(p + 1, u)
                    if SLOTS * p + slot:
                        pv(SLOTS * p + slot - 1)
                    for key in tasks.get(slot, []):
                        task(key)
            pv(SLOTS * STEPS - 1)
            for key in EPILOGUE:
                task(key)
            pe.wait_ge(cn_in, N_CN)
            pe.wait_ge(pj_free, len(PJ))
            pe.wait_ge(bvb_ready, N_POOL)
            for b in range(B):
                pe.wait_ge(x_ready, LN["E", b] + 1)
                lane_a(("xT", "F", b), transposes(tiles_of(xtile("E", b))))
            global_layers = ((gn1, gsum, 64), (gn2, gact1, 32), (gn3, gact2, P))

            def back(b):
                pe.wait_ge(state_ready, B * (CYCLES - 1) + b + 1)
                lane_v(("back", b), transposes([FS[:, b, P * t:P * t + P] for t in range(NT)]))

            for c in range(CYCLES):
                for layer, (w, src) in enumerate(((cn1, FS), (cn2, H1), (cn3, H2), (cn4, H3))):
                    for b in range(B):
                        if layer == 0 and c:
                            pe.wait_ge(state_ready, B * (c - 1) + b + 1)
                        if layer:
                            pe.wait_ge(a_free, LA["cn", c, layer - 1, b] + 1)
                        lane_a(("cn", c, layer, b), lambda bank: mm(bank, w[:], src[:, b, :]))
                        if layer == 3:
                            if c == CYCLES - 1 and b >= 2:
                                back(b - 2)
                            lane_v(("twist", c, b), lambda bank: mm(bank, twist[:], FS[:, b, :]))
                    if c == 0 and layer < 3:
                        gw, gsrc, rows = global_layers[layer]
                        if layer == 0:
                            pe.wait_ge(gs_ready, B)
                        else:
                            pe.wait_ge(a_free, LA["gn", layer - 1] + 1)
                        lane_a(("gn", layer), lambda bank: mm(bank[0:rows, 0:B], gw[:], gsrc[:]))
            for b in range(B - 2, B):
                back(b)


_INS = ["x", "ctx_1024", "L0_xattn_Wq", "L0_xattn_bq", "L0_xattn_Wk", "L0_xattn_bk", "L0_xattn_Wv", "L0_xattn_bv",
        "L0_xattn_Wo", "L0_xattn_bo", "L0_ffn_w_router", "L0_ffn_Wg", "L0_ffn_Wu", "L0_ffn_Wd", "L0_ffn_sg",
        "L0_ffn_su", "L0_ffn_sd", "L1_attn_W_qkv", "L1_xattn_ln_media_w", "L1_xattn_ln_media_b", "L1_xattn_ln_lat_w",
        "L1_xattn_ln_lat_b", "L1_xattn_Wq", "L1_xattn_bq", "L1_xattn_Wkv", "L1_xattn_bkv", "L1_xattn_Wout",
        "L1_xattn_bout", "L1_ffn_cn_w1", "L1_ffn_cn_b1", "L1_ffn_cn_w2", "L1_ffn_cn_b2", "L1_ffn_cn_w3",
        "L1_ffn_cn_b3", "L1_ffn_cn_w4", "L1_ffn_cn_b4", "L1_ffn_gc_w1", "L1_ffn_gc_b1", "L1_ffn_gc_w2",
        "L1_ffn_gc_b2", "L1_ffn_gc_w3", "L1_ffn_gc_b3", "L1_ffn_adaptive_range"]


def kernel(**inputs):
    import numpy as np
    import concourse.bacc as bacc
    from concourse.bass_utils import run_bass_kernel_spmd

    nc = bacc.Bacc("TRN2", target_bir_lowering=False, num_devices=1)
    arrays, args = {}, []
    def blocks(w):
        return w.reshape(-1, P, w.shape[-1]).transpose(1, 0, 2)

    layout = {
        "L0_ffn_Wg": lambda w: w.transpose(2, 0, 1).reshape(D, -1), "L0_ffn_Wu": lambda w: w.transpose(2, 0, 1).reshape(D, -1),
        "L0_ffn_sg": lambda w: w.T, "L0_ffn_su": lambda w: w.T,
        "L0_ffn_Wd": lambda w: blocks(w.transpose(0, 2, 1).reshape(-1, D)).reshape(P, -1),
        "L0_ffn_sd": lambda w: blocks(w.T).reshape(P, -1),
        "L0_ffn_w_router": lambda w: w.T, "L1_attn_W_qkv": lambda w: w.T,
        "L1_xattn_bq": lambda w: w.reshape(-1, P).T, "L1_xattn_bkv": lambda w: w.reshape(-1, P).T,
        "L1_xattn_Wout": blocks,
    }
    for name in _INS:
        a = np.asarray(inputs[name])
        a = np.ascontiguousarray(layout[name](a) if name in layout else a)
        arrays[f"in_{name}"] = a
        args.append(nc.dram_tensor(f"in_{name}", a.shape, mybir.dt.from_np(a.dtype), kind="ExternalInput").ap())
    args.append(nc.dram_tensor("out", (B, S, D), F32, kind="ExternalOutput").ap())
    decoder(nc, *args)
    r = run_bass_kernel_spmd(nc, [arrays], core_ids=[0])
    return r.results[0]["out"]
```

```python
from contextlib import ExitStack

import concourse.bass as bass
from concourse import mybir

F32 = mybir.dt.float32
F32R = mybir.dt.float32r
U32 = mybir.dt.uint32
ACT = mybir.ActivationFunctionType
ALU = mybir.AluOpType
AX = mybir.AxisListType

P = 128
B, S, D = 4, 512, 128
NT = S // P
TILES = B * NT
CK = 77
NH = 16
DH = D // NH
DW = 64
INNER = NH * DW
NHP = NH // 2
PAIRS = B * NHP
KEYS = S + CK
KEYS_PAD = KEYS + 1
KB = (KEYS + P - 1) // P
E, HID = 8, 256
EXPERTS = E + 1
HB = HID // P
CYCLES = 3
LN_EPS = 1e-5
COS_EPS = 1e-8
L2_EPS = 1e-12
KSUM_EPS = 1e-6
LN_SCALE = 65536.0
SCALE_N = DH ** -0.5
SCALE_W = DW ** -0.5

D_NORMS = [("D", 0), ("D", 1), ("lat", 0), ("D", 2), ("lat", 1), ("D", 3), ("lat", 2), ("lat", 3)]
LN_KEYS = ([("A", b) for b in range(B)] + [("media", 0)] + [("B", b) for b in range(B)]
           + [("C", b) for b in range(B)] + D_NORMS
           + [("E", b) for b in range(B)] + [("F", b) for b in range(B)])
LN = {key: n for n, key in enumerate(LN_KEYS)}


def between0(tt):
    b, t = divmod(tt, NT)
    work = []
    if t == 1 and b:
        work += [("cT", b - 1)]
    if t == 1 and b + 1 < B:
        work += [("x", b + 1)]
    if t == 2 and b + 1 < B:
        work += [("q", b + 1)]
    if t == 2 and b:
        work += [("y", b - 1)]
    if tt == 3:
        work += [("media", 0)]
    if t == 0 and b >= 2:
        work += [("xC", b - 2)]
    if t == 1 and b >= 2:
        work += [("route", b - 2)]
    return work


LAST_ROUTER = 3
BIAS_ROW = 5
D_INPUT, D_QKV, D_SUMS, D_NORMED = 1, 2, 3, 11


LAST_INPUT = (0, 0, B - 1)


def coupling_groups(c):
    return [range(B)] if c < CYCLES - 1 else [range(2), range(2, B)]


def early_batch(e_all, after):
    b, rest = divmod(e_all - after - EXPERTS + 1, EXPERTS)
    return b if rest == 0 and 0 <= b < B - 1 else None


def lane_a_tasks():
    t = [("xT", "A", b) for b in range(B)] + [("rb", b) for b in range(B)]
    t += [("ctxT",), ("xT", "B", 0), ("qT0", 0)]
    for tt in range(TILES):
        t += [("pT", tt, 0), ("pT", tt, 2)]
        for kind, b in between0(tt):
            t += {"cT": [("cT", b)], "x": [("xT", "B", b)], "q": [("qT0", b)], "media": [("mediaT",)], "xC": [("xT", "C", b)]}.get(kind, [])
    t += [("xT", "C", B - 2), ("cT", B - 1), ("xT", "C", B - 1)]
    for b in range(B - 1):
        t += [("xT", "D", b)] + [("qkv", b, i) for i in range(NT)]
    t += [("qT", 0), ("qT", 1), ("xT", "D", B - 1)] + [("qkv", B - 1, i) for i in range(NT)] + [("qT", 2), ("latT", 0), ("qT", 3)]
    t += [("latT", b) for b in range(1, B)]
    t += [("xT", "F", b) for b in range(B - 1)]
    for c in range(CYCLES):
        for group in coupling_groups(c):
            for layer in range(4):
                for b in group:
                    if (c, layer, b) == LAST_INPUT:
                        t += [("xT", "F", B - 1)]
                    t += [("cn", c, layer, b)]
                if c == 0 and layer < 3:
                    t += [("gn", layer)]
    return {key: n for n, key in enumerate(t)}


def lane_v_tasks():
    t = [("oA", 0), ("oA", 1), ("k0",), ("v0",), ("cb0",), ("oA", 2), ("oA", 3)]
    for tt in range(TILES):
        t += [("pT", tt, 1), ("pT", tt, 3)]
        for kind, b in between0(tt):
            t += {"y": [("yB", b)], "route": [("router", b)]}.get(kind, [])
    t += [("yB", B - 1), ("router", B - 2)]
    for e_all in range(B * EXPERTS):
        t += [("down", e_all // EXPERTS, e_all % EXPERTS)]
        if e_all == LAST_ROUTER:
            t += [("router", B - 1)]
        if e_all == BIAS_ROW:
            t += [("cb1",)]
    for kind, b in (("kv", 0), ("kv", 1), ("oD", 0), ("kv", 2), ("oD", 1), ("oD", 2), ("kv", 3), ("oD", 3)):
        t += [("kv", b)] if kind == "kv" else [("oD", b, h) for h in range(2)]
    for c in range(CYCLES):
        for b in range(B):
            if c == CYCLES - 1 and b == 2:
                t += [("back", 0), ("back", 1)]
            t += [("twist", c, b)]
    t += [("back", b) for b in range(B - 2, B)]
    return {key: n for n, key in enumerate(t)}


LA, LV = lane_a_tasks(), lane_v_tasks()

SLOTS = 2 * KB
STEPS = PAIRS
MAX_UNITS = {0: [0], 1: [1, 2], 2: [3, 4], 3: [5, 6], 4: [7], 5: [8, 9]}


def step_tasks(p):
    t = {}
    if p + 2 < PAIRS:
        t[0], t[3], t[5] = [("Q", p + 2)], [("K", p + 2)], [("Kt", p + 2)]
    if p + 1 < PAIRS:
        t[6] = [("c", p + 1)]
    b, hp = divmod(p, NHP)
    if b + 1 < B and hp < KB:
        t[2] = [("V", b + 1, 2 * hp)]
        t[7] = [("V", b + 1, 2 * hp + 1)]
    if p:
        t[8] = [("oT", p - 1)]
    if b and hp == 0:
        t[9] = [("yE", b - 1)]
    return t


def splits(tasks, slot):
    now = [(key, 0) for key in tasks.get(slot, []) if key[0] in ("Q", "K", "Kt")]
    return ([(key, 1) for key in tasks.get(slot - 1, []) if key[0] in ("Q", "K")] + now
            + [(key, 1) for key, _ in now if key[0] == "Kt"])


PROLOGUE = ([("norm", 0), ("Q", 0), ("K", 0), ("Kt", 0), ("latT", 1), ("norm", 1), ("norm", 2), ("V", 0, 0), ("V", 0, 1),
             ("max", 0), ("max", 1), ("norm", 3), ("V", 0, 2), ("max", 2), ("max", 3), ("norm", 4), ("V", 0, 3), ("max", 4),
             ("max", 5), ("norm", 5), ("latT", 2), ("V", 0, 4), ("max", 6), ("max", 7), ("V", 0, 5), ("max", 8),
             ("max", 9), ("c", 0), ("Q", 1), ("V", 0, 6), ("K", 1), ("latT", 3), ("V", 0, 7), ("Kt", 1), ("V", 0, 8), ("V", 0, 9)])
EPILOGUE = [("oT", PAIRS - 1), ("yE", B - 1)]


def proj_tasks():
    t = [key for key in PROLOGUE if key[0] not in ("max", "norm", "latT")]
    for p in range(STEPS):
        for slot in range(SLOTS):
            t += step_tasks(p).get(slot, [])
    return {key: n for n, key in enumerate(t + EPILOGUE)}


PJ = proj_tasks()


def decoder(nc, x, ctx, wq0, bq0, wk0, bk0, wv0, bv0, wo0, bo0, w_router, w_g, w_u, w_d, s_g, s_u, s_d, w_qkv,
            med_w, med_b, lat_w, lat_b, wq1, bq1, wkv1, bkv1, wout1, bout1,
            cw1, cb1_, cw2, cb2_, cw3, cb3_, cw4, cb4_, gw1, gb1, gw2, gb2, gw3, gb3, arange, out):
    es = ExitStack()
    with es:
        def sb(name, shape, dt=F32):
            return es.enter_context(nc.sbuf_tensor(name, shape, dt))

        def sem(name):
            return es.enter_context(nc.semaphore(name))

        X_EVEN = sb("X_EVEN", [P, TILES, D])
        x_odd_at = nc.sbuf_base
        X_ODD = sb("X_ODD", [P, TILES, D])
        XS = {"0": X_EVEN, "A": X_ODD, "B": X_EVEN, "C": X_ODD, "D": X_EVEN, "E": X_ODD}
        xt_at = nc.sbuf_base
        XT = sb("XT", [P, B, S])
        Y = sb("Y", [P, B, NT, D])
        big_at = nc.sbuf_base
        BIG = sb("BIG", [P, 6656])
        reg_at = nc.sbuf_base
        REG = sb("REG", [P, 6400])
        wq1_at = nc.sbuf_base
        wq1s = sb("wq1s", [P, INNER])
        medt_at = nc.sbuf_base
        MEDT = sb("MEDT", [P, B, KEYS_PAD - S])
        st = sb("st", [P, 2, NT, 6])
        mv = sb("mv", [P, len(LN), NT, 2])
        ve = sb("ve", [P, len(LN), NT])
        rs = sb("rs", [P, len(LN), NT])
        ident = sb("ident", [P, P])
        ones = sb("ones", [P, P])
        half_neg = sb("half_neg", [P, NT])
        lnb = sb("lnb", [P, 1])
        hmask = sb("hmask", [P, NH])
        hmask_s = sb("hmask_s", [P, NH])
        iota = sb("iota", [P, E])
        twist = sb("twist", [P, P])
        ctx_sb = sb("ctx_sb", [CK, B, D])
        wq0s, wk0s, wv0s, wo0s = (sb(n, [P, P]) for n in ("wq0s", "wk0s", "wv0s", "wo0s"))
        b0s = sb("b0s", [P, 3])
        bo0s = sb("bo0s", [P, D])
        wqkvT = sb("wqkvT", [P, 3, P])
        wrT = sb("wrT", [P, E])
        lnw = sb("lnw", [P, 4])
        wout1s = sb("wout1s", [P, INNER // P, D])
        b1s = sb("b1s", [P, 3, INNER // P])
        bout1s = sb("bout1s", [P, D])
        CB0, CB1 = bo0s, bout1s
        bv0b = sb("bv0b", [P, P])
        cn1, cn2, cn3, cn4 = (sb(n, [P, P]) for n in ("cn1", "cn2", "cn3", "cn4"))
        gn1, gn2, gn3 = sb("gn1", [P, 64]), sb("gn2", [64, 32]), sb("gn3", [32, P])
        cnb, gnb = sb("cnb", [P, 4]), sb("gnb", [P, 3])
        w4col = sb("w4col", [32, 2])
        ar1 = sb("ar1", [P, 1])
        ss = sb("ss", [P, TILES])
        rn = sb("rn", [P, TILES])
        rsum = sb("rsum", [P, TILES])
        rinv = sb("rinv", [P, TILES])
        v0x = sb("v0x", [CK, B, NH, DH + 1])
        mx0 = sb("mx0", [P, 2, NH])
        r0 = sb("r0", [P, 2, NH])
        lg = sb("lg", [P, B, NT, E])
        top = sb("top", [P, B, NT, E])
        topi = sb("topi", [P, B, NT, E], U32)
        topf = sb("topf", [P, B, NT, 2])
        dl = sb("dl", [P, B, NT])
        etop = sb("etop", [P, B, NT])
        wtop = sb("wtop", [P, B, 2, NT])
        eq = sb("eq", [P, 2, NT, E])
        comb = sb("comb", [P, B, NT, E])
        kse = sb("kse", [P, B])
        gsum = sb("gsum", [P, B])
        gact1, gact2 = sb("gact1", [64, B]), sb("gact2", [32, B])
        gth = sb("gth", [P, B])
        cA, cB = sb("cA", [P, 1]), sb("cB", [P, B])
        cbias = sb("cbias", [P, 2])
        QA = [[sb(f"QA{r}{h}", [P, S], F32R) for h in range(2)] for r in range(3)]
        KA = [[sb(f"KA{r}{h}", [P, KEYS_PAD], F32R) for h in range(2)] for r in range(3)]
        QB = [[sb(f"QB{r}{h}", [P, S], F32R) for h in range(2)] for r in range(3)]
        KBt = [[sb(f"KB{r}{h}", [P, KEYS_PAD], F32R) for h in range(2)] for r in range(3)]
        mxm = sb("mxm", [P, 2, 2, NT])
        mxt = sb("mxt", [P, 2, 2, NT])
        cmx = sb("cmx", [P, 2, 2, NT])
        crow = sb("crow", [2 * NT, 2, P])
        rden = sb("rden", [P, 2, NT])

        vxa_at = nc.sbuf_base
        VXA = sb("VXA", [P, 2, KB, NH, DW + 1])

        NW = HB * EXPERTS * D
        vflat = VXA[:].rearrange("p a j h d -> p (a j h d)")
        up_weights = vflat[:, 0:2 * NW].rearrange("p (a k d) -> p a k d", a=2, d=P)
        wgT, wuT, wdT = (vflat[:, NW * n:NW * n + NW].rearrange("p (k d) -> p k d", d=P) for n in range(3))

        def over(name, at, shape):
            return nc.alloc_sbuf_tensor_at(name, shape, F32R, offset=at)

        UPHI = over("UPHI", reg_at, [P, 2, EXPERTS * HB, P])
        UPLO = over("UPLO", vxa_at, [P, 2, EXPERTS * HB, P])
        XHI = over("XHI", reg_at + 4 * (6400 - 2 * S), [P, 2, S])
        XLO = over("XLO", xt_at, [P, B, S])
        WQHI, WQLO = over("WQHI", big_at + 4 * 5184, [P, INNER]), over("WQLO", wq1_at, [P, INNER])
        MEDHI, MEDLO = over("MEDHI", big_at + 4 * 6208, [P, B, KEYS_PAD - S]), over("MEDLO", medt_at, [P, B, KEYS_PAD - S])
        WKVHI, WKVLO = over("WKVHI", big_at + 4 * 3072, [P, 2 * INNER]), over("WKVLO", reg_at + 4 * (6400 - 2 * INNER), [P, 2 * INNER])
        LATHI, LATLO = over("LATHI", x_odd_at, [P, B, S]), over("LATLO", xt_at, [P, B, S])
        DG = Y[:].rearrange("p b t d -> p b (t d)")
        RBv = BIG[:, 0:2048].rearrange("p (b n) -> p b n", b=B)
        EX = BIG[:, 2048:6144].rearrange("p (r t n) -> p r t n", r=2, t=NT)
        GX = REG[:, 0:1024].rearrange("p (r n) -> p r n", r=2)
        SM = BIG[:, 0:2 * NH * CK].rearrange("p (r n) -> p r n", r=2)
        PT0 = BIG[0:CK, 2560:2560 + 2 * NH * P].rearrange("p (r h n) -> p r h n", r=2, h=NH)
        QT0 = vflat[:, 3 * NW:3 * NW + 2048].rearrange("p (b n) -> p b n", b=B)
        ctxT, k0T = (vflat[:, 3 * NW + n:3 * NW + n + B * CK].rearrange("p (b k) -> p b k", b=B) for n in (2048, 2048 + B * CK))
        ctxn = vflat[0:CK, 3 * NW + 2048 + 2 * B * CK:3 * NW + 2048 + 2 * B * CK + B * D].rearrange("p (b d) -> p b d", b=B)
        KBD = REG[:, 0:B * NH * CK].rearrange("p (b h k) -> p b h k", b=B, h=NH)
        bv1b = BIG[:, 5120:5120 + NHP * P].rearrange("p (c n) -> p c n", c=NHP)
        C0, C0T = Y, XT
        SG = BIG[:, 0:2048].rearrange("p (r n) -> p r n", r=4)
        HX = BIG[:, 2048:5120].rearrange("p (r k n) -> p r k n", r=3, k=HB)
        QD = X_EVEN[:].rearrange("p (b t) n -> p b t n", b=B)
        KD = Y
        VXv = vflat[:, 3 * NW:3 * NW + B * NT * (D + 1)].rearrange("p (b t n) -> p b t n", b=B, t=NT)
        SQ = vflat[:, 3 * NW + B * NT * (D + 1):3 * NW + B * NT * (D + 1) + 2 * NT * D].rearrange("p (a t n) -> p a t n", a=2, t=NT)
        NSQ = 2 * NT * NH
        sums_at = 3 * NW + B * NT * (D + 1) + 2 * NT * D
        SSQ = [vflat[:, sums_at + NSQ * b:sums_at + NSQ * b + NSQ] for b in range(B - 1)] + [BIG[:, 6520:6520 + NSQ]]
        KVB = BIG[:, 4096:4096 + B * (D + NH)].rearrange("p (b n) -> p b n", b=B)
        QTD = XT
        LAT, LATT = Y, XT
        PX = BIG[:, 0:2048].rearrange("p (r n) -> p r n", r=4)
        CT = BIG[:, 2048:2048 + 2 * NT * P].rearrange("p (r t n) -> p r t n", r=2, t=NT)
        OT = REG[:, 0:NHP * S].rearrange("p (c n) -> p c n", c=NHP)
        wkv1s = REG[:, 6400 - 2 * INNER:6400]
        FS = XT
        H1 = BIG[:, 0:2048].rearrange("p (b n) -> p b n", b=B)
        H2 = BIG[:, 2048:4096].rearrange("p (b n) -> p b n", b=B)
        H3 = BIG[:, 4096:6144].rearrange("p (b n) -> p b n", b=B)
        TH = REG[:, 0:2048].rearrange("p (b n) -> p b n", b=B)
        CP = REG[:, 2048:4096].rearrange("p (b n) -> p b n", b=B)

        PS = es.enter_context(nc.psum_tensor("PS", [P, 8, 512], F32))

        def bank_a(n):
            return PS[:, 4 + n % 2, :]

        def bank_v(n):
            return PS[:, 6 + n % 2, :]

        x_in = [sem(f"x_in{b}") for b in range(B)]
        ctx_in, w0_in, moe_in, qkv_in, perc_in, cn_in, wkv_in = (sem(n) for n in ("ctx_in", "w0_in", "moe_in", "qkv_in", "perc_in", "cn_in", "wkv_in"))
        consts = sem("consts")
        a_full, a_free, v_full, v_free = (sem(n) for n in ("a_full", "a_free", "v_full", "v_free"))
        var_ready, rstd_ready, x_ready = sem("var_ready"), sem("rstd_ready"), sem("x_ready")
        dve_seq, act_seq = sem("dve_seq"), sem("act_seq")
        sq_ready, ss_ready, rn_ready, diag_ready = (sem(n) for n in ("sq_ready", "ss_ready", "rn_ready", "diag_ready"))
        dots_ready, sim_ready, exp_ready = sem("dots_ready"), sem("sim_ready"), sem("exp_ready")
        xr_ready = sem("xr_ready")
        wide_hi, wide_lo, lathi_ready, latlo_ready, med_ready = (sem(n) for n in ("wide_hi", "wide_lo", "lathi_ready", "latlo_ready", "med_ready"))
        uphi_ready, uplo_ready, xhi_ready, xlo_ready = (sem(n) for n in ("uphi_ready", "uplo_ready", "xhi_ready", "xlo_ready"))
        kbd_ready, kbd_more, bv1_ready, setup_done = (sem(n) for n in ("kbd_ready", "kbd_more", "bv1_ready", "setup_done"))
        s0_ready, s0_sub, p0_ready, pv0_full, pv0_free = (sem(n) for n in ("s0_ready", "s0_sub", "p0_ready", "pv0_full", "pv0_free"))
        dl_ready, etop_ready = sem("dl_ready"), sem("etop_ready")
        g_ready, u_ready, silu_ready, h_ready = (sem(n) for n in ("g_ready", "u_ready", "silu_ready", "h_ready"))
        vx_ones, sqq_ready, ssq_ready, lnorm_ready, pow_ready, qkn_ready, spe_ready, sp_ready, kvb_ready = (
            sem(n) for n in ("vx_ones", "sqq_ready", "ssq_ready", "lnorm_ready", "pow_ready", "qkn_ready", "spe_ready", "sp_ready", "kvb_ready"))
        pj_full, pj_free, hi_ready = (sem(n) for n in ("pj_full", "pj_free", "hi_ready"))
        mu_full, mu_free, cm_ready = (sem(n) for n in ("mu_full", "mu_free", "cm_ready"))
        c_in = [sem(f"c_in{r}") for r in range(3)]
        sw_ready, pw_ready, pv_ready, on_ready = (sem(n) for n in ("sw_ready", "pw_ready", "pv_ready", "on_ready"))
        gs_ready, coef_ready, state_ready, out_sem = (sem(n) for n in ("gs_ready", "coef_ready", "state_ready", "out_sem"))

        block = es.enter_context(nc.Block())

        N_W0, N_MOE, N_QKV, N_PERC, N_CN = 16 * 8, 16 * 6, 16 * 2, 16 * 10, 16 * 15
        WIDE = ([(wq1s[:, 512 * n:512 * n + 512], WQHI[:, 512 * n:512 * n + 512], WQLO[:, 512 * n:512 * n + 512]) for n in range(2)]
                + [(MEDT[:], MEDHI[:], MEDLO[:])]
                + [(wkv1s[:, 512 * n:512 * n + 512], WKVHI[:, 512 * n:512 * n + 512], WKVLO[:, 512 * n:512 * n + 512]) for n in range(4)])
        N_CONST = 19
        N_POOL = 22
        N_E_OPERANDS = 20

        def xtile(k, b):
            return XS[k][:, NT * b:NT * b + NT, :]

        @block.sync
        def _(sp):
            for b in range(B):
                sp.dma_start(XS["0"][:, NT * b:NT * b + NT, :], x[b].rearrange("(t p) d -> p t d", p=P)).then_inc(x_in[b], 16)
            sp.dma_start(ctx_sb[:], ctx.rearrange("b k d -> k b d")).then_inc(ctx_in, 16)
            for dst, src in ((wq0s, wq0), (wk0s, wk0), (wv0s, wv0), (wo0s, wo0)):
                sp.dma_start(dst[:], src).then_inc(w0_in, 16)
            for n, src in enumerate((bq0, bk0, bv0)):
                sp.dma_start(b0s[:, n:n + 1], src.rearrange("(p a) -> p a", a=1)).then_inc(w0_in, 16)
            sp.dma_start(bo0s[:], bo0.partition_broadcast(P)).then_inc(w0_in, 16)
            ne = HB * E * P
            for dst, src, shared in ((wgT, w_g, s_g), (wuT, w_u, s_u), (wdT, w_d, s_d)):
                flat = dst.rearrange("p k d -> p (k d)")
                sp.dma_start(flat[:, 0:ne], src).then_inc(moe_in, 16)
                sp.dma_start(flat[:, ne:], shared).then_inc(moe_in, 16)
            sp.dma_start(wqkvT[:].rearrange("p k d -> p (k d)"), w_qkv).then_inc(qkv_in, 16)
            sp.dma_start(wrT[:], w_router).then_inc(qkv_in, 16)
            for n, src in enumerate((med_w, med_b, lat_w, lat_b)):
                sp.dma_start(lnw[:, n:n + 1], src.rearrange("(p a) -> p a", a=1)).then_inc(perc_in, 16)
            sp.dma_start(wq1s[:], wq1).then_inc(perc_in, 16)
            sp.dma_start(wout1s[:], wout1).then_inc(perc_in, 16)
            sp.dma_start(b1s[:, 0, :], bq1).then_inc(perc_in, 16)
            sp.dma_start(b1s[:, 1, :], bkv1[:, 0:NHP]).then_inc(perc_in, 16)
            sp.dma_start(b1s[:, 2, :], bkv1[:, NHP:2 * NHP]).then_inc(perc_in, 16)
            sp.dma_start(bout1s[:], bout1.partition_broadcast(P)).then_inc(perc_in, 16)
            sp.wait_ge(consts, N_CONST)
            for dst, src in ((cn1, cw1), (cn2, cw2), (cn3, cw3), (gn1, gw1), (gn2, gw2)):
                sp.dma_start(dst[0:src.shape[0], 0:src.shape[1]], src).then_inc(cn_in, 16)
            sp.dma_start(w4col[:, 0:1], cw4).then_inc(cn_in, 16)
            sp.dma_start(w4col[:, 1:2], gw3).then_inc(cn_in, 16)
            for n, src in enumerate((cb1_, cb2_, cb3_)):
                sp.dma_start(cnb[0:src.shape[0], n:n + 1], src.rearrange("(p a) -> p a", a=1)).then_inc(cn_in, 16)
            sp.dma_start(cnb[:, 3:4], cb4_.partition_broadcast(P)).then_inc(cn_in, 16)
            for n, src in enumerate((gb1, gb2)):
                sp.dma_start(gnb[0:src.shape[0], n:n + 1], src.rearrange("(p a) -> p a", a=1)).then_inc(cn_in, 16)
            sp.dma_start(gnb[:, 2:3], gb3.partition_broadcast(P)).then_inc(cn_in, 16)
            sp.dma_start(ar1[:], arange.partition_broadcast(P)).then_inc(cn_in, 16)
            sp.wait_ge(u_ready, B * EXPERTS * HB)
            sp.dma_start(wkv1s, wkv1).then_inc(wkv_in, 16)
            for p in range(PAIRS):
                r = p % 3
                sp.wait_ge(pj_free, PJ["c", p] + 1)
                for h in range(2):
                    row = DW * (1 - h)
                    sp.dma_start(QB[r][h][row:row + 1, :].bitcast(F32).rearrange("a (t n) -> a t n", t=NT),
                                 crow[NT * h:NT * h + NT, p % 2, :]).then_inc(c_in[r], 16)
            for b in range(B):
                sp.wait_ge(x_ready, LN["F", b] + 1)
                sp.dma_start(out[b].rearrange("(t p) d -> p t d", p=P), XS["0"][:, NT * b:NT * b + NT, :]).then_inc(out_sem, 16)
            sp.wait_ge(out_sem, 16 * B)

        @block.gpsimd
        def _(pool):
            pool.memset(ident[:], 0.0).then_inc(consts, 1)
            pool.memset(ones[:], 1.0).then_inc(consts, 1)
            pool.memset(half_neg[:], -0.5).then_inc(consts, 1)
            pool.memset(cnb[:], 0.0).then_inc(consts, 1)
            pool.memset(lnb[:], 0.5 * 11.090354888959125).then_inc(consts, 1)
            for w in (cn2, cn3, cn4):
                pool.memset(w[:], 0.0).then_inc(consts, 1)
            pool.memset(hmask[:], 1.0).then_inc(consts, 1)
            pool.memset(twist[:], 0.0).then_inc(consts, 1)
            pool.memset(v0x[:], 1.0).then_inc(consts, 1)
            pool.iota(topi[:, 0, 0, :], pattern=[[1, E]], base=0, channel_multiplier=0).then_inc(consts, 1)
            pool.wait_ge(consts, 12)
            pool.affine_select(out=ident[:], in_=ident[:], compare_op=ALU.not_equal, fill=1.0, base=0,
                               pattern=[[-1, P]], channel_multiplier=1).then_inc(consts, 1)
            pool.affine_select(out=hmask[:], in_=hmask[:], compare_op=ALU.is_ge, fill=0.0, base=0,
                               pattern=[[-DH, NH]], channel_multiplier=1).then_inc(consts, 1)
            pool.wait_ge(consts, 14)
            pool.affine_select(out=hmask[:], in_=hmask[:], compare_op=ALU.is_ge, fill=0.0, base=DH - 1,
                               pattern=[[DH, NH]], channel_multiplier=-1).then_inc(consts, 1)
            for n, (fill, off) in enumerate(((1.0, -64), (-1.0, -64), (-1.0, 64), (1.0, 64))):
                cols = twist[:, 32 * n:32 * n + 32]
                pool.affine_select(out=cols, in_=cols, compare_op=ALU.not_equal, fill=fill, base=off - 32 * n,
                                   pattern=[[-1, 32]], channel_multiplier=1).then_inc(consts, 1)
            setup = [0]

            def settled(ins):
                setup[0] += 1
                ins.then_inc(setup_done, 1)
                pool.wait_ge(setup_done, setup[0])

            def last_layers():
                pool.wait_ge(cn_in, N_CN)
                settled(pool.tensor_copy(cn4[0:32, :], w4col[:, 0:1].broadcast_to([32, P])))
                settled(pool.tensor_copy(gn3[:], w4col[:, 1:2].broadcast_to([32, P])))

            def rstd(key):
                n = LN[key]
                rows = CK if key[0] == "media" else P
                pool.wait_ge(var_ready, n + 1)
                pool.tensor_tensor(rs[0:rows, n, :], ve[0:rows, n, :], half_neg[0:rows, 0:NT], ALU.pow).then_inc(rstd_ready, 1)

            for b in range(B):
                pool.wait_ge(ss_ready, b + 1)
                pool.tensor_tensor(rn[:, NT * b:NT * b + NT], ss[:, NT * b:NT * b + NT], half_neg[:, 0:NT], ALU.pow).then_inc(rn_ready, 1)
            pool.wait_ge(w0_in, N_W0)
            settled(pool.tensor_copy(bv0b[:], b0s[:, 2:3].broadcast_to([P, P])))
            for r in range(3):
                for h in range(2):
                    lo = DW * (1 - h)
                    settled(pool.memset(QB[r][h][lo:lo + DW, :].bitcast(F32), 0.0))
                    settled(pool.memset(KBt[r][h][lo:lo + DW, :].bitcast(F32), 0.0))
            for r in range(3):
                for h in range(2):
                    lo = DW * (1 - h)
                    settled(pool.memset(KBt[r][h][lo:lo + 1, :].bitcast(F32), 1.0))
            for b in range(B):
                rstd(("A", b))
            rstd(("media", 0))
            pool.wait_ge(v_free, LV["k0",] + 1)
            for b in range(1, B):
                pool.tensor_tensor(KBD[:, b], k0T[:, b, :].unsqueeze(1).broadcast_to([P, NH, CK]),
                                   hmask[:].unsqueeze(2).broadcast_to([P, NH, CK]), ALU.mult).then_inc(kbd_more, 1)
            pool.wait_ge(v_free, LV["cb0",] + 1)
            def residual0(b):
                pool.wait_ge(a_full, LA["xT", "B", b] + 1)
                pool.tensor_tensor(xtile("A", b), xtile("A", b), CB0[:].unsqueeze(1).broadcast_to([P, NT, D]), ALU.add).then_inc(xr_ready, 1)

            for b in range(B - 1):
                residual0(b)
            def split_x(b):
                pool.wait_ge(xhi_ready, b + 1)
                pool.wait_ge(v_full, LV["router", b] + 1)
                pool.tensor_tensor(XLO[:, b, :], XT[:, b, :], XHI[:, b % 2, :].bitcast(F32), ALU.subtract).then_inc(xlo_ready, 1)

            def split_w(e):
                pool.wait_ge(uphi_ready, e + 1)
                blocks = slice(HB * e, HB * e + HB)
                pool.tensor_tensor(UPLO[:, :, blocks, :], up_weights[:, :, blocks, :], UPHI[:, :, blocks, :].bitcast(F32),
                                   ALU.subtract).then_inc(uplo_ready, 1)

            def split_wide(n):
                whole, lead, rest = WIDE[n]
                pool.wait_ge(wide_hi, n + 1)
                pool.tensor_tensor(rest, whole, lead.bitcast(F32), ALU.subtract).then_inc(wide_lo, 1)

            def split_lat(b):
                pool.wait_ge(lathi_ready, b + 1)
                pool.tensor_tensor(LATLO[:, b, :], LATT[:, b, :], LATHI[:, b, :].bitcast(F32), ALU.subtract).then_inc(latlo_ready, 1)

            rstd(("B", 0))
            residual0(B - 1)
            split_x(0)
            rstd(("B", 1))
            split_x(1)
            rstd(("B", 2))
            for e in range(EXPERTS):
                split_w(e)
                if e == 2:
                    rstd(("B", 3))
            def invert(b):
                pool.wait_ge(ssq_ready, b + 1)
                pool.tensor_tensor(SSQ[b], SSQ[b], half_neg[:, 0:1].broadcast_to([P, NSQ]), ALU.pow).then_inc(pow_ready, 1)

            pool.memset(VXv[:, :, :, D:D + 1], 1.0).then_inc(vx_ones, 1)
            for b in range(B):
                rstd(("C", b))
                if b < 2:
                    split_x(b + 2)
                if b < B - 1:
                    invert(b)
                if b == 0:
                    for n in range(3):
                        split_wide(n)
            for key in D_NORMS:
                if key == ("D", 3):
                    split_lat(0)
                    split_wide(3)
                    split_wide(4)
                rstd(key)
                if key == ("D", 3):
                    pool.wait_ge(v_full, LV["kv", B - 1] + 1)
                    settled(pool.memset(VXA[:, :, :, :, DW:DW + 1], 1.0))
                    split_wide(5)
                    split_wide(6)
                elif key == ("lat", 2):
                    split_lat(1)
            for b in range(2, B):
                split_lat(b)
            pool.wait_ge(v_free, LV["cb1",] + 1)
            for b in range(B):
                pool.wait_ge(x_ready, LN["lat", b] + 1)
                pool.tensor_tensor(xtile("D", b), xtile("D", b), CB1[:].unsqueeze(1).broadcast_to([P, NT, D]), ALU.add).then_inc(xr_ready, 1)
            last_layers()

            for p in range(STEPS):
                if p % NHP == 1 and p > 1:
                    rstd(("E", p // NHP - 1))
            rstd(("E", B - 1))
            for b in range(B):
                rstd(("F", b))

        @block.scalar
        def _(act):
            def evac(key, dst, rows=P, cols=512, func=ACT.Copy, shape=None, **kw):
                n = LA[key]
                act.wait_ge(a_full, n + 1)
                src = bank_a(n)[0:rows, 0:cols]
                if shape:
                    src = src.rearrange(shape[0], **shape[1])
                act.activation(dst, src, func, **kw).then_inc(a_free, 1)

            act.wait_ge(consts, N_CONST)
            for b in range(B):
                act.wait_ge(x_in[b], 16)
                for t in range(NT):
                    tt = NT * b + t
                    act.activation(BIG[:, 2048 + 128 * tt:2048 + 128 * tt + 128], XS["0"][:, tt, :], ACT.Square,
                                   accum_out=ss[:, tt:tt + 1]).then_inc(sq_ready, 1)
            for b in range(B):
                evac(("xT", "A", b), XT[:, b, :])
            for b in range(B):
                evac(("rb", b), RBv[:, b, :])
                if b == B - 1:
                    evac(("ctxT",), ctxT[:].rearrange("p b k -> p (b k)"), cols=B * CK)
                for j in range(NT):
                    act.wait_ge(sim_ready, NT * b + j + 1)
                    act.activation(EX[:, b % 2, j, :], EX[:, b % 2, j, :], ACT.Exp,
                                   accum_out=rsum[:, NT * b + j:NT * b + j + 1]).then_inc(exp_ready, 1)

            def input0(b):
                evac(("xT", "B", b), XT[:, b, :])

            def queries0(b):
                evac(("qT0", b), QT0[:, b, :], func=ACT.Identity, bias=b0s[:, 0:1])

            def exp0(tt):
                act.wait_ge(s0_sub, tt + 1)
                act.activation(SM[:, tt % 2, :], SM[:, tt % 2, :], ACT.Exp, scale=SCALE_N).then_inc(p0_ready, 1)

            def exp_top(b):
                act.wait_ge(dl_ready, b + 1)
                act.activation(etop[:, b, :], dl[:, b, :], ACT.Exp).then_inc(etop_ready, 1)

            input0(0)
            def split_x(b):
                act.wait_ge(a_free, LA["xT", "C", b] + 1)
                if b >= 2:
                    act.wait_ge(u_ready, HB * EXPERTS * (b - 1))
                act.activation(XHI[:, b % 2, :], XT[:, b, :], ACT.Copy).then_inc(xhi_ready, 1)

            queries0(0)
            exp0(0)
            for tt in range(TILES):
                if tt >= 2:
                    act.wait_ge(pv0_full, tt - 1)
                evac(("pT", tt, 0), PT0[:, tt % 2, 0:4, :].rearrange("p h n -> p (h n)"), rows=CK)
                evac(("pT", tt, 2), PT0[:, tt % 2, 8:12, :].rearrange("p h n -> p (h n)"), rows=CK)
                if tt + 1 < TILES:
                    exp0(tt + 1)
                for kind, b in between0(tt):
                    if kind == "cT":
                        evac(("cT", b), C0T[:, b, :])
                    elif kind == "x":
                        input0(b)
                    elif kind == "q":
                        queries0(b)
                    elif kind == "media":
                        act.wait_ge(perc_in, N_PERC)
                        evac(("mediaT",), MEDT[:, :, 0:CK], cols=B * CK, shape=("p (b k) -> p b k", {"k": CK}),
                             func=ACT.Identity, scale=lnw[:, 0:1], bias=lnw[:, 1:2])
                        act.wait_ge(a_free, LA["mediaT",] + 1)
                        act.activation(MEDT[:, :, CK:CK + 1], MEDT[:, :, CK - 1:CK], ACT.Copy).then_inc(med_ready, 1)
                    elif kind == "xC":
                        evac(("xT", "C", b), XT[:, b, :])
                        split_x(b)
                for kind, b in between0(tt - 1):
                    if kind == "route":
                        exp_top(b)
            act.wait_ge(moe_in, N_MOE)
            act.wait_ge(s0_ready, TILES)
            for e in range(EXPERTS):
                blocks = slice(HB * e, HB * e + HB)
                act.activation(UPHI[:, :, blocks, :], up_weights[:, :, blocks, :], ACT.Copy).then_inc(uphi_ready, 1)
                if e == 1:
                    evac(("xT", "C", B - 2), XT[:, B - 2, :])
                    evac(("cT", B - 1), C0T[:, B - 1, :])
            def qkv(b):
                for t in range(NT):
                    n = LA["qkv", b, t]
                    act.wait_ge(a_full, n + 1)
                    act.activation(QD[:, b, t, :], bank_a(n)[:, 0:D], ACT.Copy)
                    act.activation(KD[:, b, t, :], bank_a(n)[:, D:2 * D], ACT.Copy)
                    act.activation(VXv[:, b, t, 0:D], bank_a(n)[:, 2 * D:3 * D], ACT.Copy).then_inc(a_free, 1)
                act.wait_ge(a_free, LA["qkv", b, NT - 1] + 1)
                if b:
                    act.wait_ge(ssq_ready, b)
                act.activation(SQ[:, 0], QD[:, b], ACT.Square).then_inc(sqq_ready, 1)
                act.activation(SQ[:, 1], KD[:, b], ACT.Square).then_inc(sqq_ready, 1)

            def split_wide(n):
                act.activation(WIDE[n][1], WIDE[n][0], ACT.Copy).then_inc(wide_hi, 1)

            for n in range(B * EXPERTS * HB):
                act.wait_ge(g_ready, n + 1)
                if n >= 4:
                    act.wait_ge(h_ready, n - 3)
                act.activation(SG[:, n % 4, :], PS[:, n % 2, :], ACT.Silu).then_inc(silu_ready, 1)
                if n == HB:
                    exp_top(B - 2)
                e_all = n // HB - 1
                if n % HB == 1 and early_batch(e_all, D_INPUT) is not None:
                    b = early_batch(e_all, D_INPUT)
                    evac(("xT", "D", b), XT[:, b, :])
                if n % HB == 1 and early_batch(e_all, D_QKV) is not None:
                    qkv(early_batch(e_all, D_QKV))
                if n == HB * EXPERTS:
                    split_x(2)
                if n == HB * EXPERTS + 2:
                    act.wait_ge(v_full, LV["cb1",] + 1)
                    act.wait_ge(med_ready, 1)
                    for m in range(3):
                        split_wide(m)
                if n == 2 * HB * EXPERTS:
                    split_x(3)
                if n == HB * (LAST_ROUTER + 2) - 1:
                    evac(("xT", "C", B - 1), XT[:, B - 1, :])
                    exp_top(B - 1)
            def soft_exp(b):
                act.wait_ge(qkn_ready, b + 1)
                act.activation(QD[:, b], QD[:, b], ACT.Exp).then_inc(spe_ready, 1)
                act.activation(KD[:, b], KD[:, b], ACT.Exp).then_inc(spe_ready, 1)

            def soft_ln(b):
                act.wait_ge(spe_ready, 2 * b + 2)
                act.activation(QD[:, b], QD[:, b], ACT.Ln, bias=ones[:, 0:1])
                act.activation(KD[:, b], KD[:, b], ACT.Ln, bias=ones[:, 0:1]).then_inc(sp_ready, 1)

            def latents(b):
                evac(("latT", b), LATT[:, b, :], func=ACT.Identity, scale=lnw[:, 2:3], bias=lnw[:, 3:4])
                act.wait_ge(a_free, LA["latT", b] + 1)
                act.activation(LATHI[:, b, :], LATT[:, b, :], ACT.Copy).then_inc(lathi_ready, 1)

            for b in range(B - 1):
                soft_exp(b)
            for b in range(B - 1):
                soft_ln(b)
            last = B - 1
            evac(("qT", 0), QTD[:, 0, :])
            evac(("qT", 1), QTD[:, 1, :])
            evac(("xT", "D", last), XT[:, last, :])
            qkv(last)
            act.wait_ge(ssq_ready, B)
            act.activation(SSQ[last], SSQ[last], ACT.Ln, scale=LN_SCALE).then_inc(act_seq, 1)
            act.wait_ge(act_seq, 1)
            act.activation(SSQ[last], SSQ[last], ACT.Exp, scale=-0.5, bias=lnb[:]).then_inc(lnorm_ready, 1)
            evac(("qT", 2), QTD[:, 2, :])
            soft_exp(last)
            soft_ln(last)
            latents(0)
            evac(("qT", last), QTD[:, last, :])
            act.wait_ge(v_full, LV["oD", B - 1, 1] + 1)
            act.wait_ge(wkv_in, 16)
            for n in range(3, 7):
                split_wide(n)
            def hi(key, h):
                kind, p = key
                r, hp = p % 3, p % NHP
                n = PJ[key]
                own, other = slice(DW * h, DW * h + DW), slice(DW * (1 - h), DW * (1 - h) + DW)
                act.wait_ge(pj_full, n + 1)
                if p >= 3 and kind == "Q" and h == 0:
                    act.wait_ge(sw_ready, SLOTS * (p - 2))
                if kind == "Q":
                    dsts, width, bias = (QA[r][h][own, :], QB[r][h][own, :]), S, b1s[own, 0, hp:hp + 1]
                elif kind == "K":
                    dsts, width, bias = (KA[r][h][own, 0:S], KA[r][h][other, 0:S]), S, b1s[own, 1, hp:hp + 1]
                else:
                    dsts, width, bias = (KA[r][h][own, S:KEYS_PAD], KA[r][h][other, S:KEYS_PAD]), KEYS_PAD - S, b1s[own, 1, hp:hp + 1]
                for dst in dsts:
                    act.activation(dst, PS[own, 6 + n % 2, 0:width], ACT.Identity, bias=bias).then_inc(hi_ready, 1)

            for key in PROLOGUE:
                if key[0] in ("Q", "K", "Kt"):
                    for h in range(2):
                        hi(key, h)
                elif key[0] == "latT":
                    latents(key[1])
            for p in range(STEPS):
                tasks = step_tasks(p)
                for slot in range(SLOTS):
                    g = SLOTS * p + slot
                    j = slot % KB
                    rows = min(P, KEYS - P * j)
                    act.wait_ge(sw_ready, g + 1)
                    if g >= 4:
                        act.wait_ge(pv_ready, g - 3)
                    act.activation(PX[0:rows, g % 4, :], PS[0:rows, g % 2, :], ACT.Exp, scale=SCALE_W).then_inc(pw_ready, 1)
                    for key, h in splits(tasks, slot):
                        hi(key, h)
            act.wait_ge(on_ready, 2 * PAIRS)
            for b in range(B - 1):
                evac(("xT", "F", b), FS[:, b, :])
            act.wait_ge(cn_in, N_CN)
            global_layers = ((gact1[:], 64, ACT.Gelu, 1.0 / S, gnb[0:64, 0:1]), (gact2[:], 32, ACT.Gelu, 1.0, gnb[0:32, 1:2]),
                             (gth[:], P, ACT.Tanh, 0.5, cbias[:, 1:2]))
            layers = ((H1, ACT.Gelu, 1.0, cnb[:, 0:1]), (H2, ACT.Gelu, 1.0, cnb[:, 1:2]),
                      (H3, ACT.Gelu, 1.0, cnb[:, 2:3]), (TH, ACT.Tanh, 0.5, cbias[:, 0:1]))
            for c, group, layer in [(c, group, layer) for c in range(CYCLES) for group in coupling_groups(c) for layer in range(4)]:
                dst, func, scale, bias = layers[layer]
                for b in group:
                    if (c, layer, b) == LAST_INPUT:
                        evac(("xT", "F", b), FS[:, b, :])
                    if layer == 3 and c:
                        act.wait_ge(state_ready, B * (c - 1) + b + 1)
                    evac(("cn", c, layer, b), dst[:, b, :], func=func, scale=scale, bias=bias)
                if c == 0 and layer < 3:
                    if layer == 2:
                        act.wait_ge(coef_ready, 1)
                    gdst, rows, func, scale, bias = global_layers[layer]
                    evac(("gn", layer), gdst, rows=rows, cols=B, func=func, scale=scale, bias=bias)

        @block.vector
        def _(dve):
            count = [0]

            def link(ins):
                count[0] += 1
                ins.then_inc(dve_seq, 1)
                dve.wait_ge(dve_seq, count[0])

            def norm_stats(key, src, rows=P):
                n = LN[key]
                for t in range(NT):
                    ins = dve.bn_stats(out=st[0:rows, n % 2, t, :], in_=src[0:rows, t, :])
                link(ins)
                for t in range(NT):
                    ins = dve.bn_aggr(out=mv[0:rows, n, t, :], in_=st[0:rows, n % 2, t, :])
                link(ins)
                dve.tensor_scalar_add(ve[0:rows, n, :], mv[0:rows, n, :, 1], LN_EPS).then_inc(var_ready, 1)

            def norm_apply(key, src, dst, rows=P):
                n = LN[key]
                dve.wait_ge(rstd_ready, n + 1)
                for t in range(NT):
                    ins = dve.tensor_scalar(dst[0:rows, t, :], src[0:rows, t, :], mv[0:rows, n, t, 0:1], rs[0:rows, n, t:t + 1],
                                            ALU.subtract, ALU.mult)
                ins.then_inc(x_ready, 1)

            dve.wait_ge(consts, N_CONST)
            dve.tensor_copy(iota[:], topi[:, 0, 0, :])
            link(dve.tensor_scalar_mul(hmask_s[:], hmask[:], SCALE_N))
            for b in range(B):
                dve.wait_ge(sq_ready, NT * (b + 1))
                cols = slice(NT * b, NT * b + NT)
                dve.tensor_scalar_max(ss[:, cols], ss[:, cols], 1e-37).then_inc(ss_ready, 1)
            for b in range(B):
                dve.wait_ge(rn_ready, b + 1)
                dve.tensor_tensor(DG[:, b, :].rearrange("p (t n) -> p t n", t=NT), ident[:].unsqueeze(1).broadcast_to([P, NT, P]),
                                  rn[:, NT * b:NT * b + NT].unsqueeze(2).broadcast_to([P, NT, P]), ALU.mult).then_inc(diag_ready, 1)

            def sims(b):
                for j in range(NT):
                    n = NT * b + j
                    dve.wait_ge(a_free, LA["rb", b] + 1)
                    link(dve.tensor_scalar(GX[:, n % 2, :], RBv[:, b, :], rn[:, n:n + 1], 1.0 / COS_EPS, ALU.mult, ALU.min))
                    dve.wait_ge(dots_ready, n + 1)
                    dve.wait_ge(sq_ready, TILES)
                    if b >= 2:
                        dve.wait_ge(v_full, LV["oA", b - 2] + 1)
                    dve.tensor_tensor(EX[:, b % 2, j, :], PS[:, j, :], GX[:, n % 2, :], ALU.mult).then_inc(sim_ready, 1)

            def out_a(b):
                n = LV["oA", b]
                cols = slice(NT * b, NT * b + NT)
                dve.wait_ge(exp_ready, NT * (b + 1))
                link(dve.reciprocal(rinv[:, cols], rsum[:, cols]))
                dve.wait_ge(v_full, n + 1)
                for t in range(NT):
                    ins = dve.scalar_tensor_tensor(Y[:, b, t, :], bank_v(n)[:, P * t:P * t + P], rinv[:, NT * b + t:NT * b + t + 1],
                                                   XS["0"][:, NT * b + t, :], ALU.mult, ALU.add)
                ins.then_inc(v_free, 1)
                dve.wait_ge(v_free, n + 1)
                link(dve.tensor_tensor(Y[:, b], Y[:, b], xtile("0", b), ALU.add))
                norm_stats(("A", b), Y[:, b])

            sims(0)
            def context0():
                n = LV["k0",]
                dve.wait_ge(v_full, n + 1)
                dve.wait_ge(w0_in, N_W0)
                dve.tensor_scalar_add(k0T[:].rearrange("p b k -> p (b k)"), bank_v(n)[:, 0:B * CK], b0s[:, 1:2]).then_inc(v_free, 1)
                dve.wait_ge(v_free, n + 1)
                dve.tensor_tensor(KBD[:, 0], k0T[:, 0, :].unsqueeze(1).broadcast_to([P, NH, CK]),
                                  hmask[:].unsqueeze(2).broadcast_to([P, NH, CK]), ALU.mult).then_inc(kbd_ready, 1)
                n = LV["v0",]
                dve.wait_ge(v_full, n + 1)
                dve.tensor_copy(v0x[:, :, :, 0:DH], bank_v(n)[0:CK, :].rearrange("p (b h d) -> p b h d", b=B, h=NH)).then_inc(v_free, 1)
                n = LV["cb0",]
                dve.wait_ge(v_full, n + 1)
                dve.tensor_tensor(CB0[:], bank_v(n)[:, 0:D], bo0s[:], ALU.add).then_inc(v_free, 1)

            for b in range(B):
                if b + 1 < B:
                    sims(b + 1)
                if b:
                    norm_apply(("A", b - 1), Y[:, b - 1], xtile("A", b - 1))
                if b == 2:
                    context0()
                out_a(b)
            dve.wait_ge(ctx_in, 16)
            norm_stats(("media", 0), ctx_sb, rows=CK)
            norm_apply(("A", B - 1), Y[:, B - 1], xtile("A", B - 1))
            norm_apply(("media", 0), ctx_sb, ctxn, rows=CK)

            def max_sub(tt):
                r = tt % 2
                dve.wait_ge(s0_ready, tt + 1)
                wide = PS[:, 0:2, 0:6 * CK].rearrange("p a (h k) -> p a h k", k=CK)
                rest = PS[:, 2, 0:4 * CK].rearrange("p (h k) -> p h k", k=CK)
                dve.tensor_reduce(mx0[:, r, 0:12].rearrange("p (a h) -> p a h", a=2), wide, AX.X, ALU.max)
                link(dve.tensor_reduce(mx0[:, r, 12:16], rest, AX.X, ALU.max))
                if tt >= 2:
                    dve.wait_ge(v_full, LV["pT", tt - 2, 3] + 1)
                    dve.wait_ge(a_full, LA["pT", tt - 2, 2] + 1)
                sm = SM[:, r, :].rearrange("p (h k) -> p h k", k=CK)
                dve.tensor_tensor(sm[:, 0:12, :].rearrange("p (a h) k -> p a h k", a=2), wide,
                                  mx0[:, r, 0:12].rearrange("p (a h) -> p a h", a=2).unsqueeze(3).broadcast_to([P, 2, 6, CK]), ALU.subtract)
                dve.tensor_tensor(sm[:, 12:16, :], rest, mx0[:, r, 12:16].unsqueeze(2).broadcast_to([P, 4, CK]),
                                  ALU.subtract).then_inc(s0_sub, 1)

            def y_b(b):
                n = LV["yB", b]
                dve.wait_ge(v_full, n + 1)
                dve.wait_ge(xr_ready, b + 1)
                dve.tensor_tensor(Y[:, b], bank_v(n).rearrange("p (t d) -> p t d", t=NT), xtile("A", b), ALU.add).then_inc(v_free, 1)
                dve.wait_ge(v_free, n + 1)
                norm_stats(("B", b), Y[:, b])

            def divide0(tt):
                b, t = divmod(tt, NT)
                dve.wait_ge(pv0_full, tt + 1)
                o = PS[:, 3, 0:NH * (DH + 1)].rearrange("p (h d) -> p h d", h=NH)
                link(dve.reciprocal(r0[:, tt % 2, :], o[:, :, DH]))
                dve.tensor_tensor(C0[:, b, t, :].rearrange("p (h d) -> p h d", h=NH), o[:, :, 0:DH],
                                  r0[:, tt % 2, :].unsqueeze(2).broadcast_to([P, NH, DH]), ALU.mult).then_inc(pv0_free, 1)

            def route(b):
                n = LV["router", b]
                dve.wait_ge(v_full, n + 1)
                dve.tensor_copy(lg[:, b].rearrange("p t e -> p (t e)"), bank_v(n)[:, 0:NT * E]).then_inc(v_free, 1)
                dve.wait_ge(v_free, n + 1)
                for t in range(NT):
                    ins = dve.max(top[:, b, t, :], lg[:, b, t, :])
                link(ins)
                dve.tensor_tensor(dl[:, b, :], top[:, b, :, 1], top[:, b, :, 0], ALU.subtract).then_inc(dl_ready, 1)
                for t in range(NT):
                    ins = dve.max_index(topi[:, b, t, :], top[:, b, t, :], lg[:, b, t, :])
                link(ins)
                link(dve.tensor_copy(topf[:, b], topi[:, b, :, 0:2]))

            def combine(b):
                dve.wait_ge(etop_ready, b + 1)
                link(dve.tensor_scalar_add(wtop[:, b, 0, :], etop[:, b, :], 1.0))
                link(dve.reciprocal(wtop[:, b, 0, :], wtop[:, b, 0, :]))
                dve.tensor_tensor(wtop[:, b, 1, :], etop[:, b, :], wtop[:, b, 0, :], ALU.mult)
                for i in range(2):
                    ins = dve.tensor_tensor(eq[:, i], iota[:].unsqueeze(1).broadcast_to([P, NT, E]),
                                            topf[:, b, :, i].unsqueeze(2).broadcast_to([P, NT, E]), ALU.is_equal)
                link(ins)
                for i in range(2):
                    ins = dve.tensor_tensor(eq[:, i], eq[:, i], wtop[:, b, i, :].unsqueeze(2).broadcast_to([P, NT, E]), ALU.mult)
                link(ins)
                link(dve.tensor_tensor(comb[:, b], eq[:, 0], eq[:, 1], ALU.add))

            max_sub(0)
            for tt in range(TILES):
                if tt + 1 < TILES:
                    max_sub(tt + 1)
                if tt >= 2:
                    dve.wait_ge(pv0_full, tt - 1)
                for g in (1, 3):
                    n = LV["pT", tt, g]
                    dve.wait_ge(v_full, n + 1)
                    dve.tensor_copy(PT0[:, tt % 2, 4 * g:4 * g + 4, :].rearrange("p h n -> p (h n)"), bank_v(n)[0:CK, :]).then_inc(v_free, 1)
                if tt:
                    divide0(tt - 1)
                if tt % NT == 3 and tt > NT:
                    norm_apply(("B", tt // NT - 1), Y[:, tt // NT - 1], xtile("B", tt // NT - 1))
                for kind, b in between0(tt):
                    if kind == "y":
                        y_b(b)
                    elif kind == "route":
                        route(b)
                for kind, b in between0(tt - 1):
                    if kind == "route":
                        combine(b)
            divide0(TILES - 1)

            def gate(n):
                e_all, k = divmod(n, HB)
                dve.wait_ge(silu_ready, n + 1)
                dve.wait_ge(u_ready, n + 1)
                if e_all >= 3:
                    dve.wait_ge(v_full, LV["down", (e_all - 3) // EXPERTS, (e_all - 3) % EXPERTS] + 1)
                dve.tensor_tensor(HX[:, e_all % 3, k, :], PS[:, 2 + n % 2, :], SG[:, n % 4, :], ALU.mult).then_inc(h_ready, 1)

            def sum_squares(b):
                dve.wait_ge(sqq_ready, 2 * b + 2)
                link(dve.tensor_reduce(SSQ[b], SQ.rearrange("p a t (h d) -> p (a t h) d", d=DH), AX.X, ALU.add))
                dve.tensor_scalar_max(SSQ[b], SSQ[b], L2_EPS ** 2).then_inc(ssq_ready, 1)

            def scale_qk(b):
                if b < B - 1:
                    dve.wait_ge(pow_ready, b + 1)
                else:
                    dve.wait_ge(lnorm_ready, 1)
                for a, x in enumerate((QD, KD)):
                    x = x[:, b].rearrange("p t (h d) -> p (t h) d", d=DH)
                    ins = dve.tensor_tensor(x, x, SSQ[b][:, NT * NH * a:NT * NH * (a + 1)].unsqueeze(2).broadcast_to([P, NT * NH, DH]), ALU.mult)
                ins.then_inc(qkn_ready, 1)

            def accumulate(e_all):
                b, e = divmod(e_all, EXPERTS)
                n = LV["down", b, e]
                dve.wait_ge(v_full, n + 1)
                if e == E:
                    dve.tensor_tensor(Y[:, b], bank_v(n).rearrange("p (t d) -> p t d", t=NT), Y[:, b], ALU.add).then_inc(v_free, 1)
                else:
                    for t in range(NT):
                        ins = dve.scalar_tensor_tensor(Y[:, b, t, :], bank_v(n)[:, P * t:P * t + P], comb[:, b, t, e:e + 1],
                                                       XS["B"][:, NT * b + t, :] if e == 0 else Y[:, b, t, :], ALU.mult, ALU.add)
                    ins.then_inc(v_free, 1)
                dve.wait_ge(v_free, n + 1)
                if e == E:
                    if b == B - 1:
                        scale_qk(B - 2)
                    norm_stats(("C", b), Y[:, b])
                    norm_apply(("C", b), Y[:, b], xtile("C", b))

            for k in range(HB):
                gate(k)
            y_b(B - 1)
            route(B - 2)
            for e_all in range(B * EXPERTS):
                if e_all + 1 < B * EXPERTS:
                    for k in range(HB):
                        gate(HB * (e_all + 1) + k)
                accumulate(e_all)
                if early_batch(e_all, D_SUMS) is not None:
                    sum_squares(early_batch(e_all, D_SUMS))
                if early_batch(e_all, D_NORMED) is not None and early_batch(e_all, D_NORMED) < B - 2:
                    scale_qk(early_batch(e_all, D_NORMED))
                if e_all == 0:
                    norm_apply(("B", B - 1), Y[:, B - 1], xtile("B", B - 1))
                    combine(B - 2)
                    dve.wait_ge(perc_in, N_PERC)
                    dve.tensor_copy(bv1b, b1s[:, 2, :].unsqueeze(2).broadcast_to([P, NHP, P])).then_inc(bv1_ready, 1)
                if e_all == LAST_ROUTER:
                    route(B - 1)
                    combine(B - 1)
                if e_all == BIAS_ROW:
                    n = LV["cb1",]
                    dve.wait_ge(v_full, n + 1)
                    dve.tensor_tensor(CB1[:], bank_v(n)[:, 0:D], bout1s[:], ALU.add).then_inc(v_free, 1)
            def gather_kv(b):
                n = LV["kv", b]
                dve.wait_ge(v_full, n + 1)
                kv = bank_v(n)
                dve.tensor_tensor(KVB[:, b, 0:D].rearrange("p (h d) -> p h d", h=NH), kv[:, 0:D].rearrange("p (h d) -> p h d", h=NH),
                                  hmask_s[:].unsqueeze(2).broadcast_to([P, NH, DH]), ALU.mult)
                dve.tensor_scalar_add(kse[:, b:b + 1], kv[:, D:D + 1], KSUM_EPS).then_inc(v_free, 1)
                dve.wait_ge(v_free, n + 1)
                dve.tensor_scalar_mul(KVB[:, b, D:D + NH], hmask[:], kse[:, b:b + 1]).then_inc(kvb_ready, 1)

            def out_d(b):
                for h in range(2):
                    n = LV["oD", b, h]
                    dve.wait_ge(v_full, n + 1)
                    o = bank_v(n)[:, 0:2 * (D + NH)].rearrange("p (t n) -> p t n", t=2)
                    rec = eq[:, :, :, :].rearrange("p a t e -> p (a t e)")[:, 0:2 * NH].rearrange("p (t h) -> p t h", t=2)
                    link(dve.reciprocal(rec, o[:, :, D:D + NH]))
                    for t in range(2):
                        ins = dve.tensor_tensor(Y[:, b, 2 * h + t, :].rearrange("p (h d) -> p h d", h=NH),
                                                o[:, t, 0:D].rearrange("p (h d) -> p h d", h=NH),
                                                rec[:, t, :].unsqueeze(2).broadcast_to([P, NH, DH]), ALU.mult)
                    ins.then_inc(v_free, 1)
                    dve.wait_ge(v_free, n + 1)
                link(dve.tensor_tensor(Y[:, b], Y[:, b], xtile("C", b), ALU.add))

            def apply_d(key):
                kind, b = key
                if kind == "D":
                    norm_apply(key, Y[:, b], xtile("D", b))
                else:
                    norm_apply(key, xtile("D", b), LAT[:, b])

            gather_kv(0)
            gather_kv(1)

            def norm_d(i):
                key = D_NORMS[i]
                kind, b = key
                if key == ("D", 1):
                    sum_squares(B - 1)
                    gather_kv(2)
                if key == ("D", 2):
                    scale_qk(B - 1)
                if kind == "D":
                    out_d(b)
                    norm_stats(key, Y[:, b])
                else:
                    dve.wait_ge(x_ready, LN["D", b] + 1)
                    norm_stats(key, xtile("D", b))
                if i:
                    apply_d(D_NORMS[i - 1])

            for i in range(D_NORMS.index(("D", B - 1))):
                norm_d(i)
            gather_kv(B - 1)
            out_d(B - 1)
            norm_stats(("D", B - 1), Y[:, B - 1])

            def norm_left(i):
                if i == 0:
                    apply_d(("lat", 1))
                elif i == 1:
                    norm_stats(("lat", 2), xtile("D", 2))
                elif i == 2:
                    apply_d(("D", 3))
                elif i == 3:
                    dve.wait_ge(x_ready, LN["D", 3] + 1)
                    norm_stats(("lat", 3), xtile("D", 3))
                elif i == 4:
                    apply_d(("lat", 2))
                else:
                    apply_d(("lat", 3))

            def lo(key, h):
                kind, p = key
                r, hp = p % 3, p % NHP
                n = PJ[key]
                dve.wait_ge(hi_ready, 12 * p + {"Q": 0, "K": 4, "Kt": 8}[kind] + 2 * h + 2)
                rows, other = slice(DW * h, DW * h + DW), slice(DW * (1 - h), DW * (1 - h) + DW)
                if kind == "Q":
                    lead, dst, width, bias = QA[r][h][rows, :], QA[r][h][other, :], S, b1s[rows, 0, hp:hp + 1]
                elif kind == "K":
                    lead, dst, width, bias = KA[r][h][rows, 0:S], KBt[r][h][rows, 0:S], S, b1s[rows, 1, hp:hp + 1]
                else:
                    width = KEYS_PAD - S
                    lead, dst, bias = KA[r][h][rows, S:KEYS_PAD], KBt[r][h][rows, S:KEYS_PAD], b1s[rows, 1, hp:hp + 1]
                ins = dve.scalar_tensor_tensor(dst, PS[rows, 6 + n % 2, 0:width], bias, lead.bitcast(F32), ALU.add, ALU.subtract)
                if h == 1:
                    ins.then_inc(pj_free, 1)

            def value(key):
                _, b, u = key
                n = PJ[key]
                j, half = divmod(u, 2)
                rows = min(P, KEYS - P * j)
                if b == 0 and u == 0:
                    dve.wait_ge(setup_done, N_E_OPERANDS)
                dve.wait_ge(pj_full, n + 1)
                dve.tensor_copy(VXA[0:rows, b % 2, j, 8 * half:8 * half + 8, 0:DW],
                                PS[0:rows, 6 + n % 2, :].rearrange("p (h d) -> p h d", h=8)).then_inc(pj_free, 1)

            def c_rows(key):
                p = key[1]
                n = PJ[key]
                dve.wait_ge(pj_full, n + 1)
                if p >= 2:
                    dve.wait_ge(c_in[(p - 2) % 3], 32 * ((p - 2) // 3 + 1))
                dve.tensor_scalar_mul(crow[:, p % 2, :], PS[0:2 * NT, 6 + n % 2, 0:P], -1.0).then_inc(pj_free, 1)

            def task(key):
                kind = key[0]
                n = PJ[key]
                if kind == "V":
                    value(key)
                elif kind == "c":
                    c_rows(key)
                elif kind == "oT":
                    dve.wait_ge(pj_full, n + 1)
                    dve.tensor_copy(OT[:, key[1] % NHP, :], PS[:, 6 + n % 2, :]).then_inc(pj_free, 1)
                else:
                    b = key[1]
                    dve.wait_ge(pj_full, n + 1)
                    dve.wait_ge(xr_ready, B + b + 1)
                    dve.tensor_tensor(Y[:, b], PS[:, 6 + n % 2, :].rearrange("p (t d) -> p t d", t=NT), xtile("D", b), ALU.add).then_inc(pj_free, 1)

            def maxima(p, u):
                h, m = divmod(u, 5)
                g = 10 * p + u
                dve.wait_ge(mu_full, g + 1)
                if m < NT:
                    dve.tensor_reduce(mxm[:, p % 2, h, m:m + 1], PS[:, 2 + g % 2, :], AX.X, ALU.max).then_inc(mu_free, 1)
                else:
                    dve.tensor_reduce(mxt[:, p % 2, h, :], PS[:, 2 + g % 2, 0:NT * (KEYS_PAD - S)].rearrange("p (t k) -> p t k", t=NT),
                                      AX.X, ALU.max).then_inc(mu_free, 1)
                    dve.wait_ge(mu_free, g + 1)
                    dve.tensor_tensor(cmx[:, p % 2, h, :], mxm[:, p % 2, h, :], mxt[:, p % 2, h, :], ALU.max).then_inc(cm_ready, 1)

            def head_out(head):
                p, h = divmod(head, 2)
                b = p // NHP
                o = PS[:, 4 + head % 2, 0:NT * (DW + 1)].rearrange("p (t d) -> p t d", t=NT)
                dve.wait_ge(pv_ready, KB * (head + 1))
                link(dve.reciprocal(rden[:, head % 2, :], o[:, :, DW]))
                if p >= 2:
                    dve.wait_ge(pj_full, PJ["oT", p - 2] + 1)
                dve.tensor_tensor(CT[:, p % 2, :, DW * h:DW * h + DW], o[:, :, 0:DW],
                                  rden[:, head % 2, :].unsqueeze(2).broadcast_to([P, NT, DW]), ALU.mult).then_inc(on_ready, 1)

            for key in PROLOGUE:
                if key[0] == "max":
                    maxima(0, key[1])
                elif key[0] == "norm":
                    norm_left(key[1])
                elif key[0] == "latT":
                    continue
                elif key[0] in ("Q", "K", "Kt"):
                    for h in range(2):
                        lo(key, h)
                else:
                    task(key)
            for p in range(STEPS):
                tasks = step_tasks(p)
                for slot in range(SLOTS):
                    if p + 1 < PAIRS:
                        for u in MAX_UNITS.get(slot, []):
                            maxima(p + 1, u)
                    if slot == 0 and p:
                        head_out(2 * p - 1)
                    if slot == KB:
                        head_out(2 * p)
                    for key, h in splits(tasks, slot - 1):
                        lo(key, h)
                    if p % NHP == 1 and p > 1:
                        b = p // NHP - 1
                        if slot == 7:
                            dve.wait_ge(pj_free, PJ["yE", b] + 1)
                            norm_stats(("E", b), Y[:, b])
                        elif slot == 8:
                            norm_apply(("E", b), Y[:, b], xtile("E", b))
                    for key in tasks.get(slot, []):
                        if key[0] not in ("Q", "K", "Kt"):
                            task(key)
            head_out(2 * PAIRS - 1)
            task(EPILOGUE[0])
            dve.wait_ge(cn_in, N_CN)
            dve.tensor_scalar_mul(cbias[:, 0:1], cnb[:, 3:4], 0.5)
            dve.tensor_scalar_mul(cA[:], ar1[:], 0.3)
            dve.tensor_scalar_mul(cbias[:, 1:2], gnb[:, 2:3], 0.5).then_inc(coef_ready, 1)
            task(EPILOGUE[1])
            dve.wait_ge(pj_free, PJ["yE", B - 1] + 1)
            norm_stats(("E", B - 1), Y[:, B - 1])
            norm_apply(("E", B - 1), Y[:, B - 1], xtile("E", B - 1))

            for b in range(B):
                dve.wait_ge(a_free, LA["xT", "F", b] + 1)
                dve.tensor_reduce(gsum[:, b:b + 1], FS[:, b, :], AX.X, ALU.add).then_inc(gs_ready, 1)
            dve.wait_ge(a_free, LA["gn", 2] + 1)
            link(dve.tensor_scalar(cB[:], gth[:], ar1[:], 0.7, ALU.mult, ALU.mult))
            link(dve.tensor_scalar_add(cB[:], cB[:], 0.1))
            def back(b):
                n = LV["back", b]
                dve.wait_ge(v_full, n + 1)
                dve.tensor_tensor(Y[:, b], bank_v(n).rearrange("p (t d) -> p t d", t=NT), xtile("E", b), ALU.add).then_inc(v_free, 1)
                dve.wait_ge(v_free, n + 1)
                norm_stats(("F", b), Y[:, b])
                if b:
                    norm_apply(("F", b - 1), Y[:, b - 1], xtile("0", b - 1))

            for c in range(CYCLES):
                for b in range(B):
                    if c == CYCLES - 1 and b == 2:
                        back(0)
                        back(1)
                    dve.wait_ge(a_free, LA["cn", c, 3, b] + 1)
                    link(dve.tensor_scalar(CP[:, b, :], TH[:, b, :], cA[:], cB[:, b:b + 1], ALU.mult, ALU.add))
                    n = LV["twist", c, b]
                    dve.wait_ge(v_full, n + 1)
                    dve.tensor_tensor(CP[:, b, :], CP[:, b, :], bank_v(n), ALU.mult).then_inc(v_free, 1)
                    dve.wait_ge(v_free, n + 1)
                    dve.tensor_tensor(FS[:, b, :], FS[:, b, :], CP[:, b, :], ALU.add).then_inc(state_ready, 1)
            for b in range(B - 2, B):
                back(b)
            norm_apply(("F", B - 1), Y[:, B - 1], xtile("0", B - 1))

        @block.tensor
        def _(pe):
            def lane_a(key, emit):
                n = LA[key]
                if n >= 2:
                    pe.wait_ge(a_free, n - 1)
                emit(bank_a(n)).then_inc(a_full, 1)

            def lane_v(key, emit):
                n = LV[key]
                if n >= 2:
                    pe.wait_ge(v_free, n - 1)
                emit(bank_v(n)).then_inc(v_full, 1)

            def mm(dst, lhsT, rhs, start=True, stop=True, **kw):
                return pe.matmul(dst, lhsT, rhs, start=start, stop=stop, **kw)

            def product(dst, a_hi, a_lo, b_hi, b_lo):
                mm(dst, a_hi, b_hi, stop=False)
                mm(dst, a_hi, b_lo, start=False, stop=False)
                return mm(dst, a_lo, b_hi, start=False)

            def transposes(srcs, rows=P):
                def emit(bank):
                    for n, src in enumerate(srcs):
                        ins = pe.transpose(bank[0:src.shape[1], rows * n:rows * n + rows], src, ident[0:rows, 0:rows])
                    return ins
                return emit

            def tiles_of(x3):
                return [x3[:, t, :] for t in range(NT)]

            pe.wait_ge(consts, N_CONST)
            for b in range(B):
                pe.wait_ge(x_in[b], 16)
                lane_a(("xT", "A", b), transposes(tiles_of(xtile("0", b))))

            def dots(b):
                pe.wait_ge(diag_ready, b + 1)
                lane_a(("rb", b), lambda bank: mm(bank, ones[:], DG[:, b, :]))
                pe.wait_ge(a_free, LA["xT", "A", b] + 1)
                for j in range(NT):
                    if b:
                        pe.wait_ge(sim_ready, NT * (b - 1) + j + 1)
                    mm(PS[:, j, :], XT[:, b, P * j:P * j + P], XT[:, b, :]).then_inc(dots_ready, 1)

            def out_a(b):
                pe.wait_ge(exp_ready, NT * (b + 1))

                def emit(bank):
                    for i in range(NT):
                        for j in range(NT):
                            ins = mm(bank[:, P * i:P * i + P], EX[:, b % 2, j, P * i:P * i + P], XS["0"][:, NT * b + j, :],
                                     start=j == 0, stop=j == NT - 1)
                    return ins
                lane_v(("oA", b), emit)

            def context0():
                pe.wait_ge(ctx_in, 16)
                lane_a(("ctxT",), transposes([ctx_sb[:, b, :] for b in range(B)], rows=CK))
                pe.wait_ge(a_free, LA["ctxT",] + 1)
                pe.wait_ge(w0_in, N_W0)
                lane_v(("k0",), lambda bank: mm(bank[:, 0:B * CK], wk0s[:], ctxT[:].rearrange("p b k -> p (b k)")))

                def v0(bank):
                    for b in range(B):
                        ins = mm(bank[0:CK, D * b:D * b + D], ctxT[:, b, :], wv0s[:])
                    return ins
                lane_v(("v0",), v0)
                pe.wait_ge(setup_done, 1)
                lane_v(("cb0",), lambda bank: mm(bank[:, 0:D], bv0b[:], wo0s[:]))

            dots(0)
            for b in range(B):
                if b + 1 < B:
                    dots(b + 1)
                if b == 2:
                    context0()
                out_a(b)

            def input0(b):
                pe.wait_ge(x_ready, LN["A", b] + 1)
                lane_a(("xT", "B", b), transposes(tiles_of(xtile("A", b))))

            def queries0(b):
                pe.wait_ge(a_free, LA["xT", "B", b] + 1)
                lane_a(("qT0", b), lambda bank: mm(bank, wq0s[:], XT[:, b, :]))

            def input_c(b):
                pe.wait_ge(x_ready, LN["B", b] + 1)
                lane_a(("xT", "C", b), transposes(tiles_of(xtile("B", b))))

            def route(b):
                pe.wait_ge(a_free, LA["xT", "C", b] + 1)
                pe.wait_ge(qkv_in, N_QKV)

                def router(bank):
                    for t in range(NT):
                        ins = mm(bank[:, E * t:E * t + E], XT[:, b, P * t:P * t + P], wrT[:])
                    return ins
                lane_v(("router", b), router)

            def scores0(tt):
                b, t = divmod(tt, NT)
                pe.wait_ge(a_free, LA["qT0", b] + 1)
                if b == 0:
                    pe.wait_ge(kbd_ready, 1)
                else:
                    pe.wait_ge(kbd_more, b)
                if tt:
                    pe.wait_ge(s0_sub, tt)
                for n, (h0, hn) in enumerate(((0, 6), (6, 6), (12, 4))):
                    ins = mm(PS[:, n, 0:hn * CK], QT0[:, b, P * t:P * t + P], KBD[:, b, h0:h0 + hn, :].rearrange("p h k -> p (h k)"))
                ins.then_inc(s0_ready, 1)

            def turn0(tt):
                pe.wait_ge(p0_ready, tt + 1)
                sm = SM[:, tt % 2, :].rearrange("p (h k) -> p h k", k=CK)
                for g in range(4):
                    lane = lane_a if g % 2 == 0 else lane_v
                    lane(("pT", tt, g), transposes([sm[:, 4 * g + i, :] for i in range(4)]))

            def weigh0(tt):
                b = tt // NT
                pe.wait_ge(a_free, LA["pT", tt, 2] + 1)
                pe.wait_ge(v_free, LV["pT", tt, 3] + 1)
                if tt:
                    pe.wait_ge(pv0_free, tt)
                for h in range(NH):
                    ins = mm(PS[:, 3, (DH + 1) * h:(DH + 1) * (h + 1)], PT0[:, tt % 2, h, :], v0x[:, b, h, :])
                ins.then_inc(pv0_full, 1)

            def c_t(b):
                pe.wait_ge(pv0_free, NT * b + NT)
                lane_a(("cT", b), transposes([C0[:, b, t, :] for t in range(NT)]))

            def y_b(b):
                pe.wait_ge(a_free, LA["cT", b] + 1)

                def emit(bank):
                    for t in range(NT):
                        ins = mm(bank[:, P * t:P * t + P], C0T[:, b, P * t:P * t + P], wo0s[:])
                    return ins
                lane_v(("yB", b), emit)

            input0(0)
            queries0(0)
            scores0(0)
            for tt in range(TILES):
                if tt + 1 < TILES:
                    scores0(tt + 1)
                turn0(tt)
                if tt:
                    weigh0(tt - 1)
                for kind, b in between0(tt):
                    if kind == "cT":
                        c_t(b)
                    elif kind == "x":
                        input0(b)
                    elif kind == "q":
                        queries0(b)
                    elif kind == "y":
                        y_b(b)
                    elif kind == "media":
                        pe.wait_ge(x_ready, LN["media", 0] + 1)
                        lane_a(("mediaT",), transposes([ctxn[:, b, :] for b in range(B)], rows=CK))
                    elif kind == "xC":
                        input_c(b)
                    elif kind == "route":
                        route(b)
            weigh0(TILES - 1)
            input_c(B - 2)
            c_t(B - 1)
            pe.wait_ge(moe_in, N_MOE)

            def up(e_all):
                b, e = divmod(e_all, EXPERTS)
                if b == 0:
                    pe.wait_ge(uplo_ready, e + 1)
                if e == 0:
                    pe.wait_ge(xlo_ready, b + 1)

                parts = XHI[:, b % 2, :], XLO[:, b, :]
                for k in range(HB):
                    n = HB * e_all + k
                    if n >= 2:
                        pe.wait_ge(silu_ready, n - 1)
                    product(PS[:, n % 2, :], UPHI[:, 0, HB * e + k, :], UPLO[:, 0, HB * e + k, :], *parts).then_inc(g_ready, 1)
                    if n >= 2:
                        pe.wait_ge(h_ready, n - 1)
                    product(PS[:, 2 + n % 2, :], UPHI[:, 1, HB * e + k, :], UPLO[:, 1, HB * e + k, :], *parts).then_inc(u_ready, 1)

            def down(e_all):
                b, e = divmod(e_all, EXPERTS)
                pe.wait_ge(h_ready, HB * (e_all + 1))

                def emit(bank):
                    for t in range(NT):
                        for k in range(HB):
                            ins = mm(bank[:, P * t:P * t + P], HX[:, e_all % 3, k, P * t:P * t + P], wdT[:, HB * e + k, :],
                                     start=k == 0, stop=k == HB - 1)
                    return ins
                lane_v(("down", b, e), emit)

            def bias_row():
                pe.wait_ge(bv1_ready, 1)
                pe.wait_ge(perc_in, N_PERC)

                def emit(bank):
                    for c in range(NHP):
                        ins = mm(bank[:, 0:D], bv1b[:, c, :], wout1s[:, c, :], start=c == 0, stop=c == NHP - 1)
                    return ins
                lane_v(("cb1",), emit)

            def input_d(b):
                pe.wait_ge(x_ready, LN["C", b] + 1)
                lane_a(("xT", "D", b), transposes(tiles_of(xtile("C", b))))

            def qkv(b):
                pe.wait_ge(a_free, LA["xT", "D", b] + 1)
                pe.wait_ge(vx_ones, 1)
                for t in range(NT):
                    lane_a(("qkv", b, t), lambda bank: mm(bank[:, 0:3 * D], XT[:, b, P * t:P * t + P], wqkvT[:].rearrange("p k n -> p (k n)")))

            pe.wait_ge(s0_sub, TILES)
            up(0)
            y_b(B - 1)
            route(B - 2)
            for e_all in range(B * EXPERTS):
                if e_all + 1 < B * EXPERTS:
                    up(e_all + 1)
                down(e_all)
                if e_all == LAST_ROUTER:
                    input_c(B - 1)
                    route(B - 1)
                if e_all == BIAS_ROW:
                    bias_row()
                if early_batch(e_all, D_INPUT) is not None:
                    input_d(early_batch(e_all, D_INPUT))
                if early_batch(e_all, D_QKV) is not None:
                    qkv(early_batch(e_all, D_QKV))
            def keys_values(b):
                pe.wait_ge(sp_ready, b + 1)
                lane_a(("qT", b), transposes([QD[:, b, t, :] for t in range(NT)]))

                def kv(bank):
                    for t in range(NT):
                        ins = mm(bank[:, 0:D + 1], KD[:, b, t, :], VXv[:, b, t, :], start=t == 0, stop=t == NT - 1)
                    return ins
                lane_v(("kv", b), kv)

            def latents(b):
                pe.wait_ge(x_ready, LN["lat", b] + 1)
                lane_a(("latT", b), transposes(tiles_of(LAT[:, b])))

            def output_d(b):
                pe.wait_ge(a_free, LA["qT", b] + 1)
                pe.wait_ge(kvb_ready, b + 1)
                for h in range(2):
                    def emit(bank):
                        for t in range(2):
                            tt = 2 * h + t
                            ins = mm(bank[:, (D + NH) * t:(D + NH) * (t + 1)], QTD[:, b, P * tt:P * tt + P], KVB[:, b, :])
                        return ins
                    lane_v(("oD", b, h), emit)

            keys_values(0)
            keys_values(1)
            input_d(B - 1)
            qkv(B - 1)
            output_d(0)
            keys_values(2)
            output_d(1)
            output_d(2)
            latents(0)
            keys_values(3)
            output_d(3)
            pe.wait_ge(v_free, LV["oD", B - 1, 1] + 1)
            pe.wait_ge(silu_ready, B * EXPERTS * HB)
            pe.wait_ge(wide_lo, 5)

            def s_wide(p, slot):
                g = SLOTS * p + slot
                h, j = divmod(slot, KB)
                r, rows = p % 3, min(P, KEYS - P * j)
                if g == 0:
                    pe.wait_ge(setup_done, N_E_OPERANDS)
                    pe.wait_ge(a_free, LA["latT", B - 1] + 1)
                if slot == 0:
                    pe.wait_ge(c_in[r], 32 * (p // 3 + 1))
                if g >= 2:
                    pe.wait_ge(pw_ready, g - 1)
                dst = PS[0:rows, g % 2, :]
                mm(dst, KA[r][h][:, P * j:P * j + rows], QA[r][h][:], stop=False)
                mm(dst, KBt[r][h][:, P * j:P * j + rows], QB[r][h][:], start=False).then_inc(sw_ready, 1)

            def pv(g):
                p, slot = divmod(g, SLOTS)
                h, j = divmod(slot, KB)
                b, hp = divmod(p, NHP)
                head = 2 * p + h
                rows = min(P, KEYS - P * j)
                pe.wait_ge(pw_ready, g + 1)
                if j == 0 and head >= 2:
                    pe.wait_ge(on_ready, head - 1)
                if j == 0 and hp == 0 and h == 0:
                    pe.wait_ge(pj_free, PJ["V", b, 2 * KB - 1] + 1)
                for t in range(NT):
                    ins = mm(PS[:, 4 + head % 2, (DW + 1) * t:(DW + 1) * (t + 1)], PX[0:rows, g % 4, P * t:P * t + P],
                             VXA[0:rows, b % 2, j, 2 * hp + h, :], start=j == 0 and t == 0, stop=j == KB - 1, skip_group_check=True)
                ins.then_inc(pv_ready, 1)

            def max_unit(p, u):
                h, m = divmod(u, 5)
                g, r = 10 * p + u, p % 3
                if u == 0:
                    pe.wait_ge(hi_ready, 12 * (p + 1))
                    pe.wait_ge(pj_free, PJ["Kt", p] + 1)
                if g >= 2:
                    pe.wait_ge(mu_free, g - 1)
                if m < NT:
                    mm(PS[:, 2 + g % 2, :], QA[r][h][:, P * m:P * m + P], KA[r][h][:, 0:S]).then_inc(mu_full, 1)
                else:
                    w = KEYS_PAD - S
                    for t in range(NT):
                        ins = mm(PS[:, 2 + g % 2, w * t:w * t + w], QA[r][h][:, P * t:P * t + P], KA[r][h][:, S:KEYS_PAD])
                    ins.then_inc(mu_full, 1)

            def task(key):
                n = PJ[key]
                if n >= 2:
                    pe.wait_ge(pj_free, n - 1)
                bank = PS[:, 6 + n % 2, :]
                kind = key[0]
                if kind in ("Q", "K", "Kt"):
                    b, hp = divmod(key[1], NHP)
                    pe.wait_ge(latlo_ready, b + 1)
                    cols = slice(P * hp, P * hp + P)
                    if kind == "Q":
                        ins = product(bank, WQHI[:, cols], WQLO[:, cols], LATHI[:, b, :], LATLO[:, b, :])
                    elif kind == "K":
                        ins = product(bank, WKVHI[:, cols], WKVLO[:, cols], LATHI[:, b, :], LATLO[:, b, :])
                    else:
                        ins = product(bank[:, 0:KEYS_PAD - S], WKVHI[:, cols], WKVLO[:, cols], MEDHI[:, b, :], MEDLO[:, b, :])
                elif kind == "V":
                    _, b, u = key
                    pe.wait_ge(latlo_ready, b + 1)
                    pe.wait_ge(wide_lo, 7)
                    j, half = divmod(u, 2)
                    cols = slice(INNER + 512 * half, INNER + 512 * half + 512)
                    rows = min(P, KEYS - P * j)
                    hi, lo = (LATHI[:, b, P * j:P * j + P], LATLO[:, b, P * j:P * j + P]) if j < NT else (MEDHI[:, b, 0:CK], MEDLO[:, b, 0:CK])
                    ins = product(bank[0:rows, :], hi, lo, WKVHI[:, cols], WKVLO[:, cols])
                elif kind == "c":
                    p = key[1]
                    pe.wait_ge(cm_ready, 2 * (p + 1))
                    ins = pe.transpose(bank[0:2 * NT, 0:P], cmx[:, p % 2].rearrange("p h t -> p (h t)"), ident[:])
                elif kind == "oT":
                    p = key[1]
                    pe.wait_ge(on_ready, 2 * (p + 1))
                    for t in range(NT):
                        ins = pe.transpose(bank[:, P * t:P * t + P], CT[:, p % 2, t, :], ident[:])
                else:
                    b = key[1]
                    pe.wait_ge(pj_free, PJ["oT", NHP * b + NHP - 1] + 1)
                    for t in range(NT):
                        for c in range(NHP):
                            ins = mm(bank[:, P * t:P * t + P], OT[:, c, P * t:P * t + P], wout1s[:, c, :], start=c == 0, stop=c == NHP - 1)
                ins.then_inc(pj_full, 1)

            for key in PROLOGUE:
                if key[0] == "max":
                    max_unit(0, key[1])
                elif key[0] == "norm":
                    continue
                elif key[0] == "latT":
                    latents(key[1])
                else:
                    task(key)
            for p in range(STEPS):
                tasks = step_tasks(p)
                for slot in range(SLOTS):
                    s_wide(p, slot)
                    if p + 1 < PAIRS:
                        for u in MAX_UNITS.get(slot, []):
                            max_unit(p + 1, u)
                    if SLOTS * p + slot:
                        pv(SLOTS * p + slot - 1)
                    for key in tasks.get(slot, []):
                        task(key)
            pv(SLOTS * STEPS - 1)
            task(EPILOGUE[0])

            def input_f(b):
                pe.wait_ge(x_ready, LN["E", b] + 1)
                lane_a(("xT", "F", b), transposes(tiles_of(xtile("E", b))))

            pe.wait_ge(on_ready, 2 * PAIRS)
            for b in range(B - 1):
                input_f(b)
            task(EPILOGUE[1])
            pe.wait_ge(cn_in, N_CN)
            pe.wait_ge(setup_done, N_POOL)
            global_layers = ((gn1, gsum, 64), (gn2, gact1, 32), (gn3, gact2, P))

            def back(b):
                pe.wait_ge(state_ready, B * (CYCLES - 1) + b + 1)
                lane_v(("back", b), transposes([FS[:, b, P * t:P * t + P] for t in range(NT)]))

            layers = ((cn1, FS), (cn2, H1), (cn3, H2), (cn4, H3))
            for c, group, layer in [(c, group, layer) for c in range(CYCLES) for group in coupling_groups(c) for layer in range(4)]:
                w, src = layers[layer]
                if c == 0 and layer == 3:
                    pe.wait_ge(pj_free, len(PJ))
                for b in group:
                    if (c, layer, b) == LAST_INPUT:
                        input_f(b)
                        pe.wait_ge(a_free, LA["xT", "F", b] + 1)
                    elif c == 0 and layer == 0:
                        pe.wait_ge(a_free, LA["xT", "F", b] + 1)
                    if layer == 0 and c:
                        pe.wait_ge(state_ready, B * (c - 1) + b + 1)
                    if layer:
                        pe.wait_ge(a_free, LA["cn", c, layer - 1, b] + 1)
                    lane_a(("cn", c, layer, b), lambda bank: mm(bank, w[:], src[:, b, :]))
                    if layer == 3:
                        lane_v(("twist", c, b), lambda bank: mm(bank, twist[:], FS[:, b, :]))
                if c == 0 and layer < 3:
                    gw, gsrc, rows = global_layers[layer]
                    if layer == 0:
                        pe.wait_ge(gs_ready, B)
                    else:
                        pe.wait_ge(a_free, LA["gn", layer - 1] + 1)
                    lane_a(("gn", layer), lambda bank: mm(bank[0:rows, 0:B], gw[:], gsrc[:]))
                if c == CYCLES - 1 and group[0] == 2 and layer < 2:
                    back(layer)
            for b in range(B - 2, B):
                back(b)


_INS = ["x", "ctx_1024", "L0_xattn_Wq", "L0_xattn_bq", "L0_xattn_Wk", "L0_xattn_bk", "L0_xattn_Wv", "L0_xattn_bv",
        "L0_xattn_Wo", "L0_xattn_bo", "L0_ffn_w_router", "L0_ffn_Wg", "L0_ffn_Wu", "L0_ffn_Wd", "L0_ffn_sg",
        "L0_ffn_su", "L0_ffn_sd", "L1_attn_W_qkv", "L1_xattn_ln_media_w", "L1_xattn_ln_media_b", "L1_xattn_ln_lat_w",
        "L1_xattn_ln_lat_b", "L1_xattn_Wq", "L1_xattn_bq", "L1_xattn_Wkv", "L1_xattn_bkv", "L1_xattn_Wout",
        "L1_xattn_bout", "L1_ffn_cn_w1", "L1_ffn_cn_b1", "L1_ffn_cn_w2", "L1_ffn_cn_b2", "L1_ffn_cn_w3",
        "L1_ffn_cn_b3", "L1_ffn_cn_w4", "L1_ffn_cn_b4", "L1_ffn_gc_w1", "L1_ffn_gc_b1", "L1_ffn_gc_w2",
        "L1_ffn_gc_b2", "L1_ffn_gc_w3", "L1_ffn_gc_b3", "L1_ffn_adaptive_range"]


def kernel(**inputs):
    import numpy as np
    import concourse.bacc as bacc
    from concourse.bass_utils import run_bass_kernel_spmd

    nc = bacc.Bacc("TRN2", target_bir_lowering=False, num_devices=1)
    arrays, args = {}, []
    def blocks(w):
        return w.reshape(-1, P, w.shape[-1]).transpose(1, 0, 2)

    layout = {
        "L0_ffn_Wg": lambda w: w.transpose(2, 0, 1).reshape(D, -1), "L0_ffn_Wu": lambda w: w.transpose(2, 0, 1).reshape(D, -1),
        "L0_ffn_sg": lambda w: w.T, "L0_ffn_su": lambda w: w.T,
        "L0_ffn_Wd": lambda w: blocks(w.transpose(0, 2, 1).reshape(-1, D)).reshape(P, -1),
        "L0_ffn_sd": lambda w: blocks(w.T).reshape(P, -1),
        "L0_ffn_w_router": lambda w: w.T, "L1_attn_W_qkv": lambda w: w.T,
        "L1_xattn_bq": lambda w: w.reshape(-1, P).T, "L1_xattn_bkv": lambda w: w.reshape(-1, P).T,
        "L1_xattn_Wout": blocks,
    }
    for name in _INS:
        a = np.asarray(inputs[name])
        a = np.ascontiguousarray(layout[name](a) if name in layout else a)
        arrays[f"in_{name}"] = a
        args.append(nc.dram_tensor(f"in_{name}", a.shape, mybir.dt.from_np(a.dtype), kind="ExternalInput").ap())
    args.append(nc.dram_tensor("out", (B, S, D), F32, kind="ExternalOutput").ap())
    decoder(nc, *args)
    r = run_bass_kernel_spmd(nc, [arrays], core_ids=[0])
    return r.results[0]["out"]
```
